# Optimizing a Trainium2 kernel written in Bass

```python
import numpy as np
import jax
import jax.numpy as jnp

def _softmax(x, axis=-1):
    return jax.nn.softmax(x, axis=axis)

def _gelu(x):
    return jax.nn.gelu(x, approximate=True)

def _silu(x):
    return jax.nn.silu(x)

def _sigmoid(x):
    return jax.nn.sigmoid(x)

def _layernorm(x, axis=-1, eps=1e-05):
    m = jnp.mean(x, axis=axis, keepdims=True)
    v = jnp.var(x, axis=axis, keepdims=True)
    return (x - m) / jnp.sqrt(v + eps)

def _scatter_add(tgt, idx, src, axis=0):
    return tgt.at[idx].add(src)

def _segment_sum(src, seg, n):
    return jax.ops.segment_sum(src, seg, n)
kernel_name = 'mk_recurrent_d1_jaxref_r8_307a46'

def setup_inputs(seed: int=0):
    np.random.seed(seed)
    _w = jnp.asarray

    def _L0_attn_setup():
        import jax, jax.numpy as jnp
        import numpy as np
        B, L, C, H = (8, 256, 128, 16)
        HID = 4 * C

        def _rope(x):
            b, n, c = x.shape
            k_max = c // 2
            theta = 1.0 / 10000.0 ** (jnp.arange(k_max, dtype=jnp.float32) / k_max)
            cos_t, sin_t = (jnp.cos(theta), jnp.sin(theta))
            xr = x.reshape(b, n, k_max, 2)
            re = xr[..., 0] * cos_t - xr[..., 1] * sin_t
            im = xr[..., 0] * sin_t + xr[..., 1] * cos_t
            return jnp.stack((re, im), axis=-1).reshape(b, n, c)

        def _dwconv(x_bcl, w, bias):
            y = jax.lax.conv_general_dilated(x_bcl, w, (1,), [(1, 1)], dimension_numbers=('NCH', 'OIH', 'NCH'), feature_group_count=x_bcl.shape[1])
            return y + bias[None, :, None]

        def _ln(x, g, b, eps=1e-05):
            mu = x.mean(-1, keepdims=True)
            var = ((x - mu) ** 2).mean(-1, keepdims=True)
            return (x - mu) * jax.lax.rsqrt(var + eps) * g + b

        def _mlla_forward(x, cpe1_w, cpe1_b, norm1_g, norm1_b, in_w, in_b, actp_w, actp_b, dwc_w, dwc_b, qk_w, qk_b, lepe_w, lepe_b, out_w, out_b, cpe2_w, cpe2_b, norm2_g, norm2_b, fc1_w, fc1_b, fc2_w, fc2_b):
            b, n, c = x.shape
            h, d = (H, c // H)
            x = x + _dwconv(x.transpose(0, 2, 1), cpe1_w, cpe1_b).transpose(0, 2, 1)
            shortcut = x
            xn = _ln(x, norm1_g, norm1_b)
            act_res = jax.nn.silu(xn @ actp_w + actp_b)
            xi = xn @ in_w + in_b
            xi = jax.nn.silu(_dwconv(xi.transpose(0, 2, 1), dwc_w, dwc_b)).transpose(0, 2, 1)
            qk = xi @ qk_w + qk_b
            q = jax.nn.elu(qk[..., :c]) + 1.0
            k = jax.nn.elu(qk[..., c:]) + 1.0
            q_rope = _rope(q).reshape(b, n, h, d).transpose(0, 2, 1, 3)
            k_rope = _rope(k).reshape(b, n, h, d).transpose(0, 2, 1, 3)
            qh = q.reshape(b, n, h, d).transpose(0, 2, 1, 3)
            kh = k.reshape(b, n, h, d).transpose(0, 2, 1, 3)
            vh = xi.reshape(b, n, h, d).transpose(0, 2, 1, 3)
            k_mean = kh.mean(axis=2, keepdims=True)
            z = 1.0 / (jnp.einsum('bhnd,bhmd->bhnm', qh, k_mean) + 1e-06)
            kv = jnp.einsum('bhnd,bhne->bhde', k_rope, vh) * (1.0 / n)
            attn = jnp.einsum('bhnd,bhde->bhne', q_rope, kv) * z
            attn = attn.transpose(0, 2, 1, 3).reshape(b, n, c)
            v_bcl = vh.transpose(0, 2, 1, 3).reshape(b, n, c).transpose(0, 2, 1)
            attn = attn + _dwconv(v_bcl, lepe_w, lepe_b).transpose(0, 2, 1)
            x = shortcut + attn * act_res @ out_w + out_b
            x = x + _dwconv(x.transpose(0, 2, 1), cpe2_w, cpe2_b).transpose(0, 2, 1)
            xn2 = _ln(x, norm2_g, norm2_b)
            mlp = jax.nn.gelu(xn2 @ fc1_w + fc1_b, approximate=False) @ fc2_w + fc2_b
            return x + mlp
        key = jax.random.key(seed)
        ks = jax.random.split(key, 12)

        def nrm(k, shape, scale=0.02):
            return jax.random.normal(k, shape, jnp.float32) * scale
        return {'x': jax.random.normal(ks[0], (B, L, C), jnp.float32), 'cpe1_w': nrm(ks[1], (C, 1, 3), 0.1), 'cpe1_b': jnp.zeros((C,), jnp.float32), 'norm1_g': jnp.ones((C,), jnp.float32), 'norm1_b': jnp.zeros((C,), jnp.float32), 'in_w': nrm(ks[2], (C, C)), 'in_b': jnp.zeros((C,), jnp.float32), 'actp_w': nrm(ks[3], (C, C)), 'actp_b': jnp.zeros((C,), jnp.float32), 'dwc_w': nrm(ks[4], (C, 1, 3), 0.1), 'dwc_b': jnp.zeros((C,), jnp.float32), 'qk_w': nrm(ks[5], (C, 2 * C)), 'qk_b': jnp.zeros((2 * C,), jnp.float32), 'lepe_w': nrm(ks[6], (C, 1, 3), 0.1), 'lepe_b': jnp.zeros((C,), jnp.float32), 'out_w': nrm(ks[7], (C, C)), 'out_b': jnp.zeros((C,), jnp.float32), 'cpe2_w': nrm(ks[8], (C, 1, 3), 0.1), 'cpe2_b': jnp.zeros((C,), jnp.float32), 'norm2_g': jnp.ones((C,), jnp.float32), 'norm2_b': jnp.zeros((C,), jnp.float32), 'fc1_w': nrm(ks[9], (C, HID)), 'fc1_b': jnp.zeros((HID,), jnp.float32), 'fc2_w': nrm(ks[10], (HID, C)), 'fc2_b': jnp.zeros((C,), jnp.float32)}
    _L0_attn_in = _L0_attn_setup()

    def _L0_ffn_setup():
        import jax, jax.numpy as jnp
        import numpy as np
        B, S, D = (4, 128, 128)
        E, K = (8, 2)
        H = 2 * D
        key = jax.random.key(seed)
        ks = jax.random.split(key, 5)
        x = jax.random.normal(ks[0], (B, S, D), dtype=jnp.float32)
        Wg = jax.random.normal(ks[1], (E, D), dtype=jnp.float32) * 0.02
        W1 = jax.random.normal(ks[2], (E, H, D), dtype=jnp.float32) * 0.02
        W2 = jax.random.normal(ks[3], (E, H, D), dtype=jnp.float32) * 0.02
        W3 = jax.random.normal(ks[4], (E, D, H), dtype=jnp.float32) * 0.02
        return {'x': x, 'Wg': Wg, 'W1': W1, 'W2': W2, 'W3': W3}
    _L0_ffn_in = _L0_ffn_setup()
    _d = {'L0_attn_x': _L0_attn_in['x'], 'L0_attn_cpe1_w': _L0_attn_in['cpe1_w'], 'L0_attn_cpe1_b': _L0_attn_in['cpe1_b'], 'L0_attn_norm1_g': _L0_attn_in['norm1_g'], 'L0_attn_norm1_b': _L0_attn_in['norm1_b'], 'L0_attn_in_w': _L0_attn_in['in_w'], 'L0_attn_in_b': _L0_attn_in['in_b'], 'L0_attn_actp_w': _L0_attn_in['actp_w'], 'L0_attn_actp_b': _L0_attn_in['actp_b'], 'L0_attn_dwc_w': _L0_attn_in['dwc_w'], 'L0_attn_dwc_b': _L0_attn_in['dwc_b'], 'L0_attn_qk_w': _L0_attn_in['qk_w'], 'L0_attn_qk_b': _L0_attn_in['qk_b'], 'L0_attn_lepe_w': _L0_attn_in['lepe_w'], 'L0_attn_lepe_b': _L0_attn_in['lepe_b'], 'L0_attn_out_w': _L0_attn_in['out_w'], 'L0_attn_out_b': _L0_attn_in['out_b'], 'L0_attn_cpe2_w': _L0_attn_in['cpe2_w'], 'L0_attn_cpe2_b': _L0_attn_in['cpe2_b'], 'L0_attn_norm2_g': _L0_attn_in['norm2_g'], 'L0_attn_norm2_b': _L0_attn_in['norm2_b'], 'L0_attn_fc1_w': _L0_attn_in['fc1_w'], 'L0_attn_fc1_b': _L0_attn_in['fc1_b'], 'L0_attn_fc2_w': _L0_attn_in['fc2_w'], 'L0_attn_fc2_b': _L0_attn_in['fc2_b'], 'L0_ffn_Wg': _L0_ffn_in['Wg'], 'L0_ffn_W1': _L0_ffn_in['W1'], 'L0_ffn_W2': _L0_ffn_in['W2'], 'L0_ffn_W3': _L0_ffn_in['W3']}
    _x0 = _d['L0_attn_x']
    _d['L0_attn_x'] = jax.random.normal(jax.random.fold_in(jax.random.key(seed), 1), (2, 2048, 128), dtype=_x0.dtype)
    del _x0
    return _d

def reference(L0_attn_x, L0_attn_cpe1_w, L0_attn_cpe1_b, L0_attn_norm1_g, L0_attn_norm1_b, L0_attn_in_w, L0_attn_in_b, L0_attn_actp_w, L0_attn_actp_b, L0_attn_dwc_w, L0_attn_dwc_b, L0_attn_qk_w, L0_attn_qk_b, L0_attn_lepe_w, L0_attn_lepe_b, L0_attn_out_w, L0_attn_out_b, L0_attn_cpe2_w, L0_attn_cpe2_b, L0_attn_norm2_g, L0_attn_norm2_b, L0_attn_fc1_w, L0_attn_fc1_b, L0_attn_fc2_w, L0_attn_fc2_b, L0_ffn_Wg, L0_ffn_W1, L0_ffn_W2, L0_ffn_W3):

    def _L0_attn_ref(x, cpe1_w, cpe1_b, norm1_g, norm1_b, in_w, in_b, actp_w, actp_b, dwc_w, dwc_b, qk_w, qk_b, lepe_w, lepe_b, out_w, out_b, cpe2_w, cpe2_b, norm2_g, norm2_b, fc1_w, fc1_b, fc2_w, fc2_b):
        import jax, jax.numpy as jnp
        import numpy as np
        B, L, C, H = (8, 256, 128, 16)
        HID = 4 * C

        def _rope(x):
            b, n, c = x.shape
            k_max = c // 2
            theta = 1.0 / 10000.0 ** (jnp.arange(k_max, dtype=jnp.float32) / k_max)
            cos_t, sin_t = (jnp.cos(theta), jnp.sin(theta))
            xr = x.reshape(b, n, k_max, 2)
            re = xr[..., 0] * cos_t - xr[..., 1] * sin_t
            im = xr[..., 0] * sin_t + xr[..., 1] * cos_t
            return jnp.stack((re, im), axis=-1).reshape(b, n, c)

        def _dwconv(x_bcl, w, bias):
            y = jax.lax.conv_general_dilated(x_bcl, w, (1,), [(1, 1)], dimension_numbers=('NCH', 'OIH', 'NCH'), feature_group_count=x_bcl.shape[1])
            return y + bias[None, :, None]

        def _ln(x, g, b, eps=1e-05):
            mu = x.mean(-1, keepdims=True)
            var = ((x - mu) ** 2).mean(-1, keepdims=True)
            return (x - mu) * jax.lax.rsqrt(var + eps) * g + b

        def _mlla_forward(x, cpe1_w, cpe1_b, norm1_g, norm1_b, in_w, in_b, actp_w, actp_b, dwc_w, dwc_b, qk_w, qk_b, lepe_w, lepe_b, out_w, out_b, cpe2_w, cpe2_b, norm2_g, norm2_b, fc1_w, fc1_b, fc2_w, fc2_b):
            b, n, c = x.shape
            h, d = (H, c // H)
            x = x + _dwconv(x.transpose(0, 2, 1), cpe1_w, cpe1_b).transpose(0, 2, 1)
            shortcut = x
            xn = _ln(x, norm1_g, norm1_b)
            act_res = jax.nn.silu(xn @ actp_w + actp_b)
            xi = xn @ in_w + in_b
            xi = jax.nn.silu(_dwconv(xi.transpose(0, 2, 1), dwc_w, dwc_b)).transpose(0, 2, 1)
            qk = xi @ qk_w + qk_b
            q = jax.nn.elu(qk[..., :c]) + 1.0
            k = jax.nn.elu(qk[..., c:]) + 1.0
            q_rope = _rope(q).reshape(b, n, h, d).transpose(0, 2, 1, 3)
            k_rope = _rope(k).reshape(b, n, h, d).transpose(0, 2, 1, 3)
            qh = q.reshape(b, n, h, d).transpose(0, 2, 1, 3)
            kh = k.reshape(b, n, h, d).transpose(0, 2, 1, 3)
            vh = xi.reshape(b, n, h, d).transpose(0, 2, 1, 3)
            k_mean = kh.mean(axis=2, keepdims=True)
            z = 1.0 / (jnp.einsum('bhnd,bhmd->bhnm', qh, k_mean) + 1e-06)
            kv = jnp.einsum('bhnd,bhne->bhde', k_rope, vh) * (1.0 / n)
            attn = jnp.einsum('bhnd,bhde->bhne', q_rope, kv) * z
            attn = attn.transpose(0, 2, 1, 3).reshape(b, n, c)
            v_bcl = vh.transpose(0, 2, 1, 3).reshape(b, n, c).transpose(0, 2, 1)
            attn = attn + _dwconv(v_bcl, lepe_w, lepe_b).transpose(0, 2, 1)
            x = shortcut + attn * act_res @ out_w + out_b
            x = x + _dwconv(x.transpose(0, 2, 1), cpe2_w, cpe2_b).transpose(0, 2, 1)
            xn2 = _ln(x, norm2_g, norm2_b)
            mlp = jax.nn.gelu(xn2 @ fc1_w + fc1_b, approximate=False) @ fc2_w + fc2_b
            return x + mlp
        return _mlla_forward(x, cpe1_w, cpe1_b, norm1_g, norm1_b, in_w, in_b, actp_w, actp_b, dwc_w, dwc_b, qk_w, qk_b, lepe_w, lepe_b, out_w, out_b, cpe2_w, cpe2_b, norm2_g, norm2_b, fc1_w, fc1_b, fc2_w, fc2_b)

    def _L0_ffn_ref(x, Wg, W1, W2, W3):
        import jax, jax.numpy as jnp
        import numpy as np
        B, S, D = (4, 128, 128)
        E, K = (8, 2)
        H = 2 * D
        gate_out = jnp.einsum('bsd,ed->bse', x, Wg)
        top_v, top_i = jax.lax.top_k(gate_out, K)
        probs = jax.nn.softmax(top_v, axis=-1)
        out = jnp.zeros_like(x)
        for e in range(E):
            w_e = jnp.sum(probs * (top_i == e), axis=-1)
            h1 = jnp.einsum('bsd,hd->bsh', x, W1[e])
            h2 = jnp.einsum('bsd,hd->bsh', x, W2[e])
            g = h1 * jax.nn.sigmoid(h1) * h2
            y = jnp.einsum('bsh,dh->bsd', g, W3[e])
            out = out + y * w_e[..., None]
        return out
    x = L0_attn_x
    xn = _layernorm(x, axis=-1)
    s = _L0_attn_ref(xn, L0_attn_cpe1_w, L0_attn_cpe1_b, L0_attn_norm1_g, L0_attn_norm1_b, L0_attn_in_w, L0_attn_in_b, L0_attn_actp_w, L0_attn_actp_b, L0_attn_dwc_w, L0_attn_dwc_b, L0_attn_qk_w, L0_attn_qk_b, L0_attn_lepe_w, L0_attn_lepe_b, L0_attn_out_w, L0_attn_out_b, L0_attn_cpe2_w, L0_attn_cpe2_b, L0_attn_norm2_g, L0_attn_norm2_b, L0_attn_fc1_w, L0_attn_fc1_b, L0_attn_fc2_w, L0_attn_fc2_b)
    g = _silu(_L0_ffn_ref(xn, L0_ffn_Wg, L0_ffn_W1, L0_ffn_W2, L0_ffn_W3))
    x = x + s * g
    return x

_drawn_inputs = setup_inputs


def setup_inputs(seed=0):
    import zlib

    import numpy as np

    out = dict(_drawn_inputs(seed))
    spreads = {'L0_attn_cpe1_b': (0.0, 0.8),
     'L0_attn_norm1_g': (1.0, 0.6),
     'L0_attn_norm1_b': (0.0, 0.8),
     'L0_attn_in_b': (0.0, 0.8),
     'L0_attn_actp_b': (0.0, 0.8),
     'L0_attn_dwc_b': (0.0, 0.8),
     'L0_attn_qk_b': (0.0, 2.0),
     'L0_attn_lepe_b': (0.0, 0.8),
     'L0_attn_out_b': (0.0, 0.8),
     'L0_attn_cpe2_b': (0.0, 2.0),
     'L0_attn_norm2_g': (1.0, 0.6),
     'L0_attn_norm2_b': (0.0, 0.8),
     'L0_attn_fc1_b': (0.0, 0.8),
     'L0_attn_fc2_b': (0.0, 2.0)}
    factors = {'L0_attn_cpe1_w': 8.0,
     'L0_attn_in_w': 8.0,
     'L0_attn_actp_w': 8.0,
     'L0_attn_dwc_w': 8.0,
     'L0_attn_qk_w': 8.0,
     'L0_attn_lepe_w': 8.0,
     'L0_attn_out_w': 8.0,
     'L0_attn_cpe2_w': 8.0,
     'L0_attn_fc1_w': 8.0,
     'L0_attn_fc2_w': 8.0,
     'L0_ffn_Wg': 8.0,
     'L0_ffn_W1': 8.0,
     'L0_ffn_W2': 8.0,
     'L0_ffn_W3': 8.0}
    for name, (base, spread) in spreads.items():
        noise = np.random.default_rng([zlib.crc32(name.encode()), seed]).standard_normal(out[name].shape)
        drawn = base * np.exp(spread * noise) if base else spread * noise
        out[name] = jnp.asarray(drawn.astype(out[name].dtype))
    for name, factor in factors.items():
        out[name] = (out[name] * factor).astype(out[name].dtype)
    return out
```

```python
from contextlib import ExitStack

import numpy as np
import concourse.bass as bass
from concourse import mybir

F32 = mybir.dt.float32
BF16 = mybir.dt.bfloat16
I32 = mybir.dt.int32
ALU = mybir.AluOpType
ACT = mybir.ActivationFunctionType
AX = mybir.AxisListType

P = 128
BATCH, SEQ, C = 2, 2048, 128
HEADS = 16
HD = C // HEADS
HID = 4 * C
E = 8
EH = 2 * C
N = BATCH * SEQ
NT = N // P
CH = 512
TPC = CH // P
PADDED = SEQ + 2
EPS = 1e-5
Z_EPS = 1e-6
SLOT_TILES = 2 * NT + E
SLOTS = SLOT_TILES * P
ZT = 9

VEC = {}
_c = 0
for _name, _w in (("cpe1_w", 3), ("cpe1_b", 1), ("norm1_g", 1), ("norm1_b", 1), ("in_b", 1), ("actp_b", 1),
                  ("dwc_w", 3), ("dwc_b", 1), ("q_b", 1), ("lepe_w", 3), ("lepe_b", 1), ("out_b", 1),
                  ("cpe2_w", 3), ("cpe2_b", 1), ("norm2_g", 1), ("norm2_b", 1), ("fc1_b", 4)):
    VEC[_name] = (_c, _w)
    _c += _w
NVEC = _c

WCOL = {}
_c = 0
for _name, _w in (("in_w", C), ("actp_w", C), ("q_w", C), ("k_w", C), ("out_w", C), ("fc1_w", HID),
                  ("fc2_w", 4 * C), ("wg", E)):
    WCOL[_name] = (_c, _w)
    _c += _w
NWCOL = _c

KCOL = {}
_c = 0
for _name, _w in (("ident", P), ("headblock", P), ("rope", P), ("rope_t", P), ("headmask", HEADS),
                  ("before", P), ("tile_before", 2 * NT * E), ("same_expert", 2 * E), ("prefer", E),
                  ("expert_before", E * E), ("slot_tile", SLOT_TILES)):
    if _name == "before":
        NSTAY = _c
    KCOL[_name] = (_c, _w)
    _c += _w
NKCOL = _c


def shape_constants():
    k = np.zeros((P, NKCOL), np.float32)

    def put(name, a):
        at, w = KCOL[name]
        k[:, at:at + w] = a

    i = np.arange(P)
    put("ident", np.eye(P))
    put("headblock", i[:, None] // HD == i[None, :] // HD)
    half = np.arange(C // 2, dtype=np.float32)
    theta = np.float32(1.0) / np.float32(10000.0) ** (half / np.float32(C // 2))
    cos, sin = np.cos(theta), np.sin(theta)
    rope = np.zeros((C, C), np.float32)
    even, odd = 2 * np.arange(C // 2), 2 * np.arange(C // 2) + 1
    rope[even, even], rope[odd, even] = cos, -sin
    rope[even, odd], rope[odd, odd] = sin, cos
    put("rope", rope)
    put("rope_t", rope.T)
    put("headmask", i[:, None] // HD == np.arange(HEADS)[None, :])
    put("before", i[:, None] < i[None, :])
    te = np.arange(NT * E)
    earlier = (te[:, None] % E == te[None, :] % E) & (te[:, None] // E < te[None, :] // E)
    put("tile_before", np.concatenate([earlier[:P], earlier[P:]], axis=1))
    same = te[:, None] % E == np.arange(E)[None, :]
    put("same_expert", np.concatenate([same[:P], same[P:]], axis=1))
    put("prefer", (E - np.arange(E))[None, :])
    e = np.arange(E)
    put("expert_before", (e[None, :] < e[:, None]).reshape(1, -1))
    put("slot_tile", np.arange(SLOT_TILES)[None, :])
    return k


def build(nc, x, vecs, rows, weights, w12, w3, consts, out):
    with ExitStack() as ctx:
        def sb(name, shape, dt=F32):
            return ctx.enter_context(nc.sbuf_tensor(name, shape, dt))

        def sem(name):
            return ctx.enter_context(nc.semaphore(name))

        xn_dram = nc.dram_tensor("xn_dram", [N, C], F32).ap()
        slot_x = nc.dram_tensor("slot_x", [SLOTS, C], F32).ap()
        slot_y = nc.dram_tensor("slot_y", [SLOTS, C], F32).ap()

        x_tok = sb("x_tok", [P, N])
        padA = sb("padA", [P, BATCH * PADDED])
        padB = sb("padB", [P, BATCH * PADDED])
        padC = sb("padC", [P, BATCH * PADDED])
        x1_all = sb("x1_all", [P, N])
        act_all = x_tok
        q_all = sb("q_all", [P, N])
        vec = sb("vec", [P, NVEC])
        row = sb("row", [1, 2 * C])
        wts = sb("wts", [P, NWCOL])
        w12s = sb("w12s", [P, E * 2 * EH])
        w3s = sb("w3s", [P, E * 2 * C])
        kon = sb("kon", [P, NSTAY])
        cw1 = sb("cw1", [P, 2])
        krow = sb("krow", [1, C])
        minus_one = sb("minus_one", [P, 1])
        ones_row = sb("ones_row", [1, P])
        neg_half = sb("neg_half", [P, 2, TPC])
        bufs = sb("bufs", [P, 2, CH])
        norm_t = sb("norm_t", [P, 2, CH])
        aff = sb("aff", [P, 2, CH])
        e_q = sb("e_q", [P, 2, CH])
        r_q = sb("r_q", [P, 2, CH])
        k_tok = sb("k_tok", [P, 2, CH])
        v_tok = sb("v_tok", [P, 2, TPC, C + 1])
        hid = sb("hid", [P, 2, 4, CH])
        stats = sb("stats", [P, 2, TPC, 6])
        msum, mdif, vsum, mean, mdif2, vsum2, var_e = (
            sb(n, [P, 2, TPC]) for n in ("msum", "mdif", "vsum", "mean", "mdif2", "vsum2", "var_e"))
        rstd = sb("rstd", [P, 2, TPC])
        lg_c = sb("lg_c", [E, 2, CH])
        kv_sum = sb("kv_sum", [P, BATCH, C + 1])
        kv_s = sb("kv_s", [P, BATCH, C])
        kv_r = sb("kv_r", [P, BATCH, C])
        mk = sb("mk", [P, BATCH, C + HEADS])
        den = sb("den", [P, 2, TPC, HEADS])
        rden = sb("rden", [P, 2, TPC, HEADS])
        spare = hid[:, :, :, :].rearrange("p c i n -> p (c i n)")
        te = NT * E
        lg, eqm, key = (spare[:, i * te:(i + 1) * te].rearrange("p (t e) -> p t e", e=E) for i in range(3))
        oh = spare[:, 3 * te:5 * te].rearrange("p (s t e) -> p s t e", s=2, e=E)
        texp = spare[0:1, 5 * te:5 * te + SLOT_TILES * E].rearrange("p (t e) -> p t e", e=E)
        best = sb("best", [P, 4, NT])
        mask_b = sb("mask_b", [P, NT * E], BF16)
        before_b = sb("before_b", [P, P], BF16)
        tile_b = sb("tile_b", [P, 2 * NT * E], BF16)
        same_b = sb("same_b", [P, 2 * E], BF16)
        ones_b = sb("ones_b", [P, P], BF16)
        tot_b = sb("tot_b", [P, 2, P], BF16)
        tot_c = sb("tot_c", [P, 2])
        slot_f = sb("slot_f", [P, 2, NT])
        slot_i = sb("slot_i", [P, NT, 2], I32)
        prob = sb("prob", [P, 2, NT])
        pt_e = sb("pt_e", [P, 3, NT])
        cnt = sb("cnt", [P, 4, E])
        cnt_i = sb("cnt_i", [P, E], I32)
        ebef = sb("ebef", [P, E, E])
        texp_f = sb("texp_f", [1, SLOT_TILES])
        texp_i = sb("texp_i", [1, SLOT_TILES], I32)
        idx = sb("idx", [P, TPC, 2], I32)
        kon_r = spare[:, 8 * te:8 * te + NKCOL - NSTAY]
        stage = spare[:, 12 * te:12 * te + CH].rearrange("p (t c) -> p t c", c=C)
        xs = sb("xs", [P, 2, C])
        xs_t = sb("xs_t", [P, 2, P])
        s1 = sb("s1", [P, 2, EH])
        gg = sb("gg", [P, 2, EH])
        gg_t = sb("gg_t", [P, 2, 2, P])
        ys = sb("ys", [P, 2, C])
        idx_f = sb("idx_f", [P, 2 * TPC, 2], I32)
        yg = hid[:, :, :, 0:2 * C].rearrange("p c k (s n) -> p c k s n", s=2)
        ffn = r_q

        bank = [ctx.enter_context(nc.psum_tensor(f"bank{i}", [P, 512], F32)) for i in range(8)]
        pt, pu = bank[0:2], bank[2:4]
        mh, my = bank[4:6], bank[6:8]

        def v(name, i=0):
            at, w = VEC[name]
            return vec[:, at + i:at + i + 1]

        def w(name, a=0, b=None):
            at, n = WCOL[name]
            return wts[:, at + a:at + (n if b is None else b)]

        def k(name, parts=P):
            at, n = KCOL[name]
            if at >= NSTAY:
                return kon_r[0:parts, at - NSTAY:at - NSTAY + n]
            return kon[0:parts, at:at + n]

        def tiles(buf, c):
            return [buf[:, c, P * i:P * (i + 1)] for i in range(TPC)]

        class Pair:

            def __init__(self, eng, b, h):
                self.b, self.g = b, eng.snap(b * 2 + h)
                self.pad0 = eng.snap(b * PADDED + h * (2 * CH) + 1)
                self.flat0 = eng.snap(self.g * (2 * CH))
                self.g2 = eng.snap(self.g * 2)
                self.dones = [eng.snap(self.g2 + 1), eng.snap(self.g2 + 2)]
                self.g32 = eng.snap(self.g * 32)
                self.dones16 = [eng.snap(self.g32 + 16), eng.snap(self.g32 + 32)]

            def chunk(self, buf, c, shift=0):
                return buf[:, bass.ds(self.pad0 + (c * CH + shift), CH)]

            def flat(self, buf, c):
                return buf[:, bass.ds(self.flat0 + c * CH, CH)]

            def done(self, c):
                return self.dones[c]

            def nth(self, per_pair, n):
                return self.g * per_pair + n

            def before(self):
                return self.g2

        def each_pair(eng, body):
            with eng.Fori(0, BATCH) as b:
                with eng.Fori(0, 2) as h:
                    body(Pair(eng, b, h))

        ALL = 2 * 2 * BATCH

        names = """ld_x ld_vec ld_row ld_w ld_w12 ld_w3 ld_k
          set_zero set_pads set_const set_cw set_v1 zero_x
          a_st a_mv a_rstd a_xn a_st_dram a_tr a_xnt a_lg a_lgc a_lt a_l
          r_step r_exp r_mask r_totc r_totb r_rank r_done
          s_idx s_load s_scat s_stage
          b_ctr b_left b_x1 b_x1st b_tr b_st b_mv b_rstd b_nm b_back b_aff b_in b_gate b_xi b_act
          c_ctr c_left c_cv c_v c_vst c_q c_rq c_qt c_k c_ek c_kt c_vt c_vtok c_kv c_acc
          f_kvs f_kvr1 f_kvr f_m f_mk
          d_q0 d_q1 d_nd d_de d_rd d_at d_atT d_ctr d_left d_lp d_sum d_ac d_out d_x2
          e_ctr e_left e_x3 e_tr e_st e_mv e_rstd e_nm e_back e_aff e_f1 e_h e_s e_so
          m_ld0 m_ld1 m_xt m_xtc m_h m_s1 m_g m_gt m_gtc m_y m_ys m_st
          o_x0 o_x1 o_idx o_y o_p o_f o_sg o_m o_out o_st""".split()
        S = {n: sem(n) for n in names}

        block = ctx.enter_context(nc.Block())

        @block.sync
        def _(sp):
            for i in range(4):
                sp.dma_start(x_tok[:, i * 1024:(i + 1) * 1024].rearrange("p (t c) -> p t c", c=C),
                             x[i * 1024:(i + 1) * 1024, :].rearrange("(t p) c -> p t c", p=P)).then_inc(S["ld_x"], 16)
            sp.dma_start(w12s[:, :], w12).then_inc(S["ld_w12"], 16)
            sp.dma_start(w3s[:, :], w3).then_inc(S["ld_w3"], 16)

            def store_xn(q):
                for c in range(2):
                    sp.wait_ge(S["a_xn"], q.done(c))
                    sp.dma_start(xn_dram[bass.ds(q.flat0 + c * CH, CH), :].rearrange("(t p) c -> p t c", p=P),
                                 bufs[:, c, :].rearrange("p (t c) -> p t c", c=C)).then_inc(S["a_st_dram"], 16)
            each_pair(sp, store_xn)
            sp.wait_ge(S["set_zero"], 1)
            zero_v = slot_x.rearrange("(p t) c -> p (t c)", p=P)
            for i in range(SLOT_TILES // ZT):
                sp.dma_start(zero_v[:, i * ZT * C:(i + 1) * ZT * C], q_all[:, 0:ZT * C]).then_inc(S["zero_x"], 16)
            sp.wait_ge(S["zero_x"], 16 * (SLOT_TILES // ZT))

            def store_x1(q):
                for c in range(2):
                    sp.wait_ge(S["b_x1"], q.done(c))
                    sp.dma_start(q.flat(x1_all, c), bufs[:, c, :]).then_inc(S["b_x1st"], 16)
            each_pair(sp, store_x1)

            def store_v(q):
                for c in range(2):
                    sp.wait_ge(S["c_v"], q.done(c))
                    sp.dma_start(q.chunk(padC, c), bufs[:, c, :]).then_inc(S["c_vst"], 16)
            each_pair(sp, store_v)

            sp.wait_ge(S["c_qt"], ALL)

            def load_q(q):
                for c in range(2):
                    sp.wait_ge(S["d_nd"], q.before())
                    sp.dma_start(e_q[:, c, :], q.flat(q_all, c)).then_inc(S[f"d_q{c}"], 16)
            each_pair(sp, load_q)

            sp.wait_ge(S["s_scat"], 16 * 2 * NT)
            with sp.Fori(0, SLOT_TILES // 2) as i:
                for u in range(2):
                    sp.wait_ge(S["m_xt"], i * 2)
                    sp.dma_start(xs[:, u, :], slot_x[bass.ds(i * (2 * P) + u * P, P), :]).then_inc(S[f"m_ld{u}"], 16)

            sp.wait_ge(S["d_nd"], ALL)

            def store_out(q):
                for c in range(2):
                    sp.wait_ge(S["o_out"], q.before())
                    sp.dma_start(e_q[:, c, :].rearrange("p (t c) -> p t c", c=C),
                                 x[bass.ds(q.flat0 + c * CH, CH), :].rearrange("(t p) c -> p t c", p=P))\
                        .then_inc(S[f"o_x{c}"], 16)
                for c in range(2):
                    sp.wait_ge(S["o_out"], q.done(c))
                    sp.dma_start(out[bass.ds(q.flat0 + c * CH, CH), :].rearrange("(t p) c -> p t c", p=P),
                                 ffn[:, c, :].rearrange("p (t c) -> p t c", c=C)).then_inc(S["o_st"], 16)
            each_pair(sp, store_out)
            sp.wait_ge(S["o_st"], 16 * ALL)

        @block.gpsimd
        def _(pool):
            pool.memset(neg_half[:, :, :], -0.5).then_inc(S["set_const"], 1)
            pool.memset(q_all[:, 0:ZT * C], 0.0).then_inc(S["set_zero"], 1)
            for buf in (padA, padB, padC):
                edges = buf[:, :].rearrange("p (b n) -> p b n", b=BATCH)
                pool.memset(edges[:, :, 0:PADDED:PADDED - 1], 0.0).then_inc(S["set_pads"], 1)
            pool.wait_ge(S["set_const"], 1)

            def root(var_sem, out_sem, q):
                pool.wait_ge(var_sem, q.nth(3, 3))
                pool.tensor_tensor(rstd[:, :, :], var_e[:, :, :], neg_half[:, :, :], ALU.pow).then_inc(out_sem, 1)

            each_pair(pool, lambda q: root(S["a_mv"], S["a_rstd"], q))
            each_pair(pool, lambda q: root(S["b_mv"], S["b_rstd"], q))

            pool.wait_ge(S["r_done"], 1)
            pool.wait_ge(S["a_st_dram"], 16 * ALL)
            pool.wait_ge(S["zero_x"], 16 * (SLOT_TILES // ZT))
            with pool.Fori(1, NT // TPC + 1) as j:
                pool.wait_ge(S["s_scat"], (j - 1) * (16 * 2 * TPC))
                pool.dma_start(stage[:, :, :], xn_dram[bass.ds((j - 1) * CH, CH), :].rearrange("(t p) c -> p t c", p=P))\
                    .then_inc(S["s_stage"], 16)
                pool.wait_ge(S["s_stage"], j * 16)
                pool.tensor_copy(idx[:, :, :], slot_i[:, bass.ds((j - 1) * TPC, TPC), :]).then_inc(S["s_idx"], 1)
                pool.wait_ge(S["set_const"], 1)
                pool.wait_ge(S["s_idx"], j)
                for i in range(TPC):
                    for s in range(2):
                        pool.indirect_dma_start(out=slot_x[:, :], out_offset=bass.IndirectOffsetOnAxis(idx[:, i, s:s + 1], 0),
                                                in_=stage[:, i, :], in_offset=None).then_inc(S["s_scat"], 16)

            each_pair(pool, lambda q: root(S["e_mv"], S["e_rstd"], q))

            pool.wait_ge(S["m_st"], 16 * SLOT_TILES)

            with pool.Fori(1, ALL // 2 + 1) as j:
                pool.wait_ge(S["o_f"], (j - 1) * 2)
                pool.wait_ge(S["o_y"], (j - 1) * (2 * 16 * 2 * TPC))
                pool.tensor_copy(idx_f[:, :, :], slot_i[:, bass.ds((j - 1) * (2 * TPC), 2 * TPC), :]).then_inc(S["o_idx"], 1)
                pool.wait_ge(S["set_const"], 1)
                pool.wait_ge(S["o_idx"], j)
                for i in range(2 * TPC):
                    for s in range(2):
                        pool.indirect_dma_start(out=yg[:, i // TPC, i % TPC, s, :], out_offset=None, in_=slot_y[:, :],
                                                in_offset=bass.IndirectOffsetOnAxis(idx_f[:, i, s:s + 1], 0))\
                            .then_inc(S["o_y"], 16)

        @block.scalar
        def _(act):
            act.dma_start(kon[:, :], consts[:, 0:NSTAY]).then_inc(S["ld_k"], 16)
            act.dma_start(kon_r, consts[:, NSTAY:NKCOL]).then_inc(S["ld_k"], 16)
            act.dma_start(vec[:, :], vecs).then_inc(S["ld_vec"], 16)
            act.dma_start(row[:, :], rows).then_inc(S["ld_row"], 16)
            act.dma_start(wts[:, :], weights).then_inc(S["ld_w"], 16)
            act.wait_ge(S["ld_vec"], 16)
            act.wait_ge(S["set_cw"], 1)
            act.wait_ge(S["set_v1"], 5)

            def a(q):
                for c in range(2):
                    act.wait_ge(S["a_tr"], q.done(c))
                    nc.scalar.activation(q.chunk(padA, c), pt[c][:, :], ACT.Copy).then_inc(S["a_xnt"], 1)
                for c in range(2):
                    act.wait_ge(S["a_lg"], q.done(c))
                    act.wait_ge(S["a_lt"], q.before())
                    nc.scalar.activation(lg_c[:, c, :], pu[c][0:E, :], ACT.Copy).then_inc(S["a_lgc"], 1)
            each_pair(act, a)

            act.wait_ge(S["r_exp"], 1)
            nc.scalar.activation(pt_e[:, 1, :], pt_e[:, 0, :], ACT.Exp).then_inc(S["r_exp"], 1)

            act.wait_ge(S["set_pads"], 3)
            act.wait_ge(S["a_l"], ALL)

            def b(q):
                for c in range(2):
                    act.wait_ge(S["b_tr"], q.before())
                    act.wait_ge(S["b_x1st"], q.g32)
                    nc.scalar.activation(bufs[:, c, :], q.chunk(padA, c), ACT.Identity, bias=v("cpe1_b"),
                                         scale=cw1[:, 0:1]).then_inc(S["b_ctr"], 1)
                for c in range(2):
                    act.wait_ge(S["b_back"], q.done(c))
                    act.wait_ge(S["b_gate"], q.before())
                    nc.scalar.activation(aff[:, c, :], pu[c][:, :], ACT.Identity, bias=v("norm1_b"),
                                         scale=v("norm1_g")).then_inc(S["b_aff"], 1)
                for c in range(2):
                    act.wait_ge(S["b_in"], q.done(c))
                    nc.scalar.activation(q.chunk(padB, c), pt[c][:, :], ACT.Identity, bias=v("in_b")).then_inc(S["b_xi"], 1)
                    act.wait_ge(S["b_gate"], q.done(c))
                    nc.scalar.activation(q.flat(act_all, c), pu[c][:, :], ACT.Silu, bias=v("actp_b")).then_inc(S["b_act"], 1)
            act.wait_ge(S["a_st_dram"], 16 * ALL)
            act.wait_ge(S["a_xnt"], ALL)
            each_pair(act, b)

            act.wait_ge(S["b_xi"], ALL)
            act.wait_ge(S["b_x1st"], 16 * ALL)

            def cc(q):
                for c in range(2):
                    nc.scalar.activation(norm_t[:, c, :], q.chunk(padB, c), ACT.Identity, bias=v("dwc_b"),
                                         scale=v("dwc_w", 1)).then_inc(S["c_ctr"], 1)
                for c in range(2):
                    act.wait_ge(S["c_cv"], q.done(c))
                    act.wait_ge(S["c_vst"], q.g32)
                    act.wait_ge(S["c_vt"], q.before())
                    nc.scalar.activation(bufs[:, c, :], norm_t[:, c, :], ACT.Silu).then_inc(S["c_v"], 1)
                for c in range(2):
                    act.wait_ge(S["c_q"], q.done(c))
                    act.wait_ge(S["c_qt"], q.before())
                    nc.scalar.activation(e_q[:, c, :], pt[c][:, :], ACT.Exp, bias=v("q_b"))
                    nc.scalar.activation(r_q[:, c, :], pt[c][:, :], ACT.Relu, bias=v("q_b")).then_inc(S["c_rq"], 1)
                    act.wait_ge(S["c_k"], q.done(c))
                    nc.scalar.activation(aff[:, c, :], pu[c][:, :], ACT.Exp, bias=minus_one[:, 0:1]).then_inc(S["c_ek"], 1)
                for c in range(2):
                    act.wait_ge(S["c_vt"], q.done(c))
                    act.wait_ge(S["c_kv"], q.before())
                    nc.scalar.activation(v_tok[:, c, :, 0:C], pt[c][:, :].rearrange("p (k n) -> p k n", k=TPC),
                                         ACT.Copy).then_inc(S["c_vtok"], 1)
            each_pair(act, cc)

            act.wait_ge(S["c_vst"], 16 * ALL)

            def d(q):
                for c in range(2):
                    act.wait_ge(S["d_ac"], q.before())
                    nc.scalar.activation(norm_t[:, c, :], q.chunk(padC, c), ACT.Identity, bias=v("lepe_b"),
                                         scale=v("lepe_w", 1)).then_inc(S["d_ctr"], 1)
            each_pair(act, d)

            act.wait_ge(S["d_x2"], ALL)
            act.wait_ge(S["s_scat"], 16 * 2 * NT)

            def e(q):
                for c in range(2):
                    act.wait_ge(S["e_s"], q.before())
                    nc.scalar.activation(bufs[:, c, :], q.chunk(padA, c), ACT.Identity, bias=v("cpe2_b"),
                                         scale=cw1[:, 1:2]).then_inc(S["e_ctr"], 1)
                for c in range(2):
                    act.wait_ge(S["e_back"], q.done(c))
                    nc.scalar.activation(aff[:, c, :], pu[c][:, :], ACT.Identity, bias=v("norm2_b"),
                                         scale=v("norm2_g")).then_inc(S["e_aff"], 1)
                for i in range(4):
                    for c in range(2):
                        act.wait_ge(S["e_f1"], q.g * 8 + (2 * i + c + 1))
                        nc.scalar.activation(hid[:, c, i, :], (pt, pu)[i % 2][c][:, :], ACT.Gelu,
                                             bias=v("fc1_b", i)).then_inc(S["e_h"], 1)
                for c in range(2):
                    act.wait_ge(S["e_s"], q.done(c))
                    nc.scalar.activation(q.flat(q_all, c), pt[c][:, :], ACT.Copy).then_inc(S["e_so"], 1)
            each_pair(act, e)

            with act.Fori(0, SLOT_TILES // 2) as i:
                for u in range(2):
                    act.wait_ge(S["m_xt"], i * 2 + (u + 1))
                    act.wait_ge(S["m_h"], i * 2)
                    nc.scalar.activation(xs_t[:, u, :], pt[u][:, 0:P], ACT.Copy).then_inc(S["m_xtc"], 1)
                for u in range(2):
                    act.wait_ge(S["m_h"], i * 2 + (u + 1))
                    act.wait_ge(S["m_g"], i * 2)
                    nc.scalar.activation(s1[:, u, :], mh[u][:, 0:EH], ACT.Silu).then_inc(S["m_s1"], 1)
                for u in range(2):
                    act.wait_ge(S["m_gt"], i * 2 + (u + 1))
                    act.wait_ge(S["m_y"], i * 2)
                    nc.scalar.activation(gg_t[:, u, :, :], pu[u][:, 0:EH].rearrange("p (a n) -> p a n", a=2),
                                         ACT.Copy).then_inc(S["m_gtc"], 1)
                for u in range(2):
                    act.wait_ge(S["m_ys"], i * 2 + (u + 1))
                    act.dma_start(slot_y[bass.ds(i * (2 * P) + u * P, P), :], ys[:, u, :]).then_inc(S["m_st"], 16)

            def o(q):
                for c in range(2):
                    act.wait_ge(S["o_f"], q.done(c))
                    act.wait_ge(S["o_out"], q.before())
                    nc.scalar.activation(aff[:, c, :], norm_t[:, c, :], ACT.Silu).then_inc(S["o_sg"], 1)
            each_pair(act, o)

        @block.vector
        def _(dve):
            dve.memset(ones_row[:, :], 1.0).then_inc(S["set_v1"], 1)
            dve.memset(ones_b[:, :], 1.0).then_inc(S["set_v1"], 1)
            dve.memset(minus_one[:, :], -1.0).then_inc(S["set_v1"], 1)
            dve.memset(v_tok[:, :, :, C:C + 1], 1.0).then_inc(S["set_v1"], 1)
            dve.memset(kv_sum[:, :, :], 0.0).then_inc(S["set_v1"], 1)
            dve.wait_ge(S["ld_vec"], 16)
            dve.wait_ge(S["ld_row"], 16)
            dve.wait_ge(S["ld_k"], 32)
            dve.tensor_copy(before_b[:, :], k("before"))
            dve.tensor_copy(tile_b[:, :], k("tile_before"))
            dve.tensor_copy(same_b[:, :], k("same_expert"))
            dve.tensor_scalar(cw1[:, 0:1], v("cpe1_w", 1), 1.0, None, ALU.add)
            dve.tensor_scalar(cw1[:, 1:2], v("cpe2_w", 1), 1.0, None, ALU.add)
            dve.tensor_scalar(krow[:, :], row[:, 0:C], 1.0, None, ALU.add).then_inc(S["set_cw"], 1)

            def layer_norm(q, ph, src, dst, dst_free):
                for c in range(2):
                    for i, t in enumerate(src(c)):
                        ins = dve.bn_stats(stats[:, c, i, :], t)
                    ins.then_inc(S[ph + "_st"], 1)
                m_even, m_odd, v_even, v_odd = (stats[:, :, :, n] for n in (1, 4, 2, 5))
                dve.wait_ge(S[ph + "_st"], q.done(1))
                dve.tensor_tensor(msum[:, :, :], m_even, m_odd, ALU.add)
                dve.tensor_tensor(mdif[:, :, :], m_even, m_odd, ALU.subtract)
                dve.tensor_tensor(vsum[:, :, :], v_even, v_odd, ALU.add).then_inc(S[ph + "_mv"], 1)
                dve.wait_ge(S[ph + "_mv"], q.nth(3, 1))
                dve.tensor_scalar(mean[:, :, :], msum[:, :, :], 0.5, None, ALU.mult)
                dve.tensor_tensor(mdif2[:, :, :], mdif[:, :, :], mdif[:, :, :], ALU.mult)
                dve.tensor_scalar(vsum2[:, :, :], vsum[:, :, :], 1.0 / C, EPS, ALU.mult, ALU.add).then_inc(S[ph + "_mv"], 1)
                dve.wait_ge(S[ph + "_mv"], q.nth(3, 2))
                dve.scalar_tensor_tensor(var_e[:, :, :], mdif2[:, :, :], 0.25, vsum2[:, :, :], ALU.mult, ALU.add)\
                    .then_inc(S[ph + "_mv"], 1)
                for c in range(2):
                    dve.wait_ge(S[ph + "_rstd"], q.nth(1, 1))
                    dst_free(q)
                    for i, t in enumerate(src(c)):
                        ins = dve.tensor_scalar(dst[:, c, P * i:P * (i + 1)], t, mean[:, c, i:i + 1],
                                                rstd[:, c, i:i + 1], ALU.subtract, ALU.mult)
                    ins.then_inc(S[ph + ("_xn" if ph == "a" else "_nm")], 1)

            dve.wait_ge(S["ld_x"], 64)

            def a(q):
                def src(c):
                    return [x_tok[:, bass.ds(q.flat0 + (c * CH + P * i), P)] for i in range(TPC)]

                def free(q):
                    dve.wait_ge(S["a_tr"], q.before())
                    dve.wait_ge(S["a_st_dram"], q.g32)
                layer_norm(q, "a", src, bufs, free)
                for c in range(2):
                    dve.wait_ge(S["a_lt"], q.done(c))
                    dve.tensor_copy(lg[:, bass.ds(q.g * (2 * TPC) + c * TPC, TPC), :],
                                    mh[c][:, 0:TPC * E].rearrange("p (t e) -> p t e", e=E))\
                        .then_inc(S["a_l"], 1)
            each_pair(dve, a)

            dve.wait_ge(S["a_l"], ALL)
            steps = [0]

            def step(ins):
                steps[0] += 1
                ins.then_inc(S["r_step"], 1)

            def settled():
                dve.wait_ge(S["r_step"], steps[0])

            def over_e(a):
                return a.unsqueeze(2).broadcast_to([P, NT, E])

            prefer = k("prefer").unsqueeze(1).broadcast_to([P, NT, E])
            for s in range(2):
                src = lg if s == 0 else eqm
                step(dve.tensor_reduce(best[:, s, :], src[:, :, :], AX.X, ALU.max))
                settled()
                step(dve.tensor_tensor(key[:, :, :], src[:, :, :], over_e(best[:, s, :]), ALU.is_equal))
                settled()
                step(dve.tensor_tensor(key[:, :, :], key[:, :, :], prefer, ALU.mult))
                settled()
                step(dve.tensor_reduce(best[:, 2 + s, :], key[:, :, :], AX.X, ALU.max))
                settled()
                step(dve.tensor_tensor(oh[:, s, :, :], key[:, :, :], over_e(best[:, 2 + s, :]), ALU.is_equal))
                settled()
                if s == 0:
                    step(dve.scalar_tensor_tensor(eqm[:, :, :], oh[:, 0, :, :], -3.0e38, lg[:, :, :], ALU.mult, ALU.add))
                    settled()
            dve.tensor_tensor(mask_b[:, :].rearrange("p (t e) -> p t e", e=E), oh[:, 0, :, :], oh[:, 1, :, :], ALU.add)\
                .then_inc(S["r_mask"], 1)
            dve.tensor_tensor(pt_e[:, 0, :], best[:, 1, :], best[:, 0, :], ALU.subtract).then_inc(S["r_exp"], 1)
            dve.wait_ge(S["r_totc"], 1)
            step(dve.tensor_copy(tot_c[:, :], pt[0][:, 0:2]))
            settled()
            for s in range(2):
                ins = dve.tensor_scalar(tot_b[:, s, :], ones_b[:, :], tot_c[:, s:s + 1], None, ALU.mult)
            ins.then_inc(S["r_totb"], 1)
            dve.wait_ge(S["r_exp"], 2)
            step(dve.tensor_scalar(pt_e[:, 2, :], pt_e[:, 1, :], 1.0, None, ALU.add))
            settled()
            step(dve.reciprocal(prob[:, 0, :], pt_e[:, 2, :]))
            settled()
            step(dve.tensor_tensor(prob[:, 1, :], prob[:, 0, :], pt_e[:, 1, :], ALU.mult))
            dve.wait_ge(S["r_rank"], 1)
            step(dve.tensor_scalar(cnt_i[:, :], pt[1][:, 0:E], float(P - 1), None, ALU.add))
            settled()
            step(dve.tensor_scalar(cnt_i[:, :], cnt_i[:, :], 7, None, ALU.arith_shift_right))
            settled()
            step(dve.tensor_copy(cnt[:, 0, :], cnt_i[:, :]))
            settled()
            step(dve.tensor_tensor(ebef[:, :, :], k("expert_before").rearrange("p (a b) -> p a b", b=E),
                                   cnt[:, 0, :].unsqueeze(1).broadcast_to([P, E, E]), ALU.mult))
            settled()
            step(dve.tensor_reduce(cnt[:, 1, :], ebef[:, :, :], AX.X, ALU.add))
            settled()
            step(dve.tensor_tensor(cnt[:, 2, :], cnt[:, 0, :], cnt[:, 1, :], ALU.add))
            step(dve.scalar_tensor_tensor(eqm[:, :, :], cnt[:, 1, :].unsqueeze(1).broadcast_to([P, NT, E]), float(P),
                                          pu[0][:, 0:NT * E].rearrange("p (t e) -> p t e", e=E), ALU.mult, ALU.add))
            settled()
            for s in range(2):
                step(dve.tensor_tensor(key[:, :, :], oh[:, s, :, :], eqm[:, :, :], ALU.mult))
                settled()
                step(dve.tensor_reduce(slot_f[:, s, :], key[:, :, :], AX.X, ALU.add))
                settled()
            step(dve.tensor_copy(slot_i[:, :, :], slot_f[:, :, :].rearrange("p s t -> p t s")))
            step(dve.tensor_tensor(texp[:, :, :], k("slot_tile", 1).unsqueeze(2).broadcast_to([1, SLOT_TILES, E]),
                                   cnt[0:1, 2, :].unsqueeze(1).broadcast_to([1, SLOT_TILES, E]), ALU.is_ge))
            settled()
            step(dve.tensor_reduce(texp_f[:, :], texp[:, :, :], AX.X, ALU.add))
            settled()
            dve.tensor_scalar(texp_i[:, :], texp_f[:, :], float(E - 1), None, ALU.min).then_inc(S["r_done"], 1)

            def taps(q, ph, buf, src, names, last):
                for c in range(2):
                    dve.wait_ge(S[ph + "_ctr"], q.done(c))
                    dve.scalar_tensor_tensor(buf[:, c, :], q.chunk(src, c, -1), v(names, 0), buf[:, c, :], ALU.mult,
                                             ALU.add).then_inc(S[ph + "_left"], 1)
                for c in range(2):
                    dve.wait_ge(S[ph + "_left"], q.done(c))
                    dve.scalar_tensor_tensor(buf[:, c, :], q.chunk(src, c, 1), v(names, 2), buf[:, c, :], ALU.mult,
                                             ALU.add).then_inc(S[last], 1)

            dve.wait_ge(S["set_pads"], 3)

            def b(q):
                taps(q, "b", bufs, padA, "cpe1_w", "b_x1")
                for c in range(2):
                    dve.wait_ge(S["b_tr"], q.done(c))
                layer_norm(q, "b", lambda c: [pt[c][:, P * i:P * (i + 1)] for i in range(TPC)], norm_t,
                           lambda q: dve.wait_ge(S["b_back"], q.before()))
            each_pair(dve, b)

            dve.wait_ge(S["zero_x"], 16 * (SLOT_TILES // ZT))

            def cc(q):
                taps(q, "c", norm_t, padB, "dwc_w", "c_cv")
                for c in range(2):
                    dve.wait_ge(S["c_rq"], q.done(c))
                    dve.scalar_tensor_tensor(q.flat(q_all, c), e_q[:, c, :], 1.0, r_q[:, c, :], ALU.min, ALU.add)\
                        .then_inc(S["c_qt"], 1)
                    dve.wait_ge(S["c_ek"], q.done(c))
                    dve.wait_ge(S["c_kv"], q.before())
                    dve.scalar_tensor_tensor(k_tok[:, c, :], aff[:, c, :], 1.0, pu[c][:, :], ALU.min, ALU.max)\
                        .then_inc(S["c_kt"], 1)
                for c in range(2):
                    dve.wait_ge(S["c_kv"], q.done(c))
                    acc = kv_sum[:, bass.ds(q.b, 1), :].rearrange("p a n -> p (a n)")
                    dve.wait_ge(S["c_acc"], q.g2 + c)
                    dve.tensor_tensor(acc, acc, pu[c][:, 0:C + 1], ALU.add).then_inc(S["c_acc"], 1)
            each_pair(dve, cc)

            dve.wait_ge(S["c_acc"], ALL)
            for b_ in range(BATCH):
                dve.tensor_scalar(kv_s[:, b_, :], kv_sum[:, b_, 0:C], 1.0 / SEQ, None, ALU.mult).then_inc(S["f_kvs"], 1)
                dve.tensor_scalar(mk[:, b_, C:C + HEADS], k("headmask"), kv_sum[:, b_, C:C + 1], 1.0 / SEQ, ALU.mult,
                                  ALU.mult).then_inc(S["f_mk"], 1)
            for b_ in range(BATCH):
                dve.wait_ge(S["f_kvr1"], b_ + 1)
                dve.tensor_tensor(kv_r[:, b_, :], pt[b_][:, 0:C], k("headblock"), ALU.mult).then_inc(S["f_kvr"], 1)
            for b_ in range(BATCH):
                dve.wait_ge(S["f_m"], b_ + 1)
                dve.tensor_copy(mk[:, b_, 0:C], pu[b_][:, 0:C]).then_inc(S["f_mk"], 1)

            W = C + HEADS

            def d(q):
                halves = [(c, a, (pt, pu)[a][c][:, 0:2 * W].rearrange("p (k n) -> p k n", k=2))
                          for c in range(2) for a in range(2)]
                for c, a, nd in halves:
                    dve.wait_ge(S["d_nd"], q.done(c))
                    ins = dve.tensor_scalar(den[:, c, 2 * a:2 * a + 2, :], nd[:, :, C:W], Z_EPS, None, ALU.add)
                    if a:
                        ins.then_inc(S["d_de"], 1)
                for c in range(2):
                    dve.wait_ge(S["d_de"], q.done(c))
                    dve.reciprocal(rden[:, c, :, :], den[:, c, :, :]).then_inc(S["d_rd"], 1)
                for c, a, nd in halves:
                    dve.wait_ge(S["d_rd"], q.done(c))
                    dve.wait_ge(S["d_atT"], q.before())
                    ins = dve.tensor_tensor(
                        k_tok[:, c, 2 * a * P:(2 * a + 2) * P].rearrange("p (k h d) -> p k h d", k=2, h=HEADS),
                        nd[:, :, 0:C].rearrange("p k (h d) -> p k h d", h=HEADS),
                        rden[:, c, 2 * a:2 * a + 2, :].unsqueeze(3).broadcast_to([P, 2, HEADS, HD]), ALU.mult)
                    if a:
                        ins.then_inc(S["d_at"], 1)
                taps(q, "d", norm_t, padC, "lepe_w", "d_lp")
                for c in range(2):
                    dve.wait_ge(S["d_atT"], q.done(c))
                    dve.wait_ge(S["d_lp"], q.done(c))
                    dve.tensor_tensor(norm_t[:, c, :], norm_t[:, c, :], pt[c][:, :], ALU.add).then_inc(S["d_sum"], 1)
                for c in range(2):
                    dve.wait_ge(S["d_sum"], q.done(c))
                    dve.wait_ge(S["d_out"], q.before())
                    dve.tensor_tensor(aff[:, c, :], norm_t[:, c, :], q.flat(act_all, c), ALU.mult).then_inc(S["d_ac"], 1)
                for c in range(2):
                    dve.wait_ge(S["d_out"], q.done(c))
                    dve.scalar_tensor_tensor(q.chunk(padA, c), pu[c][:, :], v("out_b"), q.flat(x1_all, c), ALU.add,
                                             ALU.add).then_inc(S["d_x2"], 1)
            dve.wait_ge(S["b_x1st"], 16 * ALL)
            dve.wait_ge(S["c_vst"], 16 * ALL)
            each_pair(dve, d)
            dve.wait_ge(S["d_x2"], ALL)

            def e(q):
                taps(q, "e", bufs, padA, "cpe2_w", "e_x3")
                for c in range(2):
                    dve.wait_ge(S["e_tr"], q.done(c))
                layer_norm(q, "e", lambda c: [pt[c][:, P * i:P * (i + 1)] for i in range(TPC)], norm_t,
                           lambda q: dve.wait_ge(S["e_back"], q.before()))
            each_pair(dve, e)

            with dve.Fori(0, SLOT_TILES // 2) as i:
                for u in range(2):
                    dve.wait_ge(S["m_s1"], i * 2 + (u + 1))
                    dve.wait_ge(S["m_gt"], i * 2)
                    dve.tensor_tensor(gg[:, u, :], s1[:, u, :], mh[u][:, EH:2 * EH], ALU.mult).then_inc(S["m_g"], 1)
                for u in range(2):
                    dve.wait_ge(S["m_y"], i * 2 + (u + 1))
                    dve.wait_ge(S["m_st"], i * 32)
                    dve.tensor_copy(ys[:, u, :], my[u][:, 0:C]).then_inc(S["m_ys"], 1)

            def o(q):
                for c in range(2):
                    dve.wait_ge(S["o_y"], (q.g + 1) * (2 * 16 * 2 * TPC))
                    for i in range(TPC):
                        ins = dve.tensor_scalar(norm_t[:, c, P * i:P * (i + 1)], yg[:, c, i, 0, :],
                                                prob[:, 0, bass.ds(q.g * (2 * TPC) + (c * TPC + i), 1)], None, ALU.mult)
                    ins.then_inc(S["o_p"], 1)
                    dve.wait_ge(S["o_p"], q.done(c))
                    for i in range(TPC):
                        t = norm_t[:, c, P * i:P * (i + 1)]
                        ins = dve.scalar_tensor_tensor(t, yg[:, c, i, 1, :],
                                                       prob[:, 1, bass.ds(q.g * (2 * TPC) + (c * TPC + i), 1)], t,
                                                       ALU.mult, ALU.add)
                    ins.then_inc(S["o_f"], 1)
                for c in range(2):
                    dve.wait_ge(S["o_sg"], q.done(c))
                    dve.wait_ge(S["o_st"], q.g32)
                    dve.tensor_tensor(ffn[:, c, :], aff[:, c, :], q.flat(q_all, c), ALU.mult).then_inc(S["o_m"], 1)
                for c in range(2):
                    dve.wait_ge(S["o_m"], q.done(c))
                    dve.wait_ge(S[f"o_x{c}"], q.nth(1, 1) * 16)
                    dve.tensor_tensor(ffn[:, c, :], ffn[:, c, :], e_q[:, c, :], ALU.add).then_inc(S["o_out"], 1)
            dve.wait_ge(S["e_so"], ALL)
            each_pair(dve, o)

        @block.tensor
        def _(pe):
            ident = k("ident")
            pe.wait_ge(S["ld_k"], 32)
            pe.wait_ge(S["ld_w"], 16)
            pe.wait_ge(S["set_cw"], 1)
            pe.wait_ge(S["set_v1"], 5)

            def turn(dst, src, c, done):
                for i, t in enumerate(tiles(src, c)):
                    mm = nc.tensor.transpose(dst[c][:, P * i:P * (i + 1)], t, ident)
                mm.then_inc(S[done], 1)

            def a(q):
                for c in range(2):
                    pe.wait_ge(S["a_xn"], q.done(c))
                    pe.wait_ge(S["a_xnt"], q.before())
                    turn(pt, bufs, c, "a_tr")
                for c in range(2):
                    pe.wait_ge(S["a_xnt"], q.done(c))
                    pe.wait_ge(S["a_lgc"], q.before())
                    nc.tensor.matmul(pu[c][0:E, :], w("wg"), q.chunk(padA, c), start=True, stop=True).then_inc(S["a_lg"], 1)
                for c in range(2):
                    pe.wait_ge(S["set_v1"], 1)
                    pe.wait_ge(S["a_lgc"], q.done(c))
                    pe.wait_ge(S["a_l"], q.before())
                    for i in range(TPC):
                        mm = nc.tensor.transpose(mh[c][:, i * E:(i + 1) * E], lg_c[:, c, P * i:P * (i + 1)], ident[0:E, 0:E])
                    mm.then_inc(S["a_lt"], 1)
            each_pair(pe, a)

            pe.wait_ge(S["r_mask"], 1)
            for s in range(2):
                mm = nc.tensor.matmul(pt[0][:, s:s + 1], mask_b[:, s * P:(s + 1) * P], ones_b[:, 0:1], start=True, stop=True)
            mm.then_inc(S["r_totc"], 1)
            pe.wait_ge(S["r_totb"], 1)
            for s in range(2):
                nc.tensor.matmul(pu[0][:, 0:NT * E], tot_b[:, s, :], tile_b[:, s * NT * E:(s + 1) * NT * E],
                                 start=(s == 0), stop=False)
            nc.tensor.matmul(pu[0][:, 0:NT * E], before_b[:, :], mask_b[:, :], start=False, stop=True)
            for s in range(2):
                mm = nc.tensor.matmul(pt[1][:, 0:E], tot_b[:, s, :], same_b[:, s * E:(s + 1) * E],
                                      start=(s == 0), stop=(s == 1))
            mm.then_inc(S["r_rank"], 1)

            def b(q):
                for c in range(2):
                    pe.wait_ge(S["b_x1"], q.done(c))
                    pe.wait_ge(S["b_xi"], q.before())
                    turn(pt, bufs, c, "b_tr")
                for c in range(2):
                    pe.wait_ge(S["b_nm"], q.done(c))
                    pe.wait_ge(S["b_act"], q.before())
                    turn(pu, norm_t, c, "b_back")
                for c in range(2):
                    pe.wait_ge(S["b_aff"], q.done(c))
                    nc.tensor.matmul(pt[c][:, :], w("in_w"), aff[:, c, :], start=True, stop=True).then_inc(S["b_in"], 1)
                    nc.tensor.matmul(pu[c][:, :], w("actp_w"), aff[:, c, :], start=True, stop=True).then_inc(S["b_gate"], 1)
            pe.wait_ge(S["r_done"], 1)
            each_pair(pe, b)

            pe.wait_ge(S["b_act"], ALL)

            def cc(q):
                for c in range(2):
                    pe.wait_ge(S["c_v"], q.done(c))
                    pe.wait_ge(S["c_vtok"], q.before())
                    nc.tensor.matmul(pt[c][:, :], w("q_w"), bufs[:, c, :], start=True, stop=True).then_inc(S["c_q"], 1)
                    pe.wait_ge(S["c_acc"], q.before())
                    for i, t in enumerate(tiles(bufs, c)):
                        o_ = pu[c][:, P * i:P * (i + 1)]
                        nc.tensor.matmul(o_, t, w("k_w"), start=True, stop=False)
                        mm = nc.tensor.matmul(o_, ones_row[:, :], krow[:, :], start=False, stop=True)
                    mm.then_inc(S["c_k"], 1)
                for c in range(2):
                    pe.wait_ge(S["c_rq"], q.done(c))
                    turn(pt, bufs, c, "c_vt")
                for c in range(2):
                    pe.wait_ge(S["c_kt"], q.done(c))
                    pe.wait_ge(S["c_vtok"], q.done(c))
                    for i, t in enumerate(tiles(k_tok, c)):
                        mm = nc.tensor.matmul(pu[c][:, 0:C + 1], t, v_tok[:, c, i, :], start=(i == 0), stop=(i == TPC - 1))
                    mm.then_inc(S["c_kv"], 1)
            each_pair(pe, cc)

            for b_ in range(BATCH):
                pe.wait_ge(S["f_kvs"], b_ + 1)
                nc.tensor.matmul(pt[b_][:, 0:C], k("rope"), kv_s[:, b_, :], start=True, stop=True).then_inc(S["f_kvr1"], 1)
            for b_ in range(BATCH):
                pe.wait_ge(S["f_kvr"], b_ + 1)
                nc.tensor.matmul(pu[b_][:, 0:C], k("rope_t"), kv_r[:, b_, :], start=True, stop=True).then_inc(S["f_m"], 1)

            pe.wait_ge(S["f_mk"], 2 * BATCH)
            W = C + HEADS

            def d(q):
                for c in range(2):
                    pe.wait_ge(S[f"d_q{c}"], q.nth(1, 1) * 16)
                    pe.wait_ge(S["d_x2"], q.before())
                    for i, t in enumerate(tiles(e_q, c)):
                        mm = nc.tensor.matmul((pt, pu)[i // 2][c][:, (i % 2) * W:(i % 2 + 1) * W], t,
                                              mk[:, bass.ds(q.b, 1), :].rearrange("p a n -> p (a n)"),
                                              start=True, stop=True)
                    mm.then_inc(S["d_nd"], 1)
                for c in range(2):
                    pe.wait_ge(S["d_at"], q.done(c))
                    turn(pt, k_tok, c, "d_atT")
                for c in range(2):
                    pe.wait_ge(S["d_ac"], q.done(c))
                    nc.tensor.matmul(pu[c][:, :], w("out_w"), aff[:, c, :], start=True, stop=True).then_inc(S["d_out"], 1)
            each_pair(pe, d)

            pe.wait_ge(S["d_x2"], ALL)

            def e(q):
                for c in range(2):
                    pe.wait_ge(S["e_x3"], q.done(c))
                    pe.wait_ge(S["e_so"], q.before())
                    turn(pt, bufs, c, "e_tr")
                for c in range(2):
                    pe.wait_ge(S["e_nm"], q.done(c))
                    pe.wait_ge(S["e_h"], q.g * 8)
                    turn(pu, norm_t, c, "e_back")
                for i in range(4):
                    for c in range(2):
                        if i == 0:
                            pe.wait_ge(S["e_aff"], q.done(c))
                        if i >= 2:
                            pe.wait_ge(S["e_h"], q.g * 8 + (2 * (i - 2) + c + 1))
                        nc.tensor.matmul((pt, pu)[i % 2][c][:, :], w("fc1_w", C * i, C * (i + 1)), aff[:, c, :],
                                         start=True, stop=True).then_inc(S["e_f1"], 1)
                for c in range(2):
                    pe.wait_ge(S["e_h"], q.g * 8 + (6 + c + 1))
                    for i, t in enumerate(tiles(bufs, c)):
                        o_ = pt[c][:, P * i:P * (i + 1)]
                        nc.tensor.matmul(o_, t, ident, start=True, stop=False)
                        for m in range(4):
                            nc.tensor.matmul(o_, hid[:, c, m, P * i:P * (i + 1)], w("fc2_w", C * m, C * (m + 1)),
                                             start=False, stop=False)
                        mm = nc.tensor.matmul(o_, ones_row[:, :], row[:, C:2 * C], start=False, stop=True)
                    mm.then_inc(S["e_s"], 1)
            each_pair(pe, e)

            pe.wait_ge(S["ld_w12"], 16)
            pe.wait_ge(S["ld_w3"], 16)
            pe.wait_ge(S["e_so"], ALL)
            with pe.Fori(0, SLOT_TILES // 2) as i:
                ex = [pe.value_load(texp_i[0:1, bass.ds(i * 2 + u, 1)], min_val=0, max_val=E - 1) for u in range(2)]
                for u in range(2):
                    pe.wait_ge(S[f"m_ld{u}"], (i + 1) * 16)
                    nc.tensor.transpose(pt[u][:, 0:P], xs[:, u, :], ident).then_inc(S["m_xt"], 1)
                for u in range(2):
                    pe.wait_ge(S["m_xtc"], i * 2 + (u + 1))
                    pe.wait_ge(S["m_g"], i * 2)
                    nc.tensor.matmul(mh[u][:, :], xs_t[:, u, :], w12s[:, bass.ds(ex[u] * (2 * EH), 2 * EH)],
                                     start=True, stop=True).then_inc(S["m_h"], 1)
                for u in range(2):
                    pe.wait_ge(S["m_g"], i * 2 + (u + 1))
                    for a_ in range(2):
                        mm = nc.tensor.transpose(pu[u][:, a_ * P:(a_ + 1) * P],
                                                 gg[:, u, a_ * P:(a_ + 1) * P], ident)
                    mm.then_inc(S["m_gt"], 1)
                for u in range(2):
                    pe.wait_ge(S["m_gtc"], i * 2 + (u + 1))
                    pe.wait_ge(S["m_ys"], i * 2)
                    for a_ in range(2):
                        mm = nc.tensor.matmul(my[u][:, 0:C], gg_t[:, u, a_, :],
                                              w3s[:, bass.ds(ex[u] * (2 * C) + a_ * C, C)],
                                              start=(a_ == 0), stop=(a_ == 1))
                    mm.then_inc(S["m_y"], 1)


def kernel(**inputs):
    import concourse.bacc as bacc
    from concourse.bass_utils import run_bass_kernel_spmd

    f = {n: np.asarray(a) for n, a in inputs.items()}
    A = {n[len("L0_attn_"):]: a for n, a in f.items() if n.startswith("L0_attn_")}
    vecs = np.zeros((P, NVEC), np.float32)
    for name, (at, width) in VEC.items():
        src = A["qk_b"][:C] if name == "q_b" else A[name]
        vecs[:, at:at + width] = src.reshape(width, P).T if name == "fc1_b" else src.reshape(P, width)
    rows = np.concatenate([A["qk_b"][C:], A["fc2_b"]])[None, :]
    weights = np.concatenate([A["in_w"], A["actp_w"], A["qk_w"], A["out_w"], A["fc1_w"],
                              A["fc2_w"].reshape(4, P, C).transpose(1, 0, 2).reshape(P, 4 * C), f["L0_ffn_Wg"].T], axis=1)
    w12 = np.concatenate([f["L0_ffn_W1"].transpose(2, 0, 1), f["L0_ffn_W2"].transpose(2, 0, 1)], axis=2).reshape(P, -1)
    w3 = f["L0_ffn_W3"].transpose(0, 2, 1).reshape(E, 2, P, C).transpose(2, 0, 1, 3).reshape(P, -1)
    arrays = {"x": A["x"].reshape(N, C), "vecs": vecs, "rows": rows, "weights": weights, "w12": w12, "w3": w3,
              "consts": shape_constants()}
    arrays = {n: np.ascontiguousarray(a) for n, a in arrays.items()}

    nc = bacc.Bacc("TRN2", target_bir_lowering=False, num_devices=1)
    args = [nc.dram_tensor(n, a.shape, mybir.dt.from_np(a.dtype), kind="ExternalInput").ap() for n, a in arrays.items()]
    out = nc.dram_tensor("out", (N, C), F32, kind="ExternalOutput").ap()
    build(nc, *args, out)
    r = run_bass_kernel_spmd(nc, [arrays], core_ids=[0])
    return r.results[0]["out"].reshape(BATCH, SEQ, C)
```

```python
from contextlib import ExitStack

import numpy as np
import concourse.bass as bass
from concourse import mybir

F32 = mybir.dt.float32
BF16 = mybir.dt.bfloat16
I32 = mybir.dt.int32
ALU = mybir.AluOpType
ACT = mybir.ActivationFunctionType
AX = mybir.AxisListType

P = 128
BATCH, SEQ, C = 2, 2048, 128
HEADS = 16
HD = C // HEADS
HID = 4 * C
E = 8
EH = 2 * C
N = BATCH * SEQ
NT = N // P
CH = 512
TPC = CH // P
PADDED = SEQ + 2
EPS = 1e-5
Z_EPS = 1e-6
SLOT_TILES = 2 * NT + E
SLOTS = SLOT_TILES * P
ZT = 9
ROW = C + 2
NOWHERE = 1 << 20
MOE_D, MOE_E = 4, 5
assert 2 * BATCH * (MOE_D + MOE_E) * 2 == SLOT_TILES

D_ORDER = ("ctr nd0 X0 nd1 H0.0 H0.1 at0 X1 G0 H1.0 Y0 H1.1 at1 X2 G1 H2.0 Y1 out0 H2.1 X3 G2 H3.0 Y2 out1 H3.1 "
           "G3 Y3").split()
E_ORDER = ("X0 ctr H0.0 H0.1 X1 tr0 G0 tr1 H1.0 Y0 H1.1 mv X2 G1 H2.0 nm0 Y1 nm1 bk0 H2.1 bk1 X3 fc1.0.0 G2 fc1.0.1 "
           "H3.0 Y2 fc1.1.0 fc1.1.1 H3.1 fc1.2.0 X4 G3 fc1.2.1 H4.0 Y3 fc1.3.0 H4.1 fc1.3.1 fc2.0 G4 fc2.1 Y4 st0 st1").split()

VEC = {}
_c = 0
for _name, _w in (("cpe1_w", 3), ("cpe1_b", 1), ("norm1_g", 1), ("norm1_b", 1), ("in_b", 1), ("actp_b", 1),
                  ("dwc_w", 3), ("dwc_b", 1), ("q_b", 1), ("lepe_w", 3), ("lepe_b", 1), ("out_b", 1),
                  ("cpe2_w", 3), ("cpe2_b", 1), ("norm2_g", 1), ("norm2_b", 1), ("fc1_b", 4), ("fc2_b", 1)):
    VEC[_name] = (_c, _w)
    _c += _w
NVEC = _c

WCOL = {}
_c = 0
for _name, _w in (("in_w", C), ("actp_w", C), ("q_w", C), ("k_w", C), ("out_w", C), ("fc1_w", HID),
                  ("fc2_w", 4 * C), ("wg", E)):
    WCOL[_name] = (_c, _w)
    _c += _w
NWCOL = _c

KCOL = {}
_c = 0
for _name, _w in (("ident", P), ("headblock", P), ("rope", P), ("rope_t", P), ("headmask", HEADS),
                  ("before", P), ("tile_before", 2 * NT * E), ("same_expert", 2 * E), ("prefer", E),
                  ("expert_before", E * E), ("slot_tile", SLOT_TILES)):
    if _name == "before":
        NSTAY = _c
    KCOL[_name] = (_c, _w)
    _c += _w
NKCOL = _c


def shape_constants():
    k = np.zeros((P, NKCOL), np.float32)

    def put(name, a):
        at, w = KCOL[name]
        k[:, at:at + w] = a

    i = np.arange(P)
    put("ident", np.eye(P))
    put("headblock", i[:, None] // HD == i[None, :] // HD)
    half = np.arange(C // 2, dtype=np.float32)
    theta = np.float32(1.0) / np.float32(10000.0) ** (half / np.float32(C // 2))
    cos, sin = np.cos(theta), np.sin(theta)
    rope = np.zeros((C, C), np.float32)
    even, odd = 2 * np.arange(C // 2), 2 * np.arange(C // 2) + 1
    rope[even, even], rope[odd, even] = cos, -sin
    rope[even, odd], rope[odd, odd] = sin, cos
    put("rope", rope)
    put("rope_t", rope.T)
    put("headmask", i[:, None] // HD == np.arange(HEADS)[None, :])
    put("before", i[:, None] < i[None, :])
    te = np.arange(NT * E)
    earlier = (te[:, None] % E == te[None, :] % E) & (te[:, None] // E < te[None, :] // E)
    put("tile_before", np.concatenate([earlier[:P], earlier[P:]], axis=1))
    same = te[:, None] % E == np.arange(E)[None, :]
    put("same_expert", np.concatenate([same[:P], same[P:]], axis=1))
    put("prefer", (E - np.arange(E))[None, :])
    e = np.arange(E)
    put("expert_before", (e[None, :] < e[:, None]).reshape(1, -1))
    put("slot_tile", np.arange(SLOT_TILES)[None, :])
    return k


def build(nc, x, vecs, k_bias, weights, w12, w3, consts, result_rows, out):
    with ExitStack() as ctx:
        def sb(name, shape, dt=F32):
            return ctx.enter_context(nc.sbuf_tensor(name, shape, dt))

        xn_dram = nc.dram_tensor("xn_dram", [N, C], F32).ap()
        slot_x = nc.dram_tensor("slot_x", [SLOTS, ROW], F32).ap()
        y_tok = nc.dram_tensor("y_tok", [2 * N, C], F32).ap()

        x_tok = sb("x_tok", [P, N])
        act_all = x_tok
        padA = sb("padA", [P, BATCH * PADDED])
        pad_bc = sb("pad_bc", [P, 2 * BATCH * PADDED])
        padB = pad_bc[:, 0:BATCH * PADDED]
        padC = pad_bc[:, BATCH * PADDED:]
        x1_all = sb("x1_all", [P, N])
        q_all = sb("q_all", [P, N])
        vec = sb("vec", [P, NVEC])
        wts = sb("wts", [P, NWCOL])
        w12s = sb("w12s", [P, E * 2 * EH])
        w3s = sb("w3s", [P, E * 2 * C])
        kon = sb("kon", [P, NSTAY])
        cw1 = sb("cw1", [P, 2])
        kb1 = sb("kb1", [P, C])
        minus_one = sb("minus_one", [P, 1])
        neg_half = sb("neg_half", [P, 2, TPC])
        mark = sb("mark", [P, 1])
        wide = TPC * (C + 1)
        first_two = sb("first_two", [P, 2 * (4 * CH + wide)])
        last_two = sb("last_two", [P, max(2 * (4 * CH + wide), MOE_E * 2 * (ROW + C) + 4 * 2 * EH + 2 * 2 * P)])
        bufs, norm_t, aff, e_q = ([(first_two, last_two)[c // 2][:, (2 * n + c % 2) * CH:(2 * n + c % 2 + 1) * CH]
                                   for c in range(4)] for n in range(4))
        v_tok = [(first_two, last_two)[c // 2][:, 8 * CH + c % 2 * wide:8 * CH + (c % 2 + 1) * wide].rearrange(
            "p (k n) -> p k n", k=TPC) for c in range(4)]
        k_tok = norm_t
        att = sb("att", [P, 2, CH])
        hid = sb("hid", [P, 2, 4, CH])
        stats = sb("stats", [P, 4, TPC, 6])
        msum, mdif, vsum, mean, mdif2, vsum2, var_e = (
            sb(n, [P, 4, TPC]) for n in ("msum", "mdif", "vsum", "mean", "mdif2", "vsum2", "var_e"))
        rstd = sb("rstd", [P, 4, TPC])
        kv_sum = sb("kv_sum", [P, BATCH, C + 1])
        kv_s = sb("kv_s", [P, BATCH, C])
        kv_r = sb("kv_r", [P, BATCH, C])
        mk = sb("mk", [P, BATCH, C + HEADS])
        den = sb("den", [P, 2, TPC, HEADS])
        rden = sb("rden", [P, 2, TPC, HEADS])
        te = NT * E
        spare = hid[:, :, :, :].rearrange("p c i n -> p (c i n)")
        lg, eqm, key = (spare[:, i * te:(i + 1) * te].rearrange("p (t e) -> p t e", e=E) for i in range(3))
        oh = spare[:, 3 * te:5 * te].rearrange("p (s t e) -> p s t e", s=2, e=E)
        texp = spare[0:1, 5 * te:5 * te + SLOT_TILES * E].rearrange("p (t e) -> p t e", e=E)
        kon_r = spare[:, 8 * te:8 * te + NKCOL - NSTAY]
        stage_at = 8 * te + NKCOL - NSTAY
        stage = spare[:, stage_at:stage_at + 2 * TPC * ROW].rearrange("p (s t c) -> p s t c", s=2, c=ROW)
        kx = [spare[:, c * CH:(c + 1) * CH] for c in range(4)]
        lg_c = e_q
        best = sb("best", [P, 4, NT])
        mask_b = sb("mask_b", [P, NT * E], BF16)
        before_b = sb("before_b", [P, P], BF16)
        tile_b = sb("tile_b", [P, 2 * NT * E], BF16)
        same_b = sb("same_b", [P, 2 * E], BF16)
        ones_b = sb("ones_b", [P, P], BF16)
        tot_b = sb("tot_b", [P, 2, P], BF16)
        tot_c = sb("tot_c", [P, 2])
        slot_f = sb("slot_f", [P, 2, NT])
        res_rows = sb("res_rows", [P, NT, 2], I32)
        slot_i = sb("slot_i", [P, NT, 2], I32)
        prob = sb("prob", [P, NT, 2])
        pt_e = sb("pt_e", [P, 3, NT])
        cnt = sb("cnt", [P, 3, E])
        cnt_i = sb("cnt_i", [P, 2, E], I32)
        ebef = sb("ebef", [P, E, E])
        texp_f = sb("texp_f", [1, SLOT_TILES])
        texp_i = sb("texp_i", [1, SLOT_TILES], I32)
        idx = sb("idx", [P, TPC, 2], I32)
        def parts(*sizes):
            at = 0
            for size in sizes:
                yield last_two[:, at:at + size]
                at += size
        xs, ys, xs_t, s1, s2, gg, gg_t = parts(MOE_E * 2 * ROW, MOE_E * 2 * C, 2 * 2 * P, 2 * EH, 2 * EH, 2 * EH, 2 * 2 * P)
        xs = xs.rearrange("p (r u c) -> p r u c", r=MOE_E, u=2)
        ys = ys.rearrange("p (r u c) -> p r u c", r=MOE_E, u=2)
        xs_t = xs_t.rearrange("p (r u n) -> p r u n", r=2, u=2)
        s1, s2, gg = (a.rearrange("p (u n) -> p u n", u=2) for a in (s1, s2, gg))
        gg_t = gg_t.rearrange("p (u a n) -> p u a n", u=2, a=2)
        y_all = pad_bc[:, 0:2 * N]
        x_again = x1_all
        res = spare

        bank = [ctx.enter_context(nc.psum_tensor(f"bank{i}", [P, 512], F32)) for i in range(8)]
        pt, pu = bank[0:2], bank[2:4]
        mh, mxy, mg = bank[4:6], bank[6], bank[7]
        tq, uq = bank[0:4], bank[4:8]

        def v(name, i=0):
            at, w = VEC[name]
            return vec[:, at + i:at + i + 1]

        def w(name, a=0, b=None):
            at, n = WCOL[name]
            return wts[:, at + a:at + (n if b is None else b)]

        def k(name, parts=P):
            at, n = KCOL[name]
            if at >= NSTAY:
                return kon_r[0:parts, at - NSTAY:at - NSTAY + n]
            return kon[0:parts, at:at + n]

        def tiles(buf, c):
            return [buf[c][:, P * i:P * (i + 1)] for i in range(TPC)]

        WD = C + HEADS
        CHUNKS = 2 * 2 * BATCH
        ALL = CHUNKS + 2

        class Body:

            def __init__(self, eng, n, b, g, at):
                self.b, self.n, self.g = b, n, g
                self.pad0 = eng.snap(b * PADDED + at + 1)
                self.flat0 = eng.snap(b * SEQ + at)
                self.g_n = eng.snap(g * n + 2)

            def chunk(self, buf, c, shift=0):
                return buf[:, bass.ds(self.pad0 + (c * CH + shift), CH)]

            def flat(self, buf, c):
                return buf[:, bass.ds(self.flat0 + c * CH, CH)]

            def done(self, c):
                return self.g_n + (c + 1)

            def nth(self, per_body, n):
                return self.g * per_body + n

            def before(self):
                return self.g_n

            def stored(self):
                return self.g_n * 16

        def each_pair(eng, body):
            with eng.Fori(0, BATCH) as b:
                with eng.Fori(0, 2) as h:
                    body(Body(eng, 2, b, eng.snap(b * 2 + h), h * (2 * CH)))

        def each_batch(eng, body):
            with eng.Fori(0, BATCH) as b:
                body(Body(eng, 4, b, b, 0))

        class Slots:

            def __init__(self, eng, q, in_e):
                self.per = MOE_E if in_e else MOE_D
                self.first = 2 * BATCH * MOE_D if in_e else 0
                self.g = q.g
                self.p0 = eng.snap(q.g * self.per + self.first)

            def done(self, r):
                return self.p0 + (r + 3)

            def done_u(self, r, u):
                return self.p0 * 2 + (2 * r + u + 5)

            def uses(self, r):
                return self.g + ((2 * BATCH if self.first and r < MOE_D else 0) + 1)

        USES = [2 * BATCH * (1 + (r < MOE_D)) for r in range(MOE_E)]

        names = """ld_x ld_vec ld_w ld_wg ld_w12 ld_w3 ld_k ld_rows ld_kb
          set_zero set_pads set_const set_cw set_v1 zero_x
          a_st a_mv a_rstd r_step r_exp r_mask r_totc r_totb r_rank r_done s_idx s_scat s_stage
          b_st b_mv b_rstd f_kvs f_kvr1 f_kvr f_m f_mk d_q0 d_q1 e_st e_mv e_rstd e_f1 e_h
          m_ld0 m_ld1 m_ld2 m_ld3 m_ld4 m_st0 m_st1 m_st2 m_st3 m_st4 m_a ld_x2 o_y0 o_y1 carried""".split()
        by_chunk = {
            "vector": "a_xn a_l b_left b_x1 b_nm c_left c_cv c_kb c_qt c_kt c_acc d_de d_rd d_at d_left d_lp d_sum d_ac "
                      "d_x2 e_left e_x3 e_nm e_sum o_f o_m",
            "scalar": "a_xnt a_lgc b_ctr b_aff b_xi b_act c_ctr c_v c_rq c_ek c_vtok d_ctr e_ctr e_aff e_so o_sg",
            "tensor": "a_tr a_lg a_lt b_tr b_back b_in b_gate c_q c_k c_vt c_kv d_nd d_atT d_out e_tr e_back e_s e_sT",
            "gpsimd": "o_out",
        }
        by_slots = {"tensor": "m_xt m_gt m_y", "scalar": "m_xtc m_gtc", "vector": "m_ys"}
        by_tile = {"tensor": "m_h", "scalar": "m_s1", "vector": "m_g"}
        stores = ("a_st_dram", "b_x1st", "c_vst", "o_st")
        for group in (by_chunk, by_slots, by_tile):
            for listed in group.values():
                names += listed.split()
        names += stores
        S = {n: ctx.enter_context(nc.semaphore(n)) for n in names}

        def prime(eng, which):
            for group, n in ((by_chunk, 2), (by_slots, 2), (by_tile, 4)):
                for name in group.get(which, "").split():
                    eng.sem_inc(S[name], n)

        block = ctx.enter_context(nc.Block())

        @block.sync
        def _(sp):
            for i in range(4):
                sp.dma_start(x_tok[:, i * 1024:(i + 1) * 1024].rearrange("p (t c) -> p t c", c=C),
                             x[i * 1024:(i + 1) * 1024, :].rearrange("(t p) c -> p t c", p=P)).then_inc(S["ld_x"], 16)
            for name in stores:
                sp.sem_inc(S[name], 32)

            def store_xn(q):
                for c in range(4):
                    sp.wait_ge(S["a_xn"], q.done(c))
                    sp.dma_start(xn_dram[bass.ds(q.flat0 + c * CH, CH), :].rearrange("(t p) c -> p t c", p=P),
                                 bufs[c][:, :].rearrange("p (t c) -> p t c", c=C)).then_inc(S["a_st_dram"], 16)
            each_batch(sp, store_xn)
            sp.wait_ge(S["set_zero"], 2)
            zero_v = slot_x.rearrange("(p t) c -> p (t c)", p=P)
            for i in range(SLOT_TILES // ZT):
                sp.dma_start(zero_v[:, i * ZT * ROW:(i + 1) * ZT * ROW], q_all[:, 0:ZT * ROW]).then_inc(S["zero_x"], 16)
            sp.dma_start(w12s[:, :], w12).then_inc(S["ld_w12"], 16)
            sp.dma_start(w3s[:, :], w3).then_inc(S["ld_w3"], 16)

            def store_x1(q):
                for c in range(4):
                    sp.wait_ge(S["b_x1"], q.done(c))
                    sp.dma_start(q.flat(x1_all, c), bufs[c][:, :]).then_inc(S["b_x1st"], 16)
            each_batch(sp, store_x1)

            def store_v(q):
                for c in range(4):
                    sp.wait_ge(S["c_v"], q.done(c))
                    sp.dma_start(q.chunk(padC, c), bufs[c][:, :]).then_inc(S["c_vst"], 16)
            each_batch(sp, store_v)

            def load_slots(t, r):
                sp.wait_ge(S[f"m_st{r}"], t.uses(r) * 32)
                sp.dma_start(xs[:, r, :, :], slot_x[bass.ds((t.p0 + r) * (2 * P), 2 * P), :].rearrange(
                    "(u p) c -> p u c", p=P)).then_inc(S[f"m_ld{r}"], 16)

            sp.wait_ge(S["c_acc"], ALL)
            sp.wait_ge(S["c_vst"], 16 * ALL)
            sp.wait_ge(S["s_scat"], 16 * 2 * NT)

            def d(q):
                for c in range(2):
                    sp.wait_ge(S["d_nd"], q.before())
                    sp.dma_start(e_q[c][:, :], q.flat(q_all, c)).then_inc(S[f"d_q{c}"], 16)
                t = Slots(sp, q, False)
                for r in range(MOE_D):
                    load_slots(t, r)
            each_pair(sp, d)

            def e(q):
                t = Slots(sp, q, True)
                for r in range(MOE_E):
                    load_slots(t, r)
                sp.wait_ge(S["d_x2"], ALL)
                sp.dma_start(x_again[:, bass.ds(q.flat0, 2 * CH)].rearrange("p (t c) -> p t c", c=C),
                             x[bass.ds(q.flat0, 2 * CH), :].rearrange("(t p) c -> p t c", p=P)).then_inc(S["ld_x2"], 16)
            each_pair(sp, e)

            for r in range(MOE_E):
                sp.wait_ge(S[f"m_st{r}"], 32 * (USES[r] + 1))

            def load_y(g, ahead=True):
                for c in range(2):
                    if ahead:
                        sp.wait_ge(S[f"o_y{c}"], g * 16)
                    at = g * (4 * CH) + c * (2 * CH)
                    sp.dma_start(y_all[:, bass.ds(at, 2 * CH)].rearrange("p (t s c) -> p t (s c)", s=2, c=C),
                                 y_tok[bass.ds(at, 2 * CH), :].rearrange("(t p s) c -> p t (s c)", p=P, s=2))\
                        .then_inc(S[f"o_y{c}"], 16)

            def store(g):
                for c in range(2):
                    sp.wait_ge(S["o_out"], g * 2 + (3 + c))
                    sp.dma_start(out[bass.ds(g * (2 * CH) + c * CH, CH), :].rearrange("(t p) c -> p t c", p=P),
                                 res[:, bass.ds(g * (2 * CH) + c * CH, CH)].rearrange("p (t c) -> p t c", c=C))\
                        .then_inc(S["o_st"], 16)
            load_y(0, ahead=False)
            with sp.Fori(1, 2 * BATCH) as g:
                load_y(g)
                store(g - 1)
            store(2 * BATCH - 1)
            sp.wait_ge(S["o_st"], 16 * ALL)

        @block.gpsimd
        def _(pool):
            pool.memset(neg_half[:, :, :], -0.5).then_inc(S["set_const"], 1)
            for buf in (padA, padB, padC):
                edges = buf[:, :].rearrange("p (b n) -> p b n", b=BATCH)
                pool.memset(edges[:, :, 0:PADDED:PADDED - 1], 0.0).then_inc(S["set_pads"], 1)
            pool.memset(q_all[:, 0:ZT * ROW], 0.0).then_inc(S["set_zero"], 1)
            pool.wait_ge(S["set_zero"], 1)
            pool.memset(q_all[:, 0:ZT * ROW].bitcast(I32)[:, C:ZT * ROW:ROW], NOWHERE).then_inc(S["set_zero"], 1)
            prime(pool, "gpsimd")
            pool.wait_ge(S["set_zero"], 2)
            for r in range(MOE_E):
                for u in range(2):
                    pool.indirect_dma_start(out=y_tok[:, :],
                                            out_offset=bass.IndirectOffsetOnAxis(q_all[:, C:C + 1].bitcast(I32), 0),
                                            in_=q_all[:, 0:C], in_offset=None, bounds_check=2 * N - 1,
                                            oob_is_err=False).then_inc(S[f"m_st{r}"], 16)
            pool.wait_ge(S["set_const"], 1)

            def root(q, ph, h=0):
                pool.wait_ge(S[ph + "_mv"], q.nth(q.n // 2 * 3, 3 * h + 3))
                pool.tensor_tensor(rstd[:, 2 * h:2 * h + 2, :], var_e[:, 2 * h:2 * h + 2, :], neg_half[:, :, :], ALU.pow)\
                    .then_inc(S[ph + "_rstd"], 1)

            def carry():
                pool.sem_inc(S["carried"], 1)

            def a(q):
                for h in range(2):
                    root(q, "a", h)
            each_batch(pool, a)

            pool.wait_ge(S["ld_rows"], 16)
            pool.wait_ge(S["r_done"], 1)
            pool.wait_ge(S["a_st_dram"], 16 * ALL)
            pool.wait_ge(S["zero_x"], 16 * (SLOT_TILES // ZT))

            def scatter(j, first=False):
                if not first:
                    pool.wait_ge(S["s_scat"], (j - 1) * (16 * 2 * TPC))
                for s in range(2):
                    pool.dma_start(stage[:, s, :, 0:C],
                                   xn_dram[bass.ds((j - 1) * CH, CH), :].rearrange("(t p) c -> p t c", p=P))\
                        .then_inc(S["s_stage"], 16)
                pool.tensor_copy(idx[:, :, :], slot_i[:, bass.ds((j - 1) * TPC, TPC), :]).then_inc(S["s_idx"], 1)
                pool.tensor_copy(stage[:, :, :, C].bitcast(I32),
                                 res_rows[:, bass.ds((j - 1) * TPC, TPC), :].rearrange("p t s -> p s t"))\
                    .then_inc(S["s_idx"], 1)
                pool.tensor_copy(stage[:, :, :, C + 1],
                                 prob[:, bass.ds((j - 1) * TPC, TPC), :].rearrange("p t s -> p s t"))\
                    .then_inc(S["s_idx"], 1)
                pool.wait_ge(S["s_stage"], j * 32)
                pool.wait_ge(S["s_idx"], j * 3)
                carry()
                for i in range(TPC):
                    for s in range(2):
                        pool.indirect_dma_start(out=slot_x[:, :], out_offset=bass.IndirectOffsetOnAxis(idx[:, i, s:s + 1], 0),
                                                in_=stage[:, s, i, :], in_offset=None).then_inc(S["s_scat"], 16)

            scatter(1, first=True)

            def b(q):
                for h in range(2):
                    root(q, "b", h)
                    scatter(q.g * 2 + (2 + h))
            each_batch(pool, b)
            with pool.Fori(2 * BATCH + 2, NT // TPC + 1) as j:
                scatter(j)

            def store_slots(t, r):
                pool.wait_ge(S["m_ys"], t.done(r))
                carry()
                for u in range(2):
                    pool.indirect_dma_start(out=y_tok[:, :],
                                            out_offset=bass.IndirectOffsetOnAxis(xs[:, r, u, C:C + 1].bitcast(I32), 0),
                                            in_=ys[:, r, u, :], in_offset=None, bounds_check=2 * N - 1,
                                            oob_is_err=False).then_inc(S[f"m_st{r}"], 16)

            def d(q):
                t = Slots(pool, q, False)
                for step in D_ORDER:
                    if step[0] == "Y":
                        store_slots(t, int(step[1:]))
            each_pair(pool, d)

            def e(q):
                t = Slots(pool, q, True)
                for step in E_ORDER:
                    if step == "mv":
                        root(q, "e")
                    if step[0] == "Y":
                        store_slots(t, int(step[1:]))
            each_pair(pool, e)

            def f(q):
                for c in range(2):
                    pool.wait_ge(S["o_m"], q.done(c))
                    pool.tensor_tensor(q.flat(res, c), q.flat(res, c), q.flat(x_again, c), ALU.add).then_inc(S["o_out"], 1)
            pool.wait_ge(S["ld_x2"], 16 * 2 * BATCH)
            each_pair(pool, f)

        def settle(act, func):
            nc.scalar.activation(mark[:, 0:1], minus_one[:, 0:1], func)

        @block.scalar
        def _(act):
            act.dma_start(kon[:, :], consts[:, 0:NSTAY]).then_inc(S["ld_k"], 16)
            act.dma_start(w("wg"), weights[:, WCOL["wg"][0]:NWCOL]).then_inc(S["ld_wg"], 16)
            act.dma_start(kon_r, consts[:, NSTAY:NKCOL]).then_inc(S["ld_k"], 16)
            act.dma_start(vec[:, :], vecs).then_inc(S["ld_vec"], 16)
            act.dma_start(kb1[:, :], k_bias.broadcast_to([P, C])).then_inc(S["ld_kb"], 16)
            act.dma_start(res_rows[:, :, :].rearrange("p t s -> p (t s)"), result_rows).then_inc(S["ld_rows"], 16)
            act.dma_start(wts[:, 0:WCOL["wg"][0]], weights[:, 0:WCOL["wg"][0]]).then_inc(S["ld_w"], 16)
            prime(act, "scalar")
            act.wait_ge(S["set_pads"], 3)

            def a(q):
                for c in range(4):
                    act.wait_ge(S["a_tr"], q.done(c))
                    nc.scalar.activation(q.chunk(padA, c), tq[c][:, :], ACT.Copy).then_inc(S["a_xnt"], 1)
                for c in range(4):
                    act.wait_ge(S["a_lg"], q.done(c))
                    act.wait_ge(S["a_lt"], q.before())
                    nc.scalar.activation(lg_c[c][0:E, :], uq[c][0:E, :], ACT.Copy).then_inc(S["a_lgc"], 1)
            each_batch(act, a)

            act.wait_ge(S["r_exp"], 1)
            nc.scalar.activation(pt_e[:, 1, :], pt_e[:, 0, :], ACT.Exp).then_inc(S["r_exp"], 1)

            act.wait_ge(S["ld_vec"], 16)
            act.wait_ge(S["set_cw"], 1)
            act.wait_ge(S["set_v1"], 7)
            act.wait_ge(S["a_l"], ALL)
            act.wait_ge(S["a_st_dram"], 16 * ALL)
            act.wait_ge(S["a_xnt"], ALL)

            def b(q):
                for c in range(4):
                    act.wait_ge(S["b_tr"], q.before())
                    act.wait_ge(S["b_x1st"], q.stored())
                    nc.scalar.activation(bufs[c][:, :], q.chunk(padA, c), ACT.Identity, bias=v("cpe1_b"),
                                         scale=cw1[:, 0:1]).then_inc(S["b_ctr"], 1)
                for c in range(4):
                    act.wait_ge(S["b_back"], q.done(c))
                    act.wait_ge(S["b_gate"], q.before())
                    nc.scalar.activation(aff[c][:, :], uq[c][:, :], ACT.Identity, bias=v("norm1_b"),
                                         scale=v("norm1_g")).then_inc(S["b_aff"], 1)
                for c in range(4):
                    act.wait_ge(S["b_in"], q.done(c))
                    nc.scalar.activation(q.chunk(padB, c), tq[c][:, :], ACT.Identity, bias=v("in_b")).then_inc(S["b_xi"], 1)
                    act.wait_ge(S["b_gate"], q.done(c))
                    nc.scalar.activation(q.flat(act_all, c), uq[c][:, :], ACT.Silu, bias=v("actp_b")).then_inc(S["b_act"], 1)
            settle(act, ACT.Silu)
            each_batch(act, b)

            act.wait_ge(S["b_xi"], ALL)
            act.wait_ge(S["zero_x"], 16 * (SLOT_TILES // ZT))
            for r in range(MOE_E):
                act.wait_ge(S[f"m_st{r}"], 32)
            act.wait_ge(S["b_x1st"], 16 * ALL)

            def cc(q):
                for c in range(4):
                    act.wait_ge(S["c_kv"], q.before())
                    nc.scalar.activation(norm_t[c][:, :], q.chunk(padB, c), ACT.Identity, bias=v("dwc_b"),
                                         scale=v("dwc_w", 1)).then_inc(S["c_ctr"], 1)
                for c in range(4):
                    act.wait_ge(S["c_cv"], q.done(c))
                    act.wait_ge(S["c_vst"], q.stored())
                    act.wait_ge(S["c_vt"], q.before())
                    nc.scalar.activation(bufs[c][:, :], norm_t[c][:, :], ACT.Silu).then_inc(S["c_v"], 1)
                for c in range(4):
                    act.wait_ge(S["c_q"], q.done(c))
                    act.wait_ge(S["c_qt"], q.before())
                    nc.scalar.activation(q.flat(q_all, c), tq[c][:, :], ACT.Relu, bias=v("q_b"))
                    nc.scalar.activation(e_q[c][:, :], tq[c][:, :], ACT.Exp, bias=v("q_b")).then_inc(S["c_rq"], 1)
                    act.wait_ge(S["c_kb"], q.done(c))
                    nc.scalar.activation(aff[c][:, :], kx[c][:, :], ACT.Exp, bias=minus_one[:, 0:1]).then_inc(S["c_ek"], 1)
                for c in range(4):
                    act.wait_ge(S["c_vt"], q.done(c))
                    act.wait_ge(S["c_kv"], q.before())
                    nc.scalar.activation(v_tok[c][:, :, 0:C], tq[c][:, :].rearrange("p (k n) -> p k n", k=TPC),
                                         ACT.Copy).then_inc(S["c_vtok"], 1)
            each_batch(act, cc)

            def rows_out(t, r):
                act.wait_ge(S["m_xt"], t.done(r))
                nc.scalar.activation(xs_t[:, r % 2, :, :], mxy[:, 0:2 * P].rearrange("p (u n) -> p u n", u=2),
                                     ACT.Copy).then_inc(S["m_xtc"], 1)

            def gated_out(t, r):
                act.wait_ge(S["m_gt"], t.done(r))
                nc.scalar.activation(gg_t[:, :, :, :], mg[:, :].rearrange("p (u a n) -> p u a n", u=2, a=2),
                                     ACT.Copy).then_inc(S["m_gtc"], 1)

            act.wait_ge(S["c_vst"], 16 * ALL)
            act.wait_ge(S["c_kv"], ALL)

            def d(q):
                t = Slots(act, q, False)
                for step in D_ORDER:
                    if step == "ctr":
                        for c in range(2):
                            act.wait_ge(S["d_ac"], q.before())
                            nc.scalar.activation(norm_t[c][:, :], q.chunk(padC, c), ACT.Identity, bias=v("lepe_b"),
                                                 scale=v("lepe_w", 1)).then_inc(S["d_ctr"], 1)
                    elif step[0] == "X":
                        rows_out(t, int(step[1:]))
                    elif step[0] == "H":
                        r, u = map(int, step[1:].split("."))
                        act.wait_ge(S["m_h"], t.done_u(r, u))
                        act.wait_ge(S["m_g"], t.done_u(r - 1, u))
                        nc.scalar.activation(s1[:, u, :], mh[u][:, 0:EH], ACT.Silu).then_inc(S["m_s1"], 1)
                    elif step[0] == "G":
                        gated_out(t, int(step[1:]))
            settle(act, ACT.Silu)
            each_pair(act, d)

            act.wait_ge(S["d_x2"], ALL)

            def e(q):
                t = Slots(act, q, True)
                for step in E_ORDER:
                    if step == "ctr":
                        for c in range(2):
                            act.wait_ge(S["e_sum"], q.before())
                            nc.scalar.activation(bufs[c][:, :], q.chunk(padA, c), ACT.Identity, bias=v("cpe2_b"),
                                                 scale=cw1[:, 1:2]).then_inc(S["e_ctr"], 1)
                    elif step[:2] == "bk":
                        c = int(step[2])
                        act.wait_ge(S["e_back"], q.done(c))
                        nc.scalar.activation(aff[c][:, :], pu[c][:, :], ACT.Identity, bias=v("norm2_b"),
                                             scale=v("norm2_g")).then_inc(S["e_aff"], 1)
                    elif step[:3] == "fc1":
                        i, c = map(int, step[4:].split("."))
                        act.wait_ge(S["e_f1"], q.nth(8, 2 * i + c + 1))
                        nc.scalar.activation(hid[:, c, i, :], (pt, pu)[i % 2][c][:, :], ACT.Gelu,
                                             bias=v("fc1_b", i)).then_inc(S["e_h"], 1)
                    elif step[:2] == "st":
                        c = int(step[2])
                        act.wait_ge(S["e_sT"], q.done(c))
                        nc.scalar.activation(q.flat(q_all, c), pu[c][:, :], ACT.Copy).then_inc(S["e_so"], 1)
                    elif step[0] == "X":
                        rows_out(t, int(step[1:]))
                    elif step[0] == "H":
                        r, u = map(int, step[1:].split("."))
                        act.wait_ge(S["m_h"], t.done_u(r, u))
                        act.wait_ge(S["m_g"], t.done_u(r - 1, u))
                        nc.scalar.activation(s1[:, u, :], mh[u][:, 0:EH], ACT.Tanh, scale=0.5).then_inc(S["m_s1"], 1)
                    elif step[0] == "G":
                        gated_out(t, int(step[1:]))
            settle(act, ACT.Gelu)
            each_pair(act, e)

            def f(q):
                for c in range(2):
                    act.wait_ge(S["o_f"], q.done(c))
                    nc.scalar.activation(q.flat(res, c), q.flat(res, c), ACT.Silu).then_inc(S["o_sg"], 1)
            settle(act, ACT.Silu)
            each_pair(act, f)

        @block.vector
        def _(dve):
            dve.memset(ones_b[:, :], 1.0).then_inc(S["set_v1"], 1)
            dve.memset(minus_one[:, :], -1.0).then_inc(S["set_v1"], 1)
            for c in range(4):
                dve.memset(v_tok[c][:, :, C:C + 1], 1.0).then_inc(S["set_v1"], 1)
            dve.memset(kv_sum[:, :, :], 0.0).then_inc(S["set_v1"], 1)
            prime(dve, "vector")

            def stats_of(q, ph, src, c):
                for i, t in enumerate(src):
                    ins = dve.bn_stats(stats[:, c, i, :], t)
                ins.then_inc(S[ph + "_st"], 1)

            def moments(q, ph, h=0):
                two = slice(2 * h, 2 * h + 2)
                n = q.n // 2 * 3
                m_even, m_odd, v_even, v_odd = (stats[:, two, :, i] for i in (1, 4, 2, 5))
                dve.wait_ge(S[ph + "_st"], q.nth(q.n, 2 * h + 2))
                dve.tensor_tensor(msum[:, two, :], m_even, m_odd, ALU.add)
                dve.tensor_tensor(mdif[:, two, :], m_even, m_odd, ALU.subtract)
                dve.tensor_tensor(vsum[:, two, :], v_even, v_odd, ALU.add).then_inc(S[ph + "_mv"], 1)
                dve.wait_ge(S[ph + "_mv"], q.nth(n, 3 * h + 1))
                dve.tensor_scalar(mean[:, two, :], msum[:, two, :], 0.5, None, ALU.mult)
                dve.tensor_tensor(mdif2[:, two, :], mdif[:, two, :], mdif[:, two, :], ALU.mult)
                dve.tensor_scalar(vsum2[:, two, :], vsum[:, two, :], 1.0 / C, EPS, ALU.mult, ALU.add)\
                    .then_inc(S[ph + "_mv"], 1)
                dve.wait_ge(S[ph + "_mv"], q.nth(n, 3 * h + 2))
                dve.scalar_tensor_tensor(var_e[:, two, :], mdif2[:, two, :], 0.25, vsum2[:, two, :], ALU.mult, ALU.add)\
                    .then_inc(S[ph + "_mv"], 1)

            def normalize(q, ph, src, dst, c, done):
                dve.wait_ge(S[ph + "_rstd"], q.nth(q.n // 2, c // 2 + 1))
                for i, t in enumerate(src):
                    ins = dve.tensor_scalar(dst[c][:, P * i:P * (i + 1)], t, mean[:, c, i:i + 1],
                                            rstd[:, c, i:i + 1], ALU.subtract, ALU.mult)
                ins.then_inc(S[done], 1)

            def a(q):
                src = [[x_tok[:, bass.ds(q.flat0 + (c * CH + P * i), P)] for i in range(TPC)] for c in range(4)]
                for c in range(4):
                    stats_of(q, "a", src[c], c)
                    if c % 2:
                        moments(q, "a", c // 2)
                dve.wait_ge(S["a_tr"], q.before())
                dve.wait_ge(S["a_st_dram"], q.stored())
                for c in range(4):
                    normalize(q, "a", src[c], bufs, c, "a_xn")
                for c in range(4):
                    dve.wait_ge(S["a_lt"], q.done(c))
                    dve.tensor_copy(lg[:, bass.ds(q.g * (4 * TPC) + c * TPC, TPC), :],
                                    uq[c][:, 0:TPC * E].rearrange("p (t e) -> p t e", e=E)).then_inc(S["a_l"], 1)
            dve.wait_ge(S["ld_x"], 64)
            each_batch(dve, a)

            dve.wait_ge(S["ld_vec"], 16)
            dve.wait_ge(S["ld_kb"], 16)
            dve.wait_ge(S["ld_k"], 32)
            dve.wait_ge(S["a_l"], ALL)
            steps = [0]

            def step(ins):
                steps[0] += 1
                ins.then_inc(S["r_step"], 1)

            def settled():
                dve.wait_ge(S["r_step"], steps[0])

            def over_e(a):
                return a.unsqueeze(2).broadcast_to([P, NT, E])

            prefer = k("prefer").unsqueeze(1).broadcast_to([P, NT, E])
            for s in range(2):
                src = lg if s == 0 else eqm
                step(dve.tensor_reduce(best[:, s, :], src[:, :, :], AX.X, ALU.max))
                settled()
                step(dve.tensor_tensor(key[:, :, :], src[:, :, :], over_e(best[:, s, :]), ALU.is_equal))
                settled()
                step(dve.tensor_tensor(key[:, :, :], key[:, :, :], prefer, ALU.mult))
                settled()
                step(dve.tensor_reduce(best[:, 2 + s, :], key[:, :, :], AX.X, ALU.max))
                settled()
                step(dve.tensor_tensor(oh[:, s, :, :], key[:, :, :], over_e(best[:, 2 + s, :]), ALU.is_equal))
                settled()
                if s == 0:
                    step(dve.scalar_tensor_tensor(eqm[:, :, :], oh[:, 0, :, :], -3.0e38, lg[:, :, :], ALU.mult, ALU.add))
                    settled()
            dve.tensor_tensor(mask_b[:, :].rearrange("p (t e) -> p t e", e=E), oh[:, 0, :, :], oh[:, 1, :, :], ALU.add)
            dve.tensor_copy(before_b[:, :], k("before"))
            dve.tensor_copy(tile_b[:, :], k("tile_before"))
            dve.tensor_copy(same_b[:, :], k("same_expert")).then_inc(S["r_mask"], 1)
            dve.tensor_tensor(pt_e[:, 0, :], best[:, 1, :], best[:, 0, :], ALU.subtract).then_inc(S["r_exp"], 1)
            dve.wait_ge(S["r_totc"], 1)
            step(dve.tensor_copy(tot_c[:, :], pt[0][:, 0:2]))
            settled()
            for s in range(2):
                ins = dve.tensor_scalar(tot_b[:, s, :], ones_b[:, :], tot_c[:, s:s + 1], None, ALU.mult)
            ins.then_inc(S["r_totb"], 1)
            dve.wait_ge(S["r_exp"], 2)
            step(dve.tensor_scalar(pt_e[:, 2, :], pt_e[:, 1, :], 1.0, None, ALU.add))
            settled()
            step(dve.reciprocal(prob[:, :, 0], pt_e[:, 2, :]))
            settled()
            step(dve.tensor_tensor(prob[:, :, 1], prob[:, :, 0], pt_e[:, 1, :], ALU.mult))
            dve.wait_ge(S["r_rank"], 1)
            step(dve.tensor_scalar(cnt_i[:, 0, :], pt[1][:, 0:E], float(P - 1), None, ALU.add))
            settled()
            step(dve.tensor_scalar(cnt_i[:, 1, :], cnt_i[:, 0, :], 7, None, ALU.arith_shift_right))
            settled()
            step(dve.tensor_copy(cnt[:, 0, :], cnt_i[:, 1, :]))
            settled()
            step(dve.tensor_tensor(ebef[:, :, :], k("expert_before").rearrange("p (a b) -> p a b", b=E),
                                   cnt[:, 0, :].unsqueeze(1).broadcast_to([P, E, E]), ALU.mult))
            settled()
            step(dve.tensor_reduce(cnt[:, 1, :], ebef[:, :, :], AX.X, ALU.add))
            settled()
            step(dve.tensor_tensor(cnt[:, 2, :], cnt[:, 0, :], cnt[:, 1, :], ALU.add))
            step(dve.scalar_tensor_tensor(eqm[:, :, :], cnt[:, 1, :].unsqueeze(1).broadcast_to([P, NT, E]), float(P),
                                          pu[0][:, 0:NT * E].rearrange("p (t e) -> p t e", e=E), ALU.mult, ALU.add))
            settled()
            for s in range(2):
                step(dve.tensor_tensor(key[:, :, :], oh[:, s, :, :], eqm[:, :, :], ALU.mult))
                settled()
                step(dve.tensor_reduce(slot_f[:, s, :], key[:, :, :], AX.X, ALU.add))
                settled()
            dve.tensor_copy(slot_i[:, :, :], slot_f[:, :, :].rearrange("p s t -> p t s")).then_inc(S["r_done"], 1)
            step(dve.tensor_tensor(texp[:, :, :], k("slot_tile", 1).unsqueeze(2).broadcast_to([1, SLOT_TILES, E]),
                                   cnt[0:1, 2, :].unsqueeze(1).broadcast_to([1, SLOT_TILES, E]), ALU.is_ge))
            settled()
            step(dve.tensor_reduce(texp_f[:, :], texp[:, :, :], AX.X, ALU.add))
            settled()
            dve.tensor_scalar(texp_i[:, :], texp_f[:, :], float(E - 1), None, ALU.min).then_inc(S["r_done"], 1)
            step(dve.tensor_scalar(cw1[:, 0:1], v("cpe1_w", 1), 1.0, None, ALU.add))
            dve.tensor_scalar(cw1[:, 1:2], v("cpe2_w", 1), 1.0, None, ALU.add)
            dve.tensor_scalar(kb1[:, :], kb1[:, :], 1.0, None, ALU.add).then_inc(S["set_cw"], 1)
            settled()

            def taps(q, ph, buf, src, weight, last):
                for h in range(q.n // 2):
                    for c in (2 * h, 2 * h + 1):
                        dve.wait_ge(S[ph + "_ctr"], q.done(c))
                        dve.scalar_tensor_tensor(buf[c][:, :], q.chunk(src, c, -1), v(weight, 0), buf[c][:, :], ALU.mult,
                                                 ALU.add).then_inc(S[ph + "_left"], 1)
                    for c in (2 * h, 2 * h + 1):
                        dve.wait_ge(S[ph + "_left"], q.done(c))
                        dve.scalar_tensor_tensor(buf[c][:, :], q.chunk(src, c, 1), v(weight, 2), buf[c][:, :], ALU.mult,
                                                 ALU.add).then_inc(S[last], 1)

            def in_psum(c):
                return [bank[c][:, P * i:P * (i + 1)] for i in range(TPC)]

            dve.wait_ge(S["set_pads"], 3)

            def b(q):
                taps(q, "b", bufs, padA, "cpe1_w", "b_x1")
                for c in range(4):
                    dve.wait_ge(S["b_tr"], q.done(c))
                    stats_of(q, "b", in_psum(c), c)
                    if c % 2:
                        moments(q, "b", c // 2)
                dve.wait_ge(S["b_back"], q.before())
                for c in range(4):
                    normalize(q, "b", in_psum(c), norm_t, c, "b_nm")
            each_batch(dve, b)

            dve.wait_ge(S["set_cw"], 1)
            kb_tiles = kb1[:, :].unsqueeze(1).broadcast_to([P, TPC, C])

            def cc(q):
                taps(q, "c", norm_t, padB, "dwc_w", "c_cv")
                for c in range(4):
                    dve.wait_ge(S["c_k"], q.done(c))
                    dve.tensor_tensor(kx[c][:, :].rearrange("p (t n) -> p t n", n=C),
                                      uq[c][:, :].rearrange("p (t n) -> p t n", n=C), kb_tiles, ALU.add)\
                        .then_inc(S["c_kb"], 1)
                    dve.wait_ge(S["c_rq"], q.done(c))
                    dve.scalar_tensor_tensor(q.flat(q_all, c), e_q[c][:, :], 1.0, q.flat(q_all, c), ALU.min, ALU.add)\
                        .then_inc(S["c_qt"], 1)
                for c in range(4):
                    dve.wait_ge(S["c_ek"], q.done(c))
                    dve.wait_ge(S["c_kv"], q.before())
                    dve.scalar_tensor_tensor(k_tok[c][:, :], aff[c][:, :], 1.0, kx[c][:, :], ALU.min, ALU.max)\
                        .then_inc(S["c_kt"], 1)
                for c in range(4):
                    dve.wait_ge(S["c_kv"], q.done(c))
                    acc = kv_sum[:, bass.ds(q.b, 1), :].rearrange("p a n -> p (a n)")
                    dve.wait_ge(S["c_acc"], q.before() + c)
                    dve.tensor_tensor(acc, acc, uq[c][:, 0:C + 1], ALU.add).then_inc(S["c_acc"], 1)
            each_batch(dve, cc)

            dve.wait_ge(S["c_acc"], ALL)
            for b_ in range(BATCH):
                dve.tensor_scalar(kv_s[:, b_, :], kv_sum[:, b_, 0:C], 1.0 / SEQ, None, ALU.mult).then_inc(S["f_kvs"], 1)
                dve.tensor_scalar(mk[:, b_, C:C + HEADS], k("headmask"), kv_sum[:, b_, C:C + 1], 1.0 / SEQ, ALU.mult,
                                  ALU.mult).then_inc(S["f_mk"], 1)
            for b_ in range(BATCH):
                dve.wait_ge(S["f_kvr1"], b_ + 1)
                dve.tensor_tensor(kv_r[:, b_, :], pt[b_][:, 0:C], k("headblock"), ALU.mult).then_inc(S["f_kvr"], 1)
            for b_ in range(BATCH):
                dve.wait_ge(S["f_m"], b_ + 1)
                dve.tensor_copy(mk[:, b_, 0:C], pu[b_][:, 0:C]).then_inc(S["f_mk"], 1)

            def experts_out(t, r):
                dve.wait_ge(S["m_y"], t.done(r))
                dve.wait_ge(S[f"m_st{r}"], t.uses(r) * 32)
                for u in range(2):
                    ins = dve.tensor_scalar(ys[:, r, u, :], mxy[:, (2 + u) * P:(3 + u) * P], xs[:, r, u, C + 1:C + 2], None,
                                            ALU.mult)
                ins.then_inc(S["m_ys"], 1)

            def d(q):
                t = Slots(dve, q, False)
                for step in D_ORDER:
                    if step == "ctr":
                        taps(q, "d", norm_t, padC, "lepe_w", "d_lp")
                    elif step[:2] == "nd":
                        c = int(step[2])
                        halves = [(pt, pu)[a_][c][:, 0:2 * WD].rearrange("p (k n) -> p k n", k=2) for a_ in range(2)]
                        dve.wait_ge(S["d_nd"], q.done(c))
                        for a_, nd in enumerate(halves):
                            ins = dve.tensor_scalar(den[:, c, 2 * a_:2 * a_ + 2, :], nd[:, :, C:WD], Z_EPS, None, ALU.add)
                        ins.then_inc(S["d_de"], 1)
                        dve.wait_ge(S["d_de"], q.done(c))
                        dve.reciprocal(rden[:, c, :, :], den[:, c, :, :]).then_inc(S["d_rd"], 1)
                        dve.wait_ge(S["d_rd"], q.done(c))
                        for a_, nd in enumerate(halves):
                            ins = dve.tensor_tensor(
                                att[:, c, 2 * a_ * P:(2 * a_ + 2) * P].rearrange("p (k h d) -> p k h d", k=2, h=HEADS),
                                nd[:, :, 0:C].rearrange("p k (h d) -> p k h d", h=HEADS),
                                rden[:, c, 2 * a_:2 * a_ + 2, :].unsqueeze(3).broadcast_to([P, 2, HEADS, HD]), ALU.mult)
                        ins.then_inc(S["d_at"], 1)
                    elif step[:2] == "at":
                        c = int(step[2])
                        dve.wait_ge(S["d_atT"], q.done(c))
                        dve.wait_ge(S["d_lp"], q.done(c))
                        dve.tensor_tensor(norm_t[c][:, :], norm_t[c][:, :], pt[c][:, :], ALU.add).then_inc(S["d_sum"], 1)
                        dve.wait_ge(S["d_sum"], q.done(c))
                        dve.tensor_tensor(aff[c][:, :], norm_t[c][:, :], q.flat(act_all, c), ALU.mult).then_inc(S["d_ac"], 1)
                    elif step[:3] == "out":
                        c = int(step[3])
                        dve.wait_ge(S["d_out"], q.done(c))
                        dve.scalar_tensor_tensor(q.chunk(padA, c), pu[c][:, :], v("out_b"), q.flat(x1_all, c), ALU.add,
                                                 ALU.add).then_inc(S["d_x2"], 1)
                    elif step[0] == "H":
                        r, u = map(int, step[1:].split("."))
                        dve.wait_ge(S["m_s1"], t.done_u(r, u))
                        dve.wait_ge(S["m_gt"], t.done(r - 1))
                        dve.tensor_tensor(gg[:, u, :], s1[:, u, :], mh[u][:, EH:2 * EH], ALU.mult).then_inc(S["m_g"], 1)
                    elif step[0] == "Y":
                        experts_out(t, int(step[1:]))
            dve.wait_ge(S["b_x1st"], 16 * ALL)
            dve.wait_ge(S["c_vst"], 16 * ALL)
            each_pair(dve, d)
            dve.wait_ge(S["d_x2"], ALL)

            def e(q):
                t = Slots(dve, q, True)
                for step in E_ORDER:
                    if step == "ctr":
                        taps(q, "e", bufs, padA, "cpe2_w", "e_x3")
                    elif step[:2] == "tr":
                        c = int(step[2])
                        dve.wait_ge(S["e_tr"], q.done(c))
                        stats_of(q, "e", in_psum(c), c)
                    elif step == "mv":
                        moments(q, "e")
                    elif step[:2] == "nm":
                        c = int(step[2])
                        dve.wait_ge(S["e_sT"], q.before())
                        normalize(q, "e", in_psum(c), norm_t, c, "e_nm")
                    elif step[:3] == "fc2":
                        c = int(step[4])
                        dve.wait_ge(S["e_s"], q.done(c))
                        dve.scalar_tensor_tensor(norm_t[c][:, :], pt[c][:, :], v("fc2_b"), bufs[c][:, :], ALU.add,
                                                 ALU.add).then_inc(S["e_sum"], 1)
                    elif step[0] == "H":
                        r, u = map(int, step[1:].split("."))
                        dve.wait_ge(S["m_s1"], t.done_u(r, u))
                        dve.scalar_tensor_tensor(s2[:, u, :], s1[:, u, :], 1.0, mh[u][:, 0:EH], ALU.add, ALU.mult)\
                            .then_inc(S["m_a"], 1)
                        dve.wait_ge(S["m_a"], q.nth(2 * MOE_E, 2 * r + u + 1))
                        dve.wait_ge(S["m_gt"], t.done(r - 1))
                        dve.scalar_tensor_tensor(gg[:, u, :], s2[:, u, :], 0.5, mh[u][:, EH:2 * EH], ALU.mult, ALU.mult)\
                            .then_inc(S["m_g"], 1)
                    elif step[0] == "Y":
                        experts_out(t, int(step[1:]))
            each_pair(dve, e)

            def f(q):
                for c in range(2):
                    rows = y_all[:, bass.ds(q.flat0 * 2 + c * (2 * CH), 2 * CH)].rearrange("p (k s n) -> p k s n", s=2, n=C)
                    dve.wait_ge(S[f"o_y{c}"], q.nth(1, 1) * 16)
                    dve.tensor_tensor(q.flat(res, c).rearrange("p (k n) -> p k n", k=TPC), rows[:, :, 0, :],
                                      rows[:, :, 1, :], ALU.add).then_inc(S["o_f"], 1)
                for c in range(2):
                    dve.wait_ge(S["o_sg"], q.done(c))
                    dve.tensor_tensor(q.flat(res, c), q.flat(res, c), q.flat(q_all, c), ALU.mult).then_inc(S["o_m"], 1)
            dve.wait_ge(S["e_so"], ALL)
            each_pair(dve, f)

        @block.tensor
        def _(pe):
            ident = k("ident")
            prime(pe, "tensor")
            pe.wait_ge(S["ld_k"], 32)
            pe.wait_ge(S["ld_wg"], 16)
            pe.wait_ge(S["set_v1"], 7)

            def turn(dst, src, c, done):
                for i, t in enumerate(tiles(src, c)):
                    mm = nc.tensor.transpose(dst[c][:, P * i:P * (i + 1)], t, ident)
                mm.then_inc(S[done], 1)

            def a(q):
                for c in range(4):
                    pe.wait_ge(S["a_xn"], q.done(c))
                    pe.wait_ge(S["a_xnt"], q.before())
                    turn(tq, bufs, c, "a_tr")
                for c in range(4):
                    pe.wait_ge(S["a_xnt"], q.done(c))
                    pe.wait_ge(S["a_l"], q.before())
                    nc.tensor.matmul(uq[c][0:E, :], w("wg"), q.chunk(padA, c), start=True, stop=True).then_inc(S["a_lg"], 1)
                for c in range(4):
                    pe.wait_ge(S["set_v1"], 1 + c)
                    pe.wait_ge(S["a_lgc"], q.done(c))
                    for i in range(TPC):
                        mm = nc.tensor.transpose(uq[c][:, i * E:(i + 1) * E], lg_c[c][0:E, P * i:P * (i + 1)],
                                                 ident[0:E, 0:E])
                    mm.then_inc(S["a_lt"], 1)
            each_batch(pe, a)

            pe.wait_ge(S["r_mask"], 1)
            for s in range(2):
                mm = nc.tensor.matmul(pt[0][:, s:s + 1], mask_b[:, s * P:(s + 1) * P], ones_b[:, 0:1], start=True, stop=True)
            mm.then_inc(S["r_totc"], 1)
            pe.wait_ge(S["r_totb"], 1)
            for s in range(2):
                nc.tensor.matmul(pu[0][:, 0:NT * E], tot_b[:, s, :], tile_b[:, s * NT * E:(s + 1) * NT * E],
                                 start=(s == 0), stop=False)
            nc.tensor.matmul(pu[0][:, 0:NT * E], before_b[:, :], mask_b[:, :], start=False, stop=True)
            for s in range(2):
                mm = nc.tensor.matmul(pt[1][:, 0:E], tot_b[:, s, :], same_b[:, s * E:(s + 1) * E],
                                      start=(s == 0), stop=(s == 1))
            mm.then_inc(S["r_rank"], 1)

            def b(q):
                for c in range(4):
                    pe.wait_ge(S["b_x1"], q.done(c))
                    pe.wait_ge(S["b_xi"], q.before())
                    turn(tq, bufs, c, "b_tr")
                for c in range(4):
                    pe.wait_ge(S["b_nm"], q.done(c))
                    pe.wait_ge(S["b_act"], q.before())
                    turn(uq, norm_t, c, "b_back")
                for c in range(4):
                    pe.wait_ge(S["b_aff"], q.done(c))
                    nc.tensor.matmul(tq[c][:, :], w("in_w"), aff[c][:, :], start=True, stop=True).then_inc(S["b_in"], 1)
                    nc.tensor.matmul(uq[c][:, :], w("actp_w"), aff[c][:, :], start=True, stop=True).then_inc(S["b_gate"], 1)
            pe.wait_ge(S["ld_w"], 16)
            pe.wait_ge(S["r_done"], 2)
            each_batch(pe, b)

            pe.wait_ge(S["b_act"], ALL)

            def cc(q):
                for c in range(4):
                    pe.wait_ge(S["c_v"], q.done(c))
                    pe.wait_ge(S["c_vtok"], q.before())
                    nc.tensor.matmul(tq[c][:, :], w("q_w"), bufs[c][:, :], start=True, stop=True).then_inc(S["c_q"], 1)
                    pe.wait_ge(S["c_acc"], q.before())
                    for i, t in enumerate(tiles(bufs, c)):
                        mm = nc.tensor.matmul(uq[c][:, P * i:P * (i + 1)], t, w("k_w"), start=True, stop=True)
                    mm.then_inc(S["c_k"], 1)
                for c in range(4):
                    pe.wait_ge(S["c_rq"], q.done(c))
                    turn(tq, bufs, c, "c_vt")
                for c in range(4):
                    pe.wait_ge(S["c_kt"], q.done(c))
                    pe.wait_ge(S["c_vtok"], q.done(c))
                    for i, t in enumerate(tiles(k_tok, c)):
                        mm = nc.tensor.matmul(uq[c][:, 0:C + 1], t, v_tok[c][:, i, :], start=(i == 0), stop=(i == TPC - 1))
                    mm.then_inc(S["c_kv"], 1)
            each_batch(pe, cc)

            for b_ in range(BATCH):
                pe.wait_ge(S["f_kvs"], b_ + 1)
                nc.tensor.matmul(pt[b_][:, 0:C], k("rope"), kv_s[:, b_, :], start=True, stop=True).then_inc(S["f_kvr1"], 1)
            for b_ in range(BATCH):
                pe.wait_ge(S["f_kvr"], b_ + 1)
                nc.tensor.matmul(pu[b_][:, 0:C], k("rope_t"), kv_r[:, b_, :], start=True, stop=True).then_inc(S["f_m"], 1)

            experts = {}

            def X(t, r):
                for u in range(2):
                    experts[r, u] = pe.value_load(texp_i[0:1, bass.ds((t.p0 + r) * 2 + u, 1)], min_val=0, max_val=E - 1)
                pe.wait_ge(S[f"m_ld{r}"], t.uses(r) * 16)
                pe.wait_ge(S["m_ys"], t.done(r - 2 if r else -1))
                for u in range(2):
                    mm = nc.tensor.transpose(mxy[:, u * P:(u + 1) * P], xs[:, r, u, 0:C], ident)
                mm.then_inc(S["m_xt"], 1)

            def H(t, r, u):
                pe.wait_ge(S["m_xtc"], t.done(r))
                nc.tensor.matmul(mh[u][:, :], xs_t[:, r % 2, u, :], w12s[:, bass.ds(experts[r, u] * (2 * EH), 2 * EH)],
                                 start=True, stop=True).then_inc(S["m_h"], 1)

            def G(t, r):
                pe.wait_ge(S["m_g"], t.done_u(r, 1))
                for u in range(2):
                    for a_ in range(2):
                        mm = nc.tensor.transpose(mg[:, (2 * u + a_) * P:(2 * u + a_ + 1) * P],
                                                 gg[:, u, a_ * P:(a_ + 1) * P], ident)
                mm.then_inc(S["m_gt"], 1)

            def Y(t, r):
                pe.wait_ge(S["m_gtc"], t.done(r))
                for u in range(2):
                    for a_ in range(2):
                        mm = nc.tensor.matmul(mxy[:, (2 + u) * P:(3 + u) * P], gg_t[:, u, a_, :],
                                              w3s[:, bass.ds(experts[r, u] * (2 * C) + a_ * C, C)],
                                              start=(a_ == 0), stop=(a_ == 1))
                mm.then_inc(S["m_y"], 1)

            def expert_step(t, step):
                r = int(step[1])
                if step[0] == "X":
                    X(t, r)
                elif step[0] == "H":
                    H(t, r, int(step[3]))
                elif step[0] == "G":
                    G(t, r)
                else:
                    Y(t, r)

            pe.wait_ge(S["f_mk"], 2 * BATCH)
            pe.wait_ge(S["ld_w12"], 16)
            pe.wait_ge(S["ld_w3"], 16)

            def d(q):
                t = Slots(pe, q, False)
                for step in D_ORDER:
                    if step[:2] == "nd":
                        c = int(step[2])
                        pe.wait_ge(S[f"d_q{c}"], q.nth(1, 1) * 16)
                        pe.wait_ge(S["d_x2"], q.before())
                        for i, tile in enumerate(tiles(e_q, c)):
                            mm = nc.tensor.matmul((pt, pu)[i // 2][c][:, (i % 2) * WD:(i % 2 + 1) * WD], tile,
                                                  mk[:, bass.ds(q.b, 1), :].rearrange("p a n -> p (a n)"),
                                                  start=True, stop=True)
                        mm.then_inc(S["d_nd"], 1)
                    elif step[:2] == "at":
                        c = int(step[2])
                        pe.wait_ge(S["d_at"], q.done(c))
                        turn(pt, [att[:, 0, :], att[:, 1, :]], c, "d_atT")
                    elif step[:3] == "out":
                        c = int(step[3])
                        pe.wait_ge(S["d_ac"], q.done(c))
                        nc.tensor.matmul(pu[c][:, :], w("out_w"), aff[c][:, :], start=True, stop=True).then_inc(S["d_out"], 1)
                    elif step != "ctr":
                        expert_step(t, step)
            each_pair(pe, d)

            pe.wait_ge(S["d_x2"], ALL)

            def e(q):
                t = Slots(pe, q, True)
                for step in E_ORDER:
                    c = int(step[-1]) if step[-1] in "01" else 0
                    if step[:2] == "tr":
                        pe.wait_ge(S["e_x3"], q.done(c))
                        pe.wait_ge(S["e_sum"], q.before())
                        turn(pt, bufs, c, "e_tr")
                    elif step[:2] == "bk":
                        pe.wait_ge(S["e_nm"], q.done(c))
                        pe.wait_ge(S["e_so"], q.before())
                        turn(pu, norm_t, c, "e_back")
                    elif step[:3] == "fc1":
                        i = int(step[4])
                        if i < 2:
                            pe.wait_ge(S["e_aff"], q.done(c))
                        else:
                            pe.wait_ge(S["e_h"], q.nth(8, 2 * (i - 2) + c + 1))
                        nc.tensor.matmul((pt, pu)[i % 2][c][:, :], w("fc1_w", C * i, C * (i + 1)), aff[c][:, :],
                                         start=True, stop=True).then_inc(S["e_f1"], 1)
                    elif step[:3] == "fc2":
                        pe.wait_ge(S["e_h"], q.nth(8, 6 + c + 1))
                        for m in range(4):
                            mm = nc.tensor.matmul(pt[c][:, :], w("fc2_w", C * m, C * (m + 1)), hid[:, c, m, :],
                                                  start=(m == 0), stop=(m == 3))
                        mm.then_inc(S["e_s"], 1)
                    elif step[:2] == "st":
                        pe.wait_ge(S["e_sum"], q.done(c))
                        turn(pu, norm_t, c, "e_sT")
                    elif step[0] in "XHGY":
                        expert_step(t, step)
            each_pair(pe, e)


def kernel(**inputs):
    import concourse.bacc as bacc
    from concourse.bass_utils import run_bass_kernel_spmd

    f = {n: np.asarray(a) for n, a in inputs.items()}
    A = {n[len("L0_attn_"):]: a for n, a in f.items() if n.startswith("L0_attn_")}
    vecs = np.zeros((P, NVEC), np.float32)
    for name, (at, width) in VEC.items():
        src = A["qk_b"][:C] if name == "q_b" else A[name]
        vecs[:, at:at + width] = src.reshape(width, P).T if name == "fc1_b" else src.reshape(P, width)
    k_bias = A["qk_b"][None, C:]
    result_rows = (2 * (np.arange(P)[:, None, None] + P * np.arange(NT)[None, :, None]) + np.arange(2)).astype(np.int32)
    weights = np.concatenate([A["in_w"], A["actp_w"], A["qk_w"], A["out_w"], A["fc1_w"],
                              A["fc2_w"].reshape(4, P, C).transpose(1, 0, 2).reshape(P, 4 * C), f["L0_ffn_Wg"].T], axis=1)
    w12 = np.concatenate([f["L0_ffn_W1"].transpose(2, 0, 1), f["L0_ffn_W2"].transpose(2, 0, 1)], axis=2).reshape(P, -1)
    w3 = f["L0_ffn_W3"].transpose(0, 2, 1).reshape(E, 2, P, C).transpose(2, 0, 1, 3).reshape(P, -1)
    arrays = {"x": A["x"].reshape(N, C), "vecs": vecs, "k_bias": k_bias, "weights": weights, "w12": w12, "w3": w3,
              "consts": shape_constants(), "result_rows": result_rows.reshape(P, 2 * NT)}
    arrays = {n: np.ascontiguousarray(a) for n, a in arrays.items()}

    nc = bacc.Bacc("TRN2", target_bir_lowering=False, num_devices=1)
    args = [nc.dram_tensor(n, a.shape, mybir.dt.from_np(a.dtype), kind="ExternalInput").ap() for n, a in arrays.items()]
    out = nc.dram_tensor("out", (N, C), F32, kind="ExternalOutput").ap()
    build(nc, *args, out)
    r = run_bass_kernel_spmd(nc, [arrays], core_ids=[0])
    return r.results[0]["out"].reshape(BATCH, SEQ, C)
```

```python
from contextlib import ExitStack

import numpy as np
import concourse.bass as bass
from concourse import mybir

F32 = mybir.dt.float32
BF16 = mybir.dt.bfloat16
I32 = mybir.dt.int32
ALU = mybir.AluOpType
ACT = mybir.ActivationFunctionType
AX = mybir.AxisListType

P = 128
BATCH, SEQ, C = 2, 2048, 128
HEADS = 16
HD = C // HEADS
HID = 4 * C
E = 8
EH = 2 * C
N = BATCH * SEQ
NT = N // P
CH = 512
TPC = CH // P
PADDED = SEQ + 2
EPS = 1e-5
Z_EPS = 1e-6
SLOT_TILES = 2 * NT + E
SLOTS = SLOT_TILES * P
ZT = 9
ROW = C + 2
NOWHERE = 1 << 20
MOE_D, MOE_E = 4, 5
assert 2 * BATCH * (MOE_D + MOE_E) * 2 == SLOT_TILES

D_ORDER = ("ctr gate H0.0 H0.1 X1 nd0 nd1 G0 H1.0 Y0 H1.1 at0 X2 at1 G1 H2.0 H2.1 Y1 out0 out1 X3 G2 H3.0 Y2 "
           "H3.1 X4 G3 Y3").split()
E_ORDER = ("ctr0 H0.0 H0.1 tr0 X1 mv0 G0 H1.0 Y0 nm0 H1.1 bk0 X2 ctr1 G1 fc1.0.0 H2.0 Y1 tr1 mv1 H2.1 nm1 "
           "fc1.1.0 X3 fc1.2.0 H3.0 G2 fc1.3.0 H3.1 bk1 Y2 fc2.0 X4 G3 fc1.0.1 H4.0 Y3 H4.1 fc1.1.1 fc1.2.1 G4 "
           "X5 fc1.3.1 Y4 fc2.1").split()

VEC = {}
_c = 0
for _name, _w in (("cpe1_w", 3), ("cpe1_b", 1), ("norm1_g", 1), ("norm1_b", 1), ("in_b", 1), ("actp_b", 1),
                  ("dwc_w", 3), ("dwc_b", 1), ("q_b", 1), ("lepe_w", 3), ("lepe_b", 1), ("out_b", 1),
                  ("cpe2_w", 3), ("cpe2_b", 1), ("norm2_g", 1), ("norm2_b", 1), ("fc1_b", 4)):
    VEC[_name] = (_c, _w)
    _c += _w
NVEC = _c

WCOL = {}
_c = 0
for _name, _w in (("in_w", C), ("actp_w", C), ("q_w", C), ("k_w", C), ("out_w", C), ("fc1_w", HID),
                  ("fc2_w", 4 * C), ("wg", E)):
    WCOL[_name] = (_c, _w)
    _c += _w
NWCOL = _c

KCOL = {}
_c = 0
for _name, _w in (("ident", P), ("headblock", P), ("rope", P), ("rope_t", P), ("headmask", HEADS),
                  ("before", P), ("tile_before", 2 * NT * E), ("same_expert", 2 * E), ("prefer", E),
                  ("expert_before", E * E), ("slot_tile", SLOT_TILES)):
    if _name == "before":
        NSTAY = _c
    KCOL[_name] = (_c, _w)
    _c += _w
NKCOL = _c


def shape_constants():
    k = np.zeros((P, NKCOL), np.float32)

    def put(name, a):
        at, w = KCOL[name]
        k[:, at:at + w] = a

    i = np.arange(P)
    put("ident", np.eye(P))
    put("headblock", i[:, None] // HD == i[None, :] // HD)
    half = np.arange(C // 2, dtype=np.float32)
    theta = np.float32(1.0) / np.float32(10000.0) ** (half / np.float32(C // 2))
    cos, sin = np.cos(theta), np.sin(theta)
    rope = np.zeros((C, C), np.float32)
    even, odd = 2 * np.arange(C // 2), 2 * np.arange(C // 2) + 1
    rope[even, even], rope[odd, even] = cos, -sin
    rope[even, odd], rope[odd, odd] = sin, cos
    put("rope", rope)
    put("rope_t", rope.T)
    put("headmask", i[:, None] // HD == np.arange(HEADS)[None, :])
    put("before", i[:, None] < i[None, :])
    te = np.arange(NT * E)
    earlier = (te[:, None] % E == te[None, :] % E) & (te[:, None] // E < te[None, :] // E)
    put("tile_before", np.concatenate([earlier[:P], earlier[P:]], axis=1))
    same = te[:, None] % E == np.arange(E)[None, :]
    put("same_expert", np.concatenate([same[:P], same[P:]], axis=1))
    put("prefer", (E - np.arange(E))[None, :])
    e = np.arange(E)
    put("expert_before", (e[None, :] < e[:, None]).reshape(1, -1))
    put("slot_tile", np.arange(SLOT_TILES)[None, :])
    return k


def build(nc, x, vecs, row_biases, weights, w12, w3, consts, result_rows, out):
    with ExitStack() as ctx:
        def sb(name, shape, dt=F32):
            return ctx.enter_context(nc.sbuf_tensor(name, shape, dt))

        slot_x = nc.dram_tensor("slot_x", [SLOTS, ROW], F32).ap()
        y_tok = nc.dram_tensor("y_tok", [2 * N, C], F32).ap()

        x_tok = sb("x_tok", [P, N])
        act_all = x_tok
        padA = sb("padA", [P, BATCH * PADDED])
        pad_bc = sb("pad_bc", [P, BATCH * PADDED + max(BATCH * PADDED, NT * ROW)])
        rows1 = pad_bc[:, BATCH * PADDED:BATCH * PADDED + NT * ROW]
        padB = pad_bc[:, 0:BATCH * PADDED]
        padC = pad_bc[:, BATCH * PADDED:2 * BATCH * PADDED]
        x1_all = sb("x1_all", [P, N])
        rows0 = sb("rows0", [P, NT * ROW])
        blk = rows0[:, 0:N]
        vec = sb("vec", [P, NVEC])
        wts = sb("wts", [P, NWCOL])
        w12s = sb("w12s", [P, E * 2 * EH])
        w3s = sb("w3s", [P, E * 2 * C])
        kon = sb("kon", [P, NSTAY])
        cw1 = sb("cw1", [P, 2])
        row_b = sb("row_b", [P, 2 * C])
        kb1, fc2_b = row_b[:, 0:C], row_b[:, C:2 * C]
        qb1 = sb("qb1", [P, 1])
        kb_hi, kb_mid = (sb(n, [3, C], BF16) for n in ("kb_hi", "kb_mid"))
        kb_rest, kb_rest2, kb_sel, kb_sel2 = (sb(n, [3, C]) for n in ("kb_rest", "kb_rest2", "kb_sel", "kb_sel2"))
        kb3 = sb("kb3", [3, C], BF16)
        minus_one = sb("minus_one", [P, 1])
        neg_half = sb("neg_half", [P, 2, TPC])
        mark = sb("mark", [P, 1])
        wide = TPC * (C + 1)
        first_two = sb("first_two", [P, 2 * (4 * CH + wide)])
        last_two = sb("last_two", [P, max(2 * (4 * CH + wide), MOE_E * 2 * (ROW + C) + 4 * 2 * EH + 2 * 2 * P)])
        bufs, norm_t, aff, e_q = ([(first_two, last_two)[c // 2][:, (2 * n + c % 2) * CH:(2 * n + c % 2 + 1) * CH]
                                   for c in range(4)] for n in range(4))
        v_tok = [(first_two, last_two)[c // 2][:, 8 * CH + c % 2 * wide:8 * CH + (c % 2 + 1) * wide].rearrange(
            "p (k n) -> p k n", k=TPC) for c in range(4)]
        att = sb("att", [P, 2, CH])
        hid = sb("hid", [P, 2, 4, CH])
        stats = sb("stats", [P, 4, TPC, 6])
        msum, mdif, vsum, mean, mdif2, vsum2, var_e = (
            sb(n, [P, 4, TPC]) for n in ("msum", "mdif", "vsum", "mean", "mdif2", "vsum2", "var_e"))
        rstd = sb("rstd", [P, 4, TPC])
        dev = sb("dev", [P, 4, TPC])
        kv_sum = sb("kv_sum", [P, BATCH, C + 1])
        kv_s = sb("kv_s", [P, BATCH, C])
        kv_r = sb("kv_r", [P, BATCH, C])
        mk = sb("mk", [P, BATCH, C + HEADS])
        den = sb("den", [P, 2, TPC, HEADS])
        rden = sb("rden", [P, 2, TPC, HEADS])
        te = NT * E
        spare = hid[:, :, :, :].rearrange("p c i n -> p (c i n)")
        lg, eqm, key = (spare[:, i * te:(i + 1) * te].rearrange("p (t e) -> p t e", e=E) for i in range(3))
        oh = spare[:, 3 * te:5 * te].rearrange("p (s t e) -> p s t e", s=2, e=E)
        texp = spare[0:1, 5 * te:5 * te + SLOT_TILES * E].rearrange("p (t e) -> p t e", e=E)
        kon_r = spare[:, 8 * te:8 * te + NKCOL - NSTAY]
        k_tok = [spare[:, c * CH:(c + 1) * CH] for c in range(4)]
        fill = padB[:, 1:1 + ZT * ROW]
        lg_c = e_q
        best = sb("best", [P, 4, NT])
        mask_b = sb("mask_b", [P, NT * E], BF16)
        before_b = sb("before_b", [P, P], BF16)
        tile_b = sb("tile_b", [P, 2 * NT * E], BF16)
        same_b = sb("same_b", [P, 2 * E], BF16)
        ones_b = sb("ones_b", [P, P], BF16)
        tot_b = sb("tot_b", [P, 2, P], BF16)
        tot_c = sb("tot_c", [P, 2])
        slot_f = sb("slot_f", [P, 2, NT])
        res_rows = sb("res_rows", [P, NT, 2], I32)
        slot_i = sb("slot_i", [P, 2, NT], I32)
        prob = sb("prob", [P, NT, 2])
        pt_e = sb("pt_e", [P, 3, NT])
        cnt = sb("cnt", [P, 3, E])
        cnt_i = sb("cnt_i", [P, 2, E], I32)
        ebef = sb("ebef", [P, E, E])
        texp_f = sb("texp_f", [1, SLOT_TILES])
        texp_i = sb("texp_i", [1, SLOT_TILES], I32)
        def parts(*sizes):
            at = 0
            for size in sizes:
                yield last_two[:, at:at + size]
                at += size
        xs, ys, xs_t, s1, s2, gg, gg_t = parts(MOE_E * 2 * ROW, MOE_E * 2 * C, 2 * 2 * P, 2 * EH, 2 * EH, 2 * EH, 2 * 2 * P)
        xs = xs.rearrange("p (r u c) -> p r u c", r=MOE_E, u=2)
        ys = ys.rearrange("p (r u c) -> p r u c", r=MOE_E, u=2)
        xs_t = xs_t.rearrange("p (r u n) -> p r u n", r=2, u=2)
        s1, s2, gg = (a.rearrange("p (u n) -> p u n", u=2) for a in (s1, s2, gg))
        gg_t = gg_t.rearrange("p (u a n) -> p u a n", u=2, a=2)
        y_all = pad_bc[:, 0:2 * N]
        x_again = x1_all
        res = spare

        bank = [ctx.enter_context(nc.psum_tensor(f"bank{i}", [P, 512], F32)) for i in range(8)]
        pt, pu = bank[0:2], bank[2:4]
        mh, mxy, mg = bank[4:6], bank[6], bank[7]
        tq, uq = bank[0:4], bank[4:8]

        def v(name, i=0):
            at, w = VEC[name]
            return vec[:, at + i:at + i + 1]

        def w(name, a=0, b=None):
            at, n = WCOL[name]
            return wts[:, at + a:at + (n if b is None else b)]

        def k(name, parts=P):
            at, n = KCOL[name]
            if at >= NSTAY:
                return kon_r[0:parts, at - NSTAY:at - NSTAY + n]
            return kon[0:parts, at:at + n]

        def tiles(buf, c):
            return [buf[c][:, P * i:P * (i + 1)] for i in range(TPC)]

        WD = C + HEADS
        CHUNKS = 2 * 2 * BATCH
        ALL = CHUNKS + 2

        class Body:

            def __init__(self, eng, n, b, g, at):
                self.b, self.n, self.g = b, n, g
                self.pad0 = eng.snap(b * PADDED + at + 1)
                self.flat0 = eng.snap(b * SEQ + at)
                self.g_n = eng.snap(g * n + 2)

            def chunk(self, buf, c, shift=0):
                return buf[:, bass.ds(self.pad0 + (c * CH + shift), CH)]

            def flat(self, buf, c):
                return buf[:, bass.ds(self.flat0 + c * CH, CH)]

            def done(self, c):
                return self.g_n + (c + 1)

            def nth(self, per_body, n):
                return self.g * per_body + n

            def before(self):
                return self.g_n

            def stored(self):
                return self.g_n * 16

        def each_pair(eng, body):
            with eng.Fori(0, BATCH) as b:
                with eng.Fori(0, 2) as h:
                    body(Body(eng, 2, b, eng.snap(b * 2 + h), h * (2 * CH)))

        def each_batch(eng, body):
            with eng.Fori(0, BATCH) as b:
                body(Body(eng, 4, b, b, 0))

        class Slots:

            def __init__(self, eng, q, in_e):
                self.per = MOE_E if in_e else MOE_D
                self.first = 2 * BATCH * MOE_D if in_e else 0
                self.g = q.g
                self.p0 = eng.snap(q.g * self.per + self.first)

            def done(self, r):
                return self.p0 + (r + 3)

            def done_u(self, r, u):
                return self.p0 * 2 + (2 * r + u + 5)

            def uses(self, r):
                if r == self.per:
                    return self.uses(0) + 1
                return self.g + ((2 * BATCH if self.first and r < MOE_D else 0) + 1)

        USES = [2 * BATCH * (1 + (r < MOE_D)) for r in range(MOE_E)]

        names = """ld_x ld_vec ld_w ld_wg ld_w12 ld_w3 ld_k ld_rows ld_kb
          set_zero set_pads set_const set_cw set_kb3 set_b set_v1 zero_x
          a_st a_mv a_rstd r_step r_exp r_mask r_totc r_totb r_rank r_done s_meta s_scat0 s_scat1 set_padc
          b_st b_mv b_dev b_rstd f_kvs f_kvr1 f_kvr f_m f_mk d_q0 d_q1 e_st e_mv e_rstd e_f10 e_f11 e_h0 e_h1
          m_ld0 m_ld1 m_ld2 m_ld3 m_ld4 m_st0 m_st1 m_st2 m_st3 m_st4 m_a ld_x2 o_y0 o_y1 o_y2 o_y3 carried""".split()
        by_chunk = {
            "vector": "a_xn b_left b_x1 b_nm b_act c_left c_cv c_eq c_qt c_kt c_acc d_de d_rd d_at d_left d_lp d_sum d_ac "
                      "d_x2 e_left e_x3 e_nm e_so o_f o_m",
            "scalar": "a_xnt a_lgc a_l b_ctr b_aff b_xi c_ctr c_v c_rq c_ek c_vtok d_gate d_ctr e_ctr e_aff o_sg",
            "tensor": "a_tr a_lg a_lt b_tr b_back b_in b_gate c_q c_k c_vt c_kv d_nd d_atT d_out e_tr e_back e_s",
            "gpsimd": "o_out",
        }
        by_slots = {"tensor": "m_xt m_gt m_y", "scalar": "m_xtc m_gtc", "vector": "m_ys"}
        by_tile = {"tensor": "m_h", "scalar": "m_s1", "vector": "m_g"}
        stores = ("a_xnst", "a_xnst1", "b_x1st", "c_vst", "o_st")
        for group in (by_chunk, by_slots, by_tile):
            for listed in group.values():
                names += listed.split()
        names += stores
        S = {n: ctx.enter_context(nc.semaphore(n)) for n in names}

        def prime(eng, which):
            for group, n in ((by_chunk, 2), (by_slots, 2), (by_tile, 4)):
                for name in group.get(which, "").split():
                    eng.sem_inc(S[name], n)

        block = ctx.enter_context(nc.Block())

        @block.sync
        def _(sp):
            for b_ in range(BATCH):
                if b_:
                    sp.dma_start(kon[:, :], consts[:, 0:NSTAY]).then_inc(S["ld_k"], 16)
                    sp.wait_ge(S["ld_x"], 32 * b_)
                for at in range(b_ * SEQ, (b_ + 1) * SEQ, SEQ // 2):
                    sp.dma_start(x_tok[:, at:at + SEQ // 2].rearrange("p (t c) -> p t c", c=C),
                                 x[at:at + SEQ // 2, :].rearrange("(t p) c -> p t c", p=P)).then_inc(S["ld_x"], 16)
            for name in stores:
                sp.sem_inc(S[name], 32)

            def store_xn(q):
                for c in range(4):
                    sp.wait_ge(S["a_xn"], q.done(c))
                    for rows, stored in ((rows0, "a_xnst"), (rows1, "a_xnst1")):
                        sp.dma_start(rows[:, bass.ds(q.g * (4 * TPC * ROW) + c * (TPC * ROW), TPC * ROW)].rearrange(
                            "p (t r) -> p t r", r=ROW)[:, :, 0:C], bufs[c][:, :].rearrange("p (t n) -> p t n", n=C))\
                            .then_inc(S[stored], 16)
            each_batch(sp, store_xn)
            def store_x1(q):
                for c in range(4):
                    sp.wait_ge(S["b_x1"], q.done(c))
                    sp.dma_start(q.flat(x1_all, c), bufs[c][:, :]).then_inc(S["b_x1st"], 16)
            each_batch(sp, store_x1)

            sp.wait_ge(S["s_scat1"], 16 * NT)

            def store_v(q):
                for c in range(4):
                    sp.wait_ge(S["c_v"], q.done(c))
                    sp.dma_start(q.chunk(padC, c), bufs[c][:, :]).then_inc(S["c_vst"], 16)
            each_batch(sp, store_v)

            def load_slots(t, r):
                sp.wait_ge(S[f"m_st{r}"], t.uses(r) * 32)
                sp.dma_start(xs[:, r, :, :], slot_x[bass.ds((t.p0 + r) * (2 * P), 2 * P), :].rearrange(
                    "(u p) c -> p u c", p=P)).then_inc(S[f"m_ld{r}"], 16)

            sp.wait_ge(S["c_qt"], ALL)

            def d(q):
                for c in range(2):
                    sp.wait_ge(S["d_nd"], q.before())
                    sp.dma_start(e_q[c][:, :], q.chunk(padA, c)).then_inc(S[f"d_q{c}"], 16)
                sp.wait_ge(S["c_vt"], ALL)
                sp.wait_ge(S["c_vst"], 16 * ALL)
                sp.wait_ge(S["s_scat0"], 16 * NT)
                t = Slots(sp, q, False)
                for r in range(MOE_D):
                    load_slots(t, r)
            each_pair(sp, d)

            def e(q):
                t = Slots(sp, q, True)
                for r in range(MOE_E):
                    load_slots(t, r)
                sp.wait_ge(S["d_x2"], ALL)
                sp.dma_start(x_again[:, bass.ds(q.flat0, 2 * CH)].rearrange("p (t c) -> p t c", c=C),
                             x[bass.ds(q.flat0, 2 * CH), :].rearrange("(t p) c -> p t c", p=P)).then_inc(S["ld_x2"], 16)
            each_pair(sp, e)
            sp.wait_ge(S["m_ld0"], 16 * USES[0])
            sp.sem_inc(S["m_ld0"], 16)

            for r in range(MOE_E):
                sp.wait_ge(S[f"m_st{r}"], 32 * (USES[r] + 1))

            def load_y(b):
                for c in range(4):
                    if b:
                        sp.wait_ge(S[f"o_y{c}"], b * 16)
                    at = b * (2 * SEQ) + c * (2 * CH)
                    sp.dma_start(y_all[:, at:at + 2 * CH].rearrange("p (t s c) -> p t (s c)", s=2, c=C),
                                 y_tok[at:at + 2 * CH, :].rearrange("(t p s) c -> p t (s c)", p=P, s=2))\
                        .then_inc(S[f"o_y{c}"], 16)
            for b_ in range(BATCH):
                load_y(b_)

            def store(q):
                for c in range(4):
                    sp.wait_ge(S["o_out"], q.done(c))
                    sp.dma_start(out[bass.ds(q.flat0 + c * CH, CH), :].rearrange("(t p) c -> p t c", p=P),
                                 q.flat(res, c).rearrange("p (t c) -> p t c", c=C)).then_inc(S["o_st"], 16)
            each_batch(sp, store)
            sp.wait_ge(S["o_st"], 16 * ALL)

        @block.gpsimd
        def _(pool):
            pool.memset(neg_half[:, :, :], -0.5).then_inc(S["set_const"], 1)
            def zero_pads(buf, done):
                edges = buf[:, :].rearrange("p (b n) -> p b n", b=BATCH)
                pool.memset(edges[:, :, 0:PADDED:PADDED - 1], 0.0).then_inc(S[done], 1)
            zero_pads(padA, "set_pads")
            zero_pads(padB, "set_pads")
            pool.memset(fill, 0.0).then_inc(S["set_zero"], 1)
            pool.wait_ge(S["set_zero"], 1)
            pool.memset(fill.bitcast(I32)[:, C:ZT * ROW:ROW], NOWHERE).then_inc(S["set_zero"], 1)
            prime(pool, "gpsimd")
            pool.wait_ge(S["set_const"], 1)

            def root(q, ph, i=0, chunks=2):
                some = slice(chunks * i, chunks * (i + 1))
                pool.wait_ge(S[ph + "_mv"], q.nth(q.n // chunks * 3, 3 * i + 3))
                pool.tensor_tensor(rstd[:, some, :], var_e[:, some, :], neg_half[:, 0:chunks, :], ALU.pow)\
                    .then_inc(S[ph + "_rstd"], 1)

            def carry():
                pool.sem_inc(S["carried"], 1)

            def a(q):
                for h in range(2):
                    root(q, "a", h)
            each_batch(pool, a)
            pool.wait_ge(S["set_zero"], 2)
            for r in range(MOE_E):
                for u in range(2):
                    pool.indirect_dma_start(out=y_tok[:, :],
                                            out_offset=bass.IndirectOffsetOnAxis(fill[:, C:C + 1].bitcast(I32), 0),
                                            in_=fill[:, 0:C], in_offset=None, bounds_check=2 * N - 1,
                                            oob_is_err=False).then_inc(S[f"m_st{r}"], 16)

            pool.wait_ge(S["ld_k"], 32)
            for dst, name in ((before_b, "before"), (tile_b, "tile_before"), (same_b, "same_expert")):
                pool.tensor_copy(dst[:, :], k(name)).then_inc(S["set_b"], 1)

            pool.wait_ge(S["ld_rows"], 16)
            pool.wait_ge(S["r_done"], 1)
            pool.wait_ge(S["a_xnst"], 16 * ALL)
            pool.wait_ge(S["a_xnst1"], 16 * ALL)
            pool.wait_ge(S["zero_x"], 16 * (SLOT_TILES // ZT))
            for s, rows in ((1, rows1), (0, rows0)):
                row = rows[:, :].rearrange("p (t r) -> p t r", r=ROW)
                pool.tensor_copy(row[:, :, C].bitcast(I32), res_rows[:, :, s]).then_inc(S["s_meta"], 1)
                pool.tensor_copy(row[:, :, C + 1], prob[:, :, s]).then_inc(S["s_meta"], 1)
            pool.wait_ge(S["s_meta"], 4)

            for s, rows in ((1, rows1), (0, rows0)):
                for t in range(NT):
                    pool.indirect_dma_start(out=slot_x[:, :], out_offset=bass.IndirectOffsetOnAxis(slot_i[:, s, t:t + 1], 0),
                                            in_=rows[:, t * ROW:(t + 1) * ROW], in_offset=None).then_inc(S[f"s_scat{s}"], 16)
            pool.wait_ge(S["s_scat1"], 16 * NT)
            zero_pads(padC, "set_padc")

            def store_slots(t, r):
                pool.wait_ge(S["m_ys"], t.done(r))
                carry()
                for u in range(2):
                    pool.indirect_dma_start(out=y_tok[:, :],
                                            out_offset=bass.IndirectOffsetOnAxis(xs[:, r, u, C:C + 1].bitcast(I32), 0),
                                            in_=ys[:, r, u, :], in_offset=None, bounds_check=2 * N - 1,
                                            oob_is_err=False).then_inc(S[f"m_st{r}"], 16)

            def d(q):
                t = Slots(pool, q, False)
                for step in D_ORDER:
                    if step[0] == "Y":
                        store_slots(t, int(step[1:]))
            each_pair(pool, d)

            def e(q):
                t = Slots(pool, q, True)
                for step in E_ORDER:
                    if step[:2] == "mv":
                        root(q, "e", int(step[2]), chunks=1)
                    if step[0] == "Y":
                        store_slots(t, int(step[1:]))
            each_pair(pool, e)

            def f(q):
                for c in range(4):
                    pool.wait_ge(S["o_m"], q.done(c))
                    pool.tensor_tensor(q.flat(res, c), q.flat(res, c), q.flat(x_again, c), ALU.add).then_inc(S["o_out"], 1)
            pool.wait_ge(S["ld_x2"], 16 * 2 * BATCH)
            each_batch(pool, f)

        def settle(act, func):
            nc.scalar.activation(mark[:, 0:1], ones_b[:, 0:1], func)

        @block.scalar
        def _(act):
            act.dma_start(w("wg"), weights[:, WCOL["wg"][0]:NWCOL]).then_inc(S["ld_wg"], 16)
            act.dma_start(kon_r, consts[:, NSTAY:NKCOL]).then_inc(S["ld_k"], 16)
            act.dma_start(vec[:, :], vecs).then_inc(S["ld_vec"], 16)
            act.dma_start(row_b[:, :], row_biases.broadcast_to([P, 2 * C])).then_inc(S["ld_kb"], 16)
            act.dma_start(res_rows[:, :, :].rearrange("p t s -> p (t s)"), result_rows).then_inc(S["ld_rows"], 16)
            act.wait_ge(S["set_zero"], 2)
            zero_v = slot_x.rearrange("(p t) c -> p (t c)", p=P)
            def fill_slots(some):
                for i in some:
                    act.dma_start(zero_v[:, i * ZT * ROW:(i + 1) * ZT * ROW], fill).then_inc(S["zero_x"], 16)
            fill_slots(range(0, 3))
            prime(act, "scalar")
            act.wait_ge(S["set_pads"], 2)

            def a(q):
                for c in range(4):
                    act.wait_ge(S["a_tr"], q.done(c))
                    nc.scalar.activation(q.chunk(padA, c), tq[c][:, :], ACT.Copy).then_inc(S["a_xnt"], 1)
                for c in range(4):
                    act.wait_ge(S["a_lg"], q.done(c))
                    act.wait_ge(S["a_lt"], q.before())
                    nc.scalar.activation(lg_c[c][0:E, :], uq[c][0:E, :], ACT.Copy).then_inc(S["a_lgc"], 1)
                for c in range(4):
                    act.wait_ge(S["a_lt"], q.done(c))
                    nc.scalar.activation(lg[:, bass.ds(q.g * (4 * TPC) + c * TPC, TPC), :],
                                         uq[c][:, 0:TPC * E].rearrange("p (t e) -> p t e", e=E), ACT.Copy)\
                        .then_inc(S["a_l"], 1)
            act.wait_ge(S["set_v1"], 6)
            settle(act, ACT.Exp)
            each_batch(act, a)
            fill_slots(range(3, SLOT_TILES // ZT))
            act.dma_start(wts[:, 0:WCOL["wg"][0]], weights[:, 0:WCOL["wg"][0]]).then_inc(S["ld_w"], 16)

            act.wait_ge(S["r_exp"], 1)
            nc.scalar.activation(pt_e[:, 1, :], pt_e[:, 0, :], ACT.Exp).then_inc(S["r_exp"], 1)

            act.wait_ge(S["ld_vec"], 16)
            act.wait_ge(S["set_cw"], 1)
            act.wait_ge(S["a_l"], ALL)
            act.wait_ge(S["a_xnst"], 16 * ALL)
            act.wait_ge(S["a_xnst1"], 16 * ALL)
            act.wait_ge(S["a_xnt"], ALL)

            def b(q):
                for c in range(4):
                    act.wait_ge(S["b_tr"], q.before())
                    act.wait_ge(S["b_x1st"], q.stored())
                    nc.scalar.activation(bufs[c][:, :], q.chunk(padA, c), ACT.Identity, bias=v("cpe1_b"),
                                         scale=cw1[:, 0:1]).then_inc(S["b_ctr"], 1)
                def deviation(h):
                    two = slice(2 * h, 2 * h + 2)
                    act.wait_ge(S["b_mv"], q.nth(6, 3 * h + 3))
                    nc.scalar.activation(dev[:, two, :], var_e[:, two, :], ACT.Sqrt).then_inc(S["b_dev"], 1)

                def affine(c):
                    act.wait_ge(S["b_back"], q.done(c))
                    act.wait_ge(S["b_gate"], q.before())
                    nc.scalar.activation(aff[c][:, :], uq[c][:, :], ACT.Identity, bias=v("norm1_b"),
                                         scale=v("norm1_g")).then_inc(S["b_aff"], 1)

                def inner(c):
                    act.wait_ge(S["b_in"], q.done(c))
                    nc.scalar.activation(q.chunk(padB, c), tq[c][:, :], ACT.Identity, bias=v("in_b")).then_inc(S["b_xi"], 1)

                deviation(0)
                affine(0)
                affine(1)
                deviation(1)
                act.wait_ge(S["zero_x"], 16 * (SLOT_TILES // ZT))
                for r in range(MOE_E):
                    act.wait_ge(S[f"m_st{r}"], 32)
                inner(0)
                affine(2)
                inner(1)
                affine(3)
                inner(2)
                inner(3)
            settle(act, ACT.Sqrt)
            each_batch(act, b)
            act.dma_start(w12s[:, :], w12).then_inc(S["ld_w12"], 16)
            act.dma_start(w3s[:, :], w3).then_inc(S["ld_w3"], 16)

            act.wait_ge(S["b_xi"], ALL)
            act.wait_ge(S["b_x1st"], 16 * ALL)

            def cc(q):
                for c in range(4):
                    nc.scalar.activation(norm_t[c][:, :], q.chunk(padB, c), ACT.Identity, bias=v("dwc_b"),
                                         scale=v("dwc_w", 1)).then_inc(S["c_ctr"], 1)
                for c in range(4):
                    act.wait_ge(S["c_cv"], q.done(c))
                    act.wait_ge(S["c_vst"], q.stored())
                    act.wait_ge(S["c_vt"], q.before())
                    nc.scalar.activation(bufs[c][:, :], norm_t[c][:, :], ACT.Silu).then_inc(S["c_v"], 1)

                def exps(c):
                    act.wait_ge(S["c_q"], q.done(c))
                    act.wait_ge(S["c_qt"], q.before())
                    nc.scalar.activation(e_q[c][:, :], tq[c][:, :], ACT.Exp, bias=v("q_b")).then_inc(S["c_rq"], 1)
                    act.wait_ge(S["c_k"], q.done(c))
                    nc.scalar.activation(aff[c][:, :], uq[c][:, :], ACT.Exp, bias=minus_one[:, 0:1]).then_inc(S["c_ek"], 1)

                def v_out(c):
                    act.wait_ge(S["c_vt"], q.done(c))
                    act.wait_ge(S["c_kv"], q.before())
                    nc.scalar.activation(v_tok[c][:, :, 0:C], tq[c][:, :].rearrange("p (k n) -> p k n", k=TPC),
                                         ACT.Copy).then_inc(S["c_vtok"], 1)

                exps(0)
                exps(1)
                v_out(0)
                exps(2)
                v_out(1)
                exps(3)
                v_out(2)
                settle(act, ACT.Silu)
                v_out(3)
            settle(act, ACT.Silu)
            each_batch(act, cc)

            def rows_out(t, r):
                act.wait_ge(S["m_xt"], t.done(r))
                copy_rows(r % t.per % 2)

            def copy_rows(buf):
                nc.scalar.activation(xs_t[:, buf, :, :], mxy[:, 0:2 * P].rearrange("p (u n) -> p u n", u=2),
                                     ACT.Copy).then_inc(S["m_xtc"], 1)

            def gated_out(t, r):
                act.wait_ge(S["m_gt"], t.done(r))
                nc.scalar.activation(gg_t[:, :, :, :], mg[:, :].rearrange("p (u a n) -> p u a n", u=2, a=2),
                                     ACT.Copy).then_inc(S["m_gtc"], 1)

            act.wait_ge(S["c_vst"], 16 * ALL)
            act.wait_ge(S["m_xt"], 3)
            copy_rows(0)

            def d(q):
                t = Slots(act, q, False)
                for step in D_ORDER:
                    if step == "gate":
                        for c in range(2):
                            nc.scalar.activation(q.flat(act_all, c), q.flat(act_all, c), ACT.Silu).then_inc(S["d_gate"], 1)
                    elif step == "ctr":
                        for c in range(2):
                            act.wait_ge(S["d_ac"], q.before())
                            nc.scalar.activation(norm_t[c][:, :], q.chunk(padC, c), ACT.Identity, bias=v("lepe_b"),
                                                 scale=v("lepe_w", 1)).then_inc(S["d_ctr"], 1)
                    elif step[0] == "X":
                        rows_out(t, int(step[1:]))
                    elif step[0] == "H":
                        r, u = map(int, step[1:].split("."))
                        act.wait_ge(S["m_h"], t.done_u(r, u))
                        act.wait_ge(S["m_g"], t.done_u(r - 1, u))
                        nc.scalar.activation(s1[:, u, :], mh[u][:, 0:EH], ACT.Silu).then_inc(S["m_s1"], 1)
                    elif step[0] == "G":
                        gated_out(t, int(step[1:]))
            each_pair(act, d)

            act.wait_ge(S["d_x2"], ALL)

            def e(q):
                t = Slots(act, q, True)
                for step in E_ORDER:
                    if step[:3] == "ctr":
                        c = int(step[3])
                        act.wait_ge(S["e_s"], q.before())
                        nc.scalar.activation(bufs[c][:, :], q.chunk(padA, c), ACT.Identity, bias=v("cpe2_b"),
                                             scale=cw1[:, 1:2]).then_inc(S["e_ctr"], 1)
                    elif step[:2] == "bk":
                        c = int(step[2])
                        act.wait_ge(S["e_back"], q.done(c))
                        nc.scalar.activation(aff[c][:, :], pu[c][:, :], ACT.Identity, bias=v("norm2_b"),
                                             scale=v("norm2_g")).then_inc(S["e_aff"], 1)
                    elif step[:3] == "fc1":
                        i, c = map(int, step[4:].split("."))
                        act.wait_ge(S[f"e_f1{c}"], q.nth(4, i + 1))
                        nc.scalar.activation(hid[:, c, i, :], (pt, pu)[i % 2][c][:, :], ACT.Gelu,
                                             bias=v("fc1_b", i)).then_inc(S[f"e_h{c}"], 1)
                    elif step[0] == "X":
                        rows_out(t, int(step[1:]))
                    elif step[0] == "H":
                        r, u = map(int, step[1:].split("."))
                        act.wait_ge(S["m_h"], t.done_u(r, u))
                        act.wait_ge(S["m_g"], t.done_u(r - 1, u))
                        nc.scalar.activation(s1[:, u, :], mh[u][:, 0:EH], ACT.Tanh, scale=0.5).then_inc(S["m_s1"], 1)
                    elif step[0] == "G":
                        gated_out(t, int(step[1:]))
            settle(act, ACT.Gelu)
            each_pair(act, e)

            def f(q):
                for c in range(4):
                    act.wait_ge(S["o_f"], q.done(c))
                    nc.scalar.activation(q.flat(res, c), q.flat(res, c), ACT.Silu).then_inc(S["o_sg"], 1)
            settle(act, ACT.Silu)
            each_batch(act, f)

        @block.vector
        def _(dve):
            dve.memset(ones_b[:, :], 1.0).then_inc(S["set_v1"], 1)
            dve.memset(minus_one[:, :], -1.0).then_inc(S["set_v1"], 1)
            for c in range(4):
                dve.memset(v_tok[c][:, :, C:C + 1], 1.0).then_inc(S["set_v1"], 1)
            prime(dve, "vector")

            def stats_of(q, ph, src, c):
                for i, t in enumerate(src):
                    ins = dve.bn_stats(stats[:, c, i, :], t)
                ins.then_inc(S[ph + "_st"], 1)

            def moments(q, ph, i=0, chunks=2):
                some = slice(chunks * i, chunks * (i + 1))
                n = q.n // chunks * 3
                m_even, m_odd, v_even, v_odd = (stats[:, some, :, at] for at in (1, 4, 2, 5))
                dve.wait_ge(S[ph + "_st"], q.nth(q.n, chunks * (i + 1)))
                dve.tensor_tensor(msum[:, some, :], m_even, m_odd, ALU.add)
                dve.tensor_tensor(mdif[:, some, :], m_even, m_odd, ALU.subtract)
                dve.tensor_tensor(vsum[:, some, :], v_even, v_odd, ALU.add).then_inc(S[ph + "_mv"], 1)
                dve.wait_ge(S[ph + "_mv"], q.nth(n, 3 * i + 1))
                dve.tensor_scalar(mean[:, some, :], msum[:, some, :], 0.5, None, ALU.mult)
                dve.tensor_tensor(mdif2[:, some, :], mdif[:, some, :], mdif[:, some, :], ALU.mult)
                dve.tensor_scalar(vsum2[:, some, :], vsum[:, some, :], 1.0 / C, EPS, ALU.mult, ALU.add)\
                    .then_inc(S[ph + "_mv"], 1)
                dve.wait_ge(S[ph + "_mv"], q.nth(n, 3 * i + 2))
                dve.scalar_tensor_tensor(var_e[:, some, :], mdif2[:, some, :], 0.25, vsum2[:, some, :], ALU.mult, ALU.add)\
                    .then_inc(S[ph + "_mv"], 1)

            def normalize(q, ph, src, dst, c, done, chunks=2):
                dve.wait_ge(S[ph + "_rstd"], q.nth(q.n // chunks, c // chunks + 1))
                for i, t in enumerate(src):
                    ins = dve.tensor_scalar(dst[c][:, P * i:P * (i + 1)], t, mean[:, c, i:i + 1],
                                            rstd[:, c, i:i + 1], ALU.subtract, ALU.mult)
                ins.then_inc(S[done], 1)

            def a(q):
                src = [[x_tok[:, bass.ds(q.flat0 + (c * CH + P * i), P)] for i in range(TPC)] for c in range(4)]
                dve.wait_ge(S["ld_x"], q.nth(32, 32))
                for c in range(4):
                    stats_of(q, "a", src[c], c)
                    if c % 2:
                        moments(q, "a", c // 2)
                dve.wait_ge(S["a_tr"], q.before())
                dve.wait_ge(S["a_xnst"], q.stored())
                dve.wait_ge(S["a_xnst1"], q.stored())
                for c in range(4):
                    normalize(q, "a", src[c], bufs, c, "a_xn")
            each_batch(dve, a)
            dve.wait_ge(S["ld_vec"], 16)
            dve.wait_ge(S["ld_kb"], 16)
            dve.tensor_scalar(cw1[:, 0:1], v("cpe1_w", 1), 1.0, None, ALU.add)
            dve.tensor_scalar(cw1[:, 1:2], v("cpe2_w", 1), 1.0, None, ALU.add)
            dve.tensor_scalar(qb1[:, :], v("q_b"), 1.0, None, ALU.add)
            dve.tensor_scalar(kb1, kb1, 1.0, None, ALU.add).then_inc(S["set_cw"], 1)

            kb, ident3 = row_b[0:3, 0:C], k("ident", 3)
            dve.wait_ge(S["ld_k"], 32)
            dve.wait_ge(S["set_cw"], 1)
            dve.tensor_copy(kb_hi[:, :], kb).then_inc(S["set_kb3"], 1)
            dve.wait_ge(S["set_kb3"], 1)
            dve.tensor_scalar(kb_sel[:, :], kb_hi[:, :], ident3[:, 0:1], None, ALU.mult)
            dve.tensor_tensor(kb_rest[:, :], kb, kb_hi[:, :], ALU.subtract).then_inc(S["set_kb3"], 1)
            dve.wait_ge(S["set_kb3"], 2)
            dve.tensor_copy(kb_mid[:, :], kb_rest[:, :]).then_inc(S["set_kb3"], 1)
            dve.wait_ge(S["set_kb3"], 3)
            dve.scalar_tensor_tensor(kb_sel2[:, :], kb_mid[:, :], ident3[:, 1:2], kb_sel[:, :], ALU.mult, ALU.add)
            dve.tensor_tensor(kb_rest2[:, :], kb_rest[:, :], kb_mid[:, :], ALU.subtract).then_inc(S["set_kb3"], 1)
            dve.wait_ge(S["set_kb3"], 4)
            dve.scalar_tensor_tensor(kb3[:, :], kb_rest2[:, :], ident3[:, 2:3], kb_sel2[:, :], ALU.mult, ALU.add)\
                .then_inc(S["set_kb3"], 1)

            dve.wait_ge(S["a_l"], ALL)
            steps = [0]

            def step(ins):
                steps[0] += 1
                ins.then_inc(S["r_step"], 1)

            def settled():
                dve.wait_ge(S["r_step"], steps[0])

            def over_e(a):
                return a.unsqueeze(2).broadcast_to([P, NT, E])

            prefer = k("prefer").unsqueeze(1).broadcast_to([P, NT, E])
            for s in range(2):
                src = lg if s == 0 else eqm
                step(dve.tensor_reduce(best[:, s, :], src[:, :, :], AX.X, ALU.max))
                settled()
                step(dve.tensor_tensor(key[:, :, :], src[:, :, :], over_e(best[:, s, :]), ALU.is_equal))
                settled()
                step(dve.tensor_tensor(key[:, :, :], key[:, :, :], prefer, ALU.mult))
                settled()
                step(dve.tensor_reduce(best[:, 2 + s, :], key[:, :, :], AX.X, ALU.max))
                settled()
                step(dve.tensor_tensor(oh[:, s, :, :], key[:, :, :], over_e(best[:, 2 + s, :]), ALU.is_equal))
                settled()
                if s == 0:
                    step(dve.scalar_tensor_tensor(eqm[:, :, :], oh[:, 0, :, :], -3.0e38, lg[:, :, :], ALU.mult, ALU.add))
                    settled()
            dve.tensor_tensor(mask_b[:, :].rearrange("p (t e) -> p t e", e=E), oh[:, 0, :, :], oh[:, 1, :, :], ALU.add)\
                .then_inc(S["r_mask"], 1)
            dve.tensor_tensor(pt_e[:, 0, :], best[:, 1, :], best[:, 0, :], ALU.subtract).then_inc(S["r_exp"], 1)
            dve.wait_ge(S["r_totc"], 1)
            step(dve.tensor_copy(tot_c[:, :], pt[0][:, 0:2]))
            settled()
            for s in range(2):
                ins = dve.tensor_scalar(tot_b[:, s, :], ones_b[:, :], tot_c[:, s:s + 1], None, ALU.mult)
            ins.then_inc(S["r_totb"], 1)
            dve.wait_ge(S["r_exp"], 2)
            step(dve.tensor_scalar(pt_e[:, 2, :], pt_e[:, 1, :], 1.0, None, ALU.add))
            settled()
            step(dve.reciprocal(prob[:, :, 0], pt_e[:, 2, :]))
            settled()
            step(dve.tensor_tensor(prob[:, :, 1], prob[:, :, 0], pt_e[:, 1, :], ALU.mult))
            dve.wait_ge(S["r_rank"], 1)
            step(dve.tensor_scalar(cnt_i[:, 0, :], pt[1][:, 0:E], float(P - 1), None, ALU.add))
            settled()
            step(dve.tensor_scalar(cnt_i[:, 1, :], cnt_i[:, 0, :], 7, None, ALU.arith_shift_right))
            settled()
            step(dve.tensor_copy(cnt[:, 0, :], cnt_i[:, 1, :]))
            settled()
            step(dve.tensor_tensor(ebef[:, :, :], k("expert_before").rearrange("p (a b) -> p a b", b=E),
                                   cnt[:, 0, :].unsqueeze(1).broadcast_to([P, E, E]), ALU.mult))
            settled()
            step(dve.tensor_reduce(cnt[:, 1, :], ebef[:, :, :], AX.X, ALU.add))
            settled()
            step(dve.tensor_tensor(cnt[:, 2, :], cnt[:, 0, :], cnt[:, 1, :], ALU.add))
            step(dve.scalar_tensor_tensor(eqm[:, :, :], cnt[:, 1, :].unsqueeze(1).broadcast_to([P, NT, E]), float(P),
                                          pu[0][:, 0:NT * E].rearrange("p (t e) -> p t e", e=E), ALU.mult, ALU.add))
            settled()
            for s in range(2):
                step(dve.tensor_tensor(key[:, :, :], oh[:, s, :, :], eqm[:, :, :], ALU.mult))
                settled()
                step(dve.tensor_reduce(slot_f[:, s, :], key[:, :, :], AX.X, ALU.add))
                settled()
            dve.tensor_copy(slot_i[:, :, :], slot_f[:, :, :]).then_inc(S["r_done"], 1)

            def outer_tap(q, ph, buf, src, weight, c, side, done):
                dve.wait_ge(S[ph + ("_ctr" if side < 0 else "_left")], q.done(c))
                dve.scalar_tensor_tensor(buf[c][:, :], q.chunk(src, c, side), v(weight, 1 + side), buf[c][:, :], ALU.mult,
                                         ALU.add).then_inc(S[ph + "_left" if side < 0 else done], 1)

            def taps(q, ph, buf, src, weight, done, groups=None):
                for group in groups or [(c, c + 1) for c in range(0, q.n, 2)]:
                    for side in (-1, 1):
                        for c in group:
                            outer_tap(q, ph, buf, src, weight, c, side, done)

            def in_psum(c):
                return [bank[c][:, P * i:P * (i + 1)] for i in range(TPC)]

            dve.wait_ge(S["set_pads"], 2)

            def b(q):
                def tap(c, side):
                    outer_tap(q, "b", bufs, padA, "cpe1_w", c, side, "b_x1")

                def half_stats(h):
                    for c in (2 * h, 2 * h + 1):
                        dve.wait_ge(S["b_tr"], q.done(c))
                        stats_of(q, "b", in_psum(c), c)
                    moments(q, "b", h)

                def half_norm(h):
                    dve.wait_ge(S["b_dev"], q.nth(2, h + 1))
                    dve.reciprocal(rstd[:, 2 * h:2 * h + 2, :], dev[:, 2 * h:2 * h + 2, :]).then_inc(S["b_rstd"], 1)
                    for c in (2 * h, 2 * h + 1):
                        normalize(q, "b", in_psum(c), norm_t, c, "b_nm")

                for c, side in ((0, -1), (1, -1), (0, 1), (1, 1), (2, -1), (3, -1)):
                    tap(c, side)
                half_stats(0)
                tap(2, 1)
                tap(3, 1)
                dve.wait_ge(S["b_back"], q.before())
                half_norm(0)
                half_stats(1)
                half_norm(1)
                for c in range(4):
                    dve.wait_ge(S["b_gate"], q.done(c))
                    dve.tensor_scalar(q.flat(act_all, c), uq[c][:, :], v("actp_b"), None, ALU.add).then_inc(S["b_act"], 1)
            each_batch(dve, b)

            step(dve.tensor_tensor(texp[:, :, :], k("slot_tile", 1).unsqueeze(2).broadcast_to([1, SLOT_TILES, E]),
                                   cnt[0:1, 2, :].unsqueeze(1).broadcast_to([1, SLOT_TILES, E]), ALU.is_ge))
            settled()
            step(dve.tensor_reduce(texp_f[:, :], texp[:, :, :], AX.X, ALU.add))
            settled()
            dve.tensor_scalar(texp_i[:, :], texp_f[:, :], float(E - 1), None, ALU.min).then_inc(S["r_done"], 1)

            dve.wait_ge(S["set_cw"], 1)

            def cc(q):
                taps(q, "c", norm_t, padB, "dwc_w", "c_cv")
                for c in range(4):
                    dve.wait_ge(S["c_rq"], q.done(c))
                    dve.tensor_scalar(e_q[c][:, :], e_q[c][:, :], 1.0, None, ALU.min).then_inc(S["c_eq"], 1)
                    dve.wait_ge(S["c_eq"], q.done(c))
                    dve.scalar_tensor_tensor(q.chunk(padA, c), tq[c][:, :], qb1[:, 0:1], e_q[c][:, :], ALU.add, ALU.max)\
                        .then_inc(S["c_qt"], 1)
                    dve.wait_ge(S["c_ek"], q.done(c))
                    dve.wait_ge(S["c_kv"], q.before())
                    dve.scalar_tensor_tensor(k_tok[c][:, :], aff[c][:, :], 1.0, uq[c][:, :], ALU.min, ALU.max)\
                        .then_inc(S["c_kt"], 1)
                dve.wait_ge(S["c_kv"], q.done(3))
                dve.tensor_copy(kv_sum[:, bass.ds(q.b, 1), :].rearrange("p a n -> p (a n)"), uq[0][:, 0:C + 1])\
                    .then_inc(S["c_acc"], 4)
            each_batch(dve, cc)

            dve.wait_ge(S["c_acc"], ALL)
            for b_ in range(BATCH):
                dve.tensor_scalar(kv_s[:, b_, :], kv_sum[:, b_, 0:C], 1.0 / SEQ, None, ALU.mult).then_inc(S["f_kvs"], 1)
                dve.tensor_scalar(mk[:, b_, C:C + HEADS], k("headmask"), kv_sum[:, b_, C:C + 1], 1.0 / SEQ, ALU.mult,
                                  ALU.mult).then_inc(S["f_mk"], 1)
            for b_ in range(BATCH):
                dve.wait_ge(S["f_kvr1"], b_ + 1)
                dve.tensor_tensor(kv_r[:, b_, :], pt[b_][:, 0:C], k("headblock"), ALU.mult).then_inc(S["f_kvr"], 1)
            for b_ in range(BATCH):
                dve.wait_ge(S["f_m"], b_ + 1)
                dve.tensor_copy(mk[:, b_, 0:C], pu[b_][:, 0:C]).then_inc(S["f_mk"], 1)

            def experts_out(t, r):
                dve.wait_ge(S["m_y"], t.done(r))
                dve.wait_ge(S[f"m_st{r}"], t.uses(r) * 32)
                for u in range(2):
                    ins = dve.tensor_scalar(ys[:, r, u, :], mxy[:, (2 + u) * P:(3 + u) * P], xs[:, r, u, C + 1:C + 2], None,
                                            ALU.mult)
                ins.then_inc(S["m_ys"], 1)

            def d(q):
                t = Slots(dve, q, False)
                for step in D_ORDER:
                    if step == "ctr":
                        taps(q, "d", norm_t, padC, "lepe_w", "d_lp")
                    elif step[:2] == "nd":
                        c = int(step[2])
                        halves = [(pt, pu)[a_][c][:, 0:2 * WD].rearrange("p (k n) -> p k n", k=2) for a_ in range(2)]
                        dve.wait_ge(S["d_nd"], q.done(c))
                        for a_, nd in enumerate(halves):
                            ins = dve.tensor_scalar(den[:, c, 2 * a_:2 * a_ + 2, :], nd[:, :, C:WD], Z_EPS, None, ALU.add)
                        ins.then_inc(S["d_de"], 1)
                        dve.wait_ge(S["d_de"], q.done(c))
                        dve.reciprocal(rden[:, c, :, :], den[:, c, :, :]).then_inc(S["d_rd"], 1)
                        dve.wait_ge(S["d_rd"], q.done(c))
                        for a_, nd in enumerate(halves):
                            ins = dve.tensor_tensor(
                                att[:, c, 2 * a_ * P:(2 * a_ + 2) * P].rearrange("p (k h d) -> p k h d", k=2, h=HEADS),
                                nd[:, :, 0:C].rearrange("p k (h d) -> p k h d", h=HEADS),
                                rden[:, c, 2 * a_:2 * a_ + 2, :].unsqueeze(3).broadcast_to([P, 2, HEADS, HD]), ALU.mult)
                        ins.then_inc(S["d_at"], 1)
                    elif step[:2] == "at":
                        c = int(step[2])
                        dve.wait_ge(S["d_atT"], q.done(c))
                        dve.wait_ge(S["d_lp"], q.done(c))
                        dve.tensor_tensor(norm_t[c][:, :], norm_t[c][:, :], pt[c][:, :], ALU.add).then_inc(S["d_sum"], 1)
                        dve.wait_ge(S["d_sum"], q.done(c))
                        dve.wait_ge(S["d_gate"], q.done(c))
                        dve.tensor_tensor(aff[c][:, :], norm_t[c][:, :], q.flat(act_all, c), ALU.mult).then_inc(S["d_ac"], 1)
                    elif step[:3] == "out":
                        c = int(step[3])
                        dve.wait_ge(S["d_out"], q.done(c))
                        dve.scalar_tensor_tensor(q.chunk(padA, c), pu[c][:, :], v("out_b"), q.flat(x1_all, c), ALU.add,
                                                 ALU.add).then_inc(S["d_x2"], 1)
                    elif step[0] == "H":
                        r, u = map(int, step[1:].split("."))
                        dve.wait_ge(S["m_s1"], t.done_u(r, u))
                        dve.wait_ge(S["m_gt"], t.done(r - 1))
                        dve.tensor_tensor(gg[:, u, :], s1[:, u, :], mh[u][:, EH:2 * EH], ALU.mult).then_inc(S["m_g"], 1)
                    elif step[0] == "Y":
                        experts_out(t, int(step[1:]))
            dve.wait_ge(S["b_x1st"], 16 * ALL)
            dve.wait_ge(S["c_vst"], 16 * ALL)
            dve.wait_ge(S["set_padc"], 1)
            each_pair(dve, d)
            dve.wait_ge(S["d_x2"], ALL)

            def e(q):
                t = Slots(dve, q, True)
                for step in E_ORDER:
                    if step[:3] == "ctr":
                        taps(q, "e", bufs, padA, "cpe2_w", "e_x3", [(int(step[3]),)])
                    elif step[:2] == "tr":
                        c = int(step[2])
                        dve.wait_ge(S["e_tr"], q.done(c))
                        stats_of(q, "e", in_psum(c), c)
                    elif step[:2] == "mv":
                        moments(q, "e", int(step[2]), chunks=1)
                    elif step[:2] == "nm":
                        c = int(step[2])
                        dve.wait_ge(S["e_back"], q.before())
                        normalize(q, "e", in_psum(c), norm_t, c, "e_nm", chunks=1)
                    elif step[:3] == "fc2":
                        c = int(step[4])
                        dve.wait_ge(S["e_s"], q.done(c))
                        dve.tensor_tensor(q.flat(blk, c).rearrange("p (t n) -> p t n", n=C),
                                          pt[c][:, :].rearrange("p (t n) -> p t n", n=C),
                                          fc2_b.unsqueeze(1).broadcast_to([P, TPC, C]), ALU.add).then_inc(S["e_so"], 1)
                    elif step[0] == "H":
                        r, u = map(int, step[1:].split("."))
                        dve.wait_ge(S["m_s1"], t.done_u(r, u))
                        dve.scalar_tensor_tensor(s2[:, u, :], s1[:, u, :], 1.0, mh[u][:, 0:EH], ALU.add, ALU.mult)\
                            .then_inc(S["m_a"], 1)
                        dve.wait_ge(S["m_a"], q.nth(2 * MOE_E, 2 * r + u + 1))
                        dve.wait_ge(S["m_gt"], t.done(r - 1))
                        dve.scalar_tensor_tensor(gg[:, u, :], s2[:, u, :], 0.5, mh[u][:, EH:2 * EH], ALU.mult, ALU.mult)\
                            .then_inc(S["m_g"], 1)
                    elif step[0] == "Y":
                        experts_out(t, int(step[1:]))
            each_pair(dve, e)

            def f(q):
                def mixture(c):
                    rows = y_all[:, bass.ds(q.flat0 * 2 + c * (2 * CH), 2 * CH)].rearrange("p (k s n) -> p k s n", s=2, n=C)
                    dve.wait_ge(S[f"o_y{c}"], q.nth(1, 1) * 16)
                    dve.tensor_tensor(q.flat(res, c).rearrange("p (k n) -> p k n", k=TPC), rows[:, :, 0, :],
                                      rows[:, :, 1, :], ALU.add).then_inc(S["o_f"], 1)

                def product(c):
                    dve.wait_ge(S["o_sg"], q.done(c))
                    dve.tensor_tensor(q.flat(res, c), q.flat(res, c), q.flat(blk, c), ALU.mult).then_inc(S["o_m"], 1)

                mixture(0)
                for c in range(1, 4):
                    mixture(c)
                    product(c - 1)
                product(3)
            dve.wait_ge(S["e_so"], ALL)
            each_batch(dve, f)

        @block.tensor
        def _(pe):
            ident = k("ident")
            prime(pe, "tensor")
            pe.wait_ge(S["ld_k"], 32)
            pe.wait_ge(S["ld_wg"], 16)
            pe.wait_ge(S["set_v1"], 6)

            def turn(dst, src, c, done):
                for i, t in enumerate(tiles(src, c)):
                    mm = nc.tensor.transpose(dst[c][:, P * i:P * (i + 1)], t, ident)
                mm.then_inc(S[done], 1)

            def a(q):
                for c in range(4):
                    pe.wait_ge(S["a_xn"], q.done(c))
                    pe.wait_ge(S["a_xnt"], q.before())
                    turn(tq, bufs, c, "a_tr")
                for c in range(4):
                    pe.wait_ge(S["a_xnt"], q.done(c))
                    pe.wait_ge(S["a_l"], q.before())
                    nc.tensor.matmul(uq[c][0:E, :], w("wg"), q.chunk(padA, c), start=True, stop=True).then_inc(S["a_lg"], 1)
                for c in range(4):
                    pe.wait_ge(S["set_v1"], 1 + c)
                    pe.wait_ge(S["a_lgc"], q.done(c))
                    for i in range(TPC):
                        mm = nc.tensor.transpose(uq[c][:, i * E:(i + 1) * E], lg_c[c][0:E, P * i:P * (i + 1)],
                                                 ident[0:E, 0:E])
                    mm.then_inc(S["a_lt"], 1)
            each_batch(pe, a)

            pe.wait_ge(S["r_mask"], 1)
            pe.wait_ge(S["set_b"], 3)
            for s in range(2):
                mm = nc.tensor.matmul(pt[0][:, s:s + 1], mask_b[:, s * P:(s + 1) * P], ones_b[:, 0:1], start=True, stop=True)
            mm.then_inc(S["r_totc"], 1)
            pe.wait_ge(S["r_totb"], 1)
            for s in range(2):
                nc.tensor.matmul(pu[0][:, 0:NT * E], tot_b[:, s, :], tile_b[:, s * NT * E:(s + 1) * NT * E],
                                 start=(s == 0), stop=False)
            nc.tensor.matmul(pu[0][:, 0:NT * E], before_b[:, :], mask_b[:, :], start=False, stop=True)
            for s in range(2):
                mm = nc.tensor.matmul(pt[1][:, 0:E], tot_b[:, s, :], same_b[:, s * E:(s + 1) * E],
                                      start=(s == 0), stop=(s == 1))
            mm.then_inc(S["r_rank"], 1)

            def b(q):
                for c in range(4):
                    pe.wait_ge(S["b_x1"], q.done(c))
                    pe.wait_ge(S["b_xi"], q.before())
                    turn(tq, bufs, c, "b_tr")
                def back(c):
                    pe.wait_ge(S["b_nm"], q.done(c))
                    pe.wait_ge(S["b_act"], q.before())
                    turn(uq, norm_t, c, "b_back")

                def project(c):
                    pe.wait_ge(S["b_aff"], q.done(c))
                    nc.tensor.matmul(tq[c][:, :], w("in_w"), aff[c][:, :], start=True, stop=True).then_inc(S["b_in"], 1)
                    nc.tensor.matmul(uq[c][:, :], w("actp_w"), aff[c][:, :], start=True, stop=True).then_inc(S["b_gate"], 1)

                back(0)
                back(1)
                project(0)
                back(2)
                project(1)
                back(3)
                project(2)
                project(3)
            pe.wait_ge(S["ld_w"], 16)
            each_batch(pe, b)

            pe.wait_ge(S["b_act"], ALL)
            pe.wait_ge(S["set_kb3"], 5)

            def cc(q):
                def q_k(c):
                    pe.wait_ge(S["c_v"], q.done(c))
                    pe.wait_ge(S["c_vtok"], q.before())
                    nc.tensor.matmul(tq[c][:, :], w("q_w"), bufs[c][:, :], start=True, stop=True).then_inc(S["c_q"], 1)
                    pe.wait_ge(S["c_acc"], q.before())
                    for i, t in enumerate(tiles(bufs, c)):
                        nc.tensor.matmul(uq[c][:, P * i:P * (i + 1)], t, w("k_w"), start=True, stop=False)
                        mm = nc.tensor.matmul(uq[c][:, P * i:P * (i + 1)], ones_b[0:3, :], kb3[:, :], start=False, stop=True)
                    mm.then_inc(S["c_k"], 1)

                def v_turned(c):
                    pe.wait_ge(S["c_qt"], q.done(c))
                    turn(tq, bufs, c, "c_vt")

                def kv(c):
                    pe.wait_ge(S["c_kt"], q.done(c))
                    pe.wait_ge(S["c_vtok"], q.done(c))
                    for i, t in enumerate(tiles(k_tok, c)):
                        mm = nc.tensor.matmul(uq[0][:, 0:C + 1], t, v_tok[c][:, i, :], start=(c == i == 0),
                                              stop=(c == 3 and i == TPC - 1))
                    mm.then_inc(S["c_kv"], 1)

                q_k(0)
                q_k(1)
                v_turned(0)
                q_k(2)
                v_turned(1)
                kv(0)
                q_k(3)
                v_turned(2)
                kv(1)
                v_turned(3)
                kv(2)
                kv(3)
            each_batch(pe, cc)

            def turn_rows(r):
                for u in range(2):
                    mm = nc.tensor.transpose(mxy[:, u * P:(u + 1) * P], xs[:, r, u, 0:C], ident)
                mm.then_inc(S["m_xt"], 1)

            for b_ in range(BATCH):
                pe.wait_ge(S["f_kvs"], b_ + 1)
                nc.tensor.matmul(pt[b_][:, 0:C], k("rope"), kv_s[:, b_, :], start=True, stop=True).then_inc(S["f_kvr1"], 1)
            pe.wait_ge(S["m_ld0"], 16)
            turn_rows(0)
            for b_ in range(BATCH):
                pe.wait_ge(S["f_kvr"], b_ + 1)
                nc.tensor.matmul(pu[b_][:, 0:C], k("rope_t"), kv_r[:, b_, :], start=True, stop=True).then_inc(S["f_m"], 1)

            expert = []

            def load_experts(t):
                expert[:] = nc.values_load_multi_w_load_instructions(
                    texp_i[0:1, bass.ds(t.p0 * 2, 2 * t.per)], engines=(mybir.EngineType.PE,), min_val=0, max_val=E - 1,
                    skip_runtime_bounds_check_because="texp_i is a count clamped to E - 1")[1]

            def last(order, i, kind):
                return max([int(step[1]) for step in order[:i] if step[0] == kind], default=-1)

            def X(t, r, y):
                pe.wait_ge(S[f"m_ld{r % t.per}"], t.uses(r) * 16)
                pe.wait_ge(S["m_ys"], t.done(y))
                turn_rows(r % t.per)


            def H(t, r, u):
                pe.wait_ge(S["m_xtc"], t.done(r))
                nc.tensor.matmul(mh[u][:, :], xs_t[:, r % 2, u, :], w12s[:, bass.ds(expert[2 * r + u] * (2 * EH), 2 * EH)],
                                 start=True, stop=True).then_inc(S["m_h"], 1)

            def G(t, r):
                pe.wait_ge(S["m_g"], t.done_u(r, 1))
                for u in range(2):
                    for a_ in range(2):
                        mm = nc.tensor.transpose(mg[:, (2 * u + a_) * P:(2 * u + a_ + 1) * P],
                                                 gg[:, u, a_ * P:(a_ + 1) * P], ident)
                mm.then_inc(S["m_gt"], 1)

            def Y(t, r, x):
                pe.wait_ge(S["m_gtc"], t.done(r))
                pe.wait_ge(S["m_xtc"], t.done(x))
                for u in range(2):
                    for a_ in range(2):
                        mm = nc.tensor.matmul(mxy[:, (2 + u) * P:(3 + u) * P], gg_t[:, u, a_, :],
                                              w3s[:, bass.ds(expert[2 * r + u] * (2 * C) + a_ * C, C)],
                                              start=(a_ == 0), stop=(a_ == 1))
                mm.then_inc(S["m_y"], 1)

            def expert_step(t, order, i):
                step = order[i]
                r = int(step[1])
                if step[0] == "X":
                    X(t, r, last(order, i, "Y"))
                elif step[0] == "H":
                    H(t, r, int(step[3]))
                elif step[0] == "G":
                    G(t, r)
                else:
                    Y(t, r, max(last(order, i, "X"), 0))

            pe.wait_ge(S["f_mk"], 2 * BATCH)
            pe.wait_ge(S["r_done"], 2)
            pe.wait_ge(S["ld_w12"], 16)
            pe.wait_ge(S["ld_w3"], 16)

            def d(q):
                t = Slots(pe, q, False)
                load_experts(t)
                for at, step in enumerate(D_ORDER):
                    if step[:2] == "nd":
                        c = int(step[2])
                        pe.wait_ge(S[f"d_q{c}"], q.nth(1, 1) * 16)
                        pe.wait_ge(S["d_x2"], q.before())
                        for i, tile in enumerate(tiles(e_q, c)):
                            mm = nc.tensor.matmul((pt, pu)[i // 2][c][:, (i % 2) * WD:(i % 2 + 1) * WD], tile,
                                                  mk[:, bass.ds(q.b, 1), :].rearrange("p a n -> p (a n)"),
                                                  start=True, stop=True)
                        mm.then_inc(S["d_nd"], 1)
                    elif step[:2] == "at":
                        c = int(step[2])
                        pe.wait_ge(S["d_at"], q.done(c))
                        turn(pt, [att[:, 0, :], att[:, 1, :]], c, "d_atT")
                    elif step[:3] == "out":
                        c = int(step[3])
                        pe.wait_ge(S["d_ac"], q.done(c))
                        nc.tensor.matmul(pu[c][:, :], w("out_w"), aff[c][:, :], start=True, stop=True).then_inc(S["d_out"], 1)
                    elif step[0] in "XHGY":
                        expert_step(t, D_ORDER, at)
            each_pair(pe, d)

            pe.wait_ge(S["d_x2"], ALL)

            def e(q):
                t = Slots(pe, q, True)
                load_experts(t)
                for at, step in enumerate(E_ORDER):
                    c = int(step[-1]) if step[-1] in "01" else 0
                    if step[:2] == "tr":
                        pe.wait_ge(S["e_x3"], q.done(c))
                        pe.wait_ge(S["e_so"], q.before())
                        turn(pt, bufs, c, "e_tr")
                    elif step[:2] == "bk":
                        pe.wait_ge(S["e_nm"], q.done(c))
                        pe.wait_ge(S["e_so"], q.before())
                        turn(pu, norm_t, c, "e_back")
                    elif step[:3] == "fc1":
                        i = int(step[4])
                        if i < 2:
                            pe.wait_ge(S["e_aff"], q.done(c))
                        else:
                            pe.wait_ge(S[f"e_h{c}"], q.nth(4, i - 1))
                        nc.tensor.matmul((pt, pu)[i % 2][c][:, :], w("fc1_w", C * i, C * (i + 1)), aff[c][:, :],
                                         start=True, stop=True).then_inc(S[f"e_f1{c}"], 1)
                    elif step[:3] == "fc2":
                        pe.wait_ge(S[f"e_h{c}"], q.nth(4, 4))
                        for i, x3 in enumerate(tiles(bufs, c)):
                            tok = pt[c][:, P * i:P * (i + 1)]
                            for m in range(4):
                                nc.tensor.matmul(tok, hid[:, c, m, P * i:P * (i + 1)], w("fc2_w", C * m, C * (m + 1)),
                                                 start=(m == 0), stop=False)
                            mm = nc.tensor.matmul(tok, x3, ident, start=False, stop=True)
                        mm.then_inc(S["e_s"], 1)
                    elif step[0] in "XHGY":
                        expert_step(t, E_ORDER, at)
            each_pair(pe, e)


def kernel(**inputs):
    import concourse.bacc as bacc
    from concourse.bass_utils import run_bass_kernel_spmd

    f = {n: np.asarray(a) for n, a in inputs.items()}
    A = {n[len("L0_attn_"):]: a for n, a in f.items() if n.startswith("L0_attn_")}
    vecs = np.zeros((P, NVEC), np.float32)
    for name, (at, width) in VEC.items():
        src = A["qk_b"][:C] if name == "q_b" else A[name]
        vecs[:, at:at + width] = src.reshape(width, P).T if name == "fc1_b" else src.reshape(P, width)
    row_biases = np.concatenate([A["qk_b"][C:], A["fc2_b"]])[None, :]
    result_rows = (2 * (np.arange(P)[:, None, None] + P * np.arange(NT)[None, :, None]) + np.arange(2)).astype(np.int32)
    weights = np.concatenate([A["in_w"], A["actp_w"], A["qk_w"], A["out_w"], A["fc1_w"],
                              A["fc2_w"].reshape(4, P, C).transpose(1, 0, 2).reshape(P, 4 * C), f["L0_ffn_Wg"].T], axis=1)
    w12 = np.concatenate([f["L0_ffn_W1"].transpose(2, 0, 1), f["L0_ffn_W2"].transpose(2, 0, 1)], axis=2).reshape(P, -1)
    w3 = f["L0_ffn_W3"].transpose(0, 2, 1).reshape(E, 2, P, C).transpose(2, 0, 1, 3).reshape(P, -1)
    arrays = {"x": A["x"].reshape(N, C), "vecs": vecs, "row_biases": row_biases, "weights": weights, "w12": w12, "w3": w3,
              "consts": shape_constants(), "result_rows": result_rows.reshape(P, 2 * NT)}
    arrays = {n: np.ascontiguousarray(a) for n, a in arrays.items()}

    nc = bacc.Bacc("TRN2", target_bir_lowering=False, num_devices=1)
    args = [nc.dram_tensor(n, a.shape, mybir.dt.from_np(a.dtype), kind="ExternalInput").ap() for n, a in arrays.items()]
    out = nc.dram_tensor("out", (N, C), F32, kind="ExternalOutput").ap()
    build(nc, *args, out)
    r = run_bass_kernel_spmd(nc, [arrays], core_ids=[0])
    return r.results[0]["out"].reshape(BATCH, SEQ, C)
```
